# Optimizing a Trainium2 kernel written in Bass

```python
import numpy as np
import jax
import jax.numpy as jnp

def _softmax(x, axis=-1):
    return jax.nn.softmax(x, axis=axis)

def _gelu(x):
    return jax.nn.gelu(x, approximate=True)

def _silu(x):
    return jax.nn.silu(x)

def _sigmoid(x):
    return jax.nn.sigmoid(x)

def _layernorm(x, axis=-1, eps=1e-05):
    m = jnp.mean(x, axis=axis, keepdims=True)
    v = jnp.var(x, axis=axis, keepdims=True)
    return (x - m) / jnp.sqrt(v + eps)

def _scatter_add(tgt, idx, src, axis=0):
    return tgt.at[idx].add(src)

def _segment_sum(src, seg, n):
    return jax.ops.segment_sum(src, seg, n)
kernel_name = 'mk_adaln_attn_ffn_d1_seqx_r8_f32149'

def setup_inputs(seed: int=0):
    np.random.seed(seed)
    _w = jnp.asarray

    def _rec_inputs():
        import jax
        import jax.numpy as jnp
        _rk = jax.random.key(seed)
        x = -0.000125 + 0.9999 * jax.random.normal(jax.random.fold_in(_rk, 1), (8, 128, 512), jnp.float32)
        _lenS = 128 - jax.random.randint(jax.random.fold_in(_rk, 7), (8,), 0, max(1, 128 // 4) + 1, jnp.int32)
        _lenS2 = 128 - jax.random.randint(jax.random.fold_in(_rk, 8), (8,), 0, max(1, 128 // 4) + 1, jnp.int32)
        itok_B_3_7 = jax.random.randint(jax.random.fold_in(_rk, 11), (8,), 3, 8, jnp.int32)
        itok_Bx16_0_63 = jax.random.randint(jax.random.fold_in(_rk, 12), (8, 16), 0, 64, jnp.int32)
        itok_B_207_1644 = jax.random.randint(jax.random.fold_in(_rk, 13), (8,), 207, 1645, jnp.int32)
        return (x, itok_B_3_7, itok_Bx16_0_63, itok_B_207_1644)
    x, itok_B_3_7, itok_Bx16_0_63, itok_B_207_1644 = _rec_inputs()

    def _L0_cond_setup():
        import jax, jax.numpy as jnp
        import numpy as np
        RANK = 16
        ALPHA = 16.0
        SCALING = ALPHA / RANK
        N_ADAPTERS = 8
        IN_F = 512
        OUT_F = 512
        BATCH = 4
        SEQ = 256
        key = jax.random.key(seed)
        kx, ka, kb, ki = jax.random.split(key, 4)
        x = jax.random.normal(kx, (BATCH, SEQ, IN_F), dtype=jnp.float32)
        A = jax.random.normal(ka, (N_ADAPTERS, OUT_F, RANK), dtype=jnp.float32) * 0.02
        B = jax.random.normal(kb, (N_ADAPTERS, RANK, IN_F), dtype=jnp.float32) * 0.02
        adapter_ids = jax.random.randint(ki, (BATCH,), 0, N_ADAPTERS, dtype=jnp.int32)
        return {'x': x, 'A': A, 'B': B, 'adapter_ids': adapter_ids}
    _L0_cond_all = _L0_cond_setup()
    _L0_cond_in = {k: v for k, v in _L0_cond_all.items() if k in ('A', 'B')}
    del _L0_cond_all

    def _L0_attn_setup():
        import jax, jax.numpy as jnp
        import numpy as np
        SEQ, BATCH, HIDDEN = (256, 1, 512)
        NUM_HEADS, NUM_KV_HEADS, HEAD_DIM = (32, 8, 128)
        Q_PER_GROUP = NUM_HEADS // NUM_KV_HEADS
        TOTAL_PROJ = NUM_KV_HEADS * (Q_PER_GROUP + 2) * HEAD_DIM
        key = jax.random.key(seed)
        k1, k2, k3 = jax.random.split(key, 3)
        tokens = jax.random.normal(k1, (SEQ, BATCH, HIDDEN), dtype=jnp.float32)
        weight_qkv = jax.random.normal(k2, (TOTAL_PROJ, HIDDEN), dtype=jnp.float32) * (2.0 / (TOTAL_PROJ + HIDDEN)) ** 0.5
        weight_proj = jax.random.normal(k3, (HIDDEN, NUM_HEADS * HEAD_DIM), dtype=jnp.float32) * (2.0 / (HIDDEN + NUM_HEADS * HEAD_DIM)) ** 0.5
        return {'tokens': tokens, 'weight_qkv': weight_qkv, 'weight_proj': weight_proj}
    _L0_attn_all = _L0_attn_setup()
    _L0_attn_in = {k: v for k, v in _L0_attn_all.items() if k in ('weight_qkv', 'weight_proj')}
    del _L0_attn_all

    def _L0_cond2_setup():
        import jax, jax.numpy as jnp
        import numpy as np
        B, S, HID = (4, 128, 512)
        D, HQ, HK = (128, 32, 8)
        PAGES, PSIZE, NPP = (64, 32, 16)
        THETA = 10000.0
        EPS = 1e-06
        SCALE = 1.0 / float(np.sqrt(D))

        def _rmsnorm(t, w):
            var = jnp.mean(t * t, axis=-1, keepdims=True)
            return t * jax.lax.rsqrt(var + EPS) * w

        def _rope(t, pos):
            inv_freq = 1.0 / THETA ** (jnp.arange(0, D, 2, dtype=jnp.float32) / D)
            freqs = pos[..., None].astype(jnp.float32) * inv_freq
            cos = jnp.cos(freqs)[:, :, None, :]
            sin = jnp.sin(freqs)[:, :, None, :]
            t1, t2 = (t[..., :D // 2], t[..., D // 2:])
            return jnp.concatenate([t1 * cos - t2 * sin, t2 * cos + t1 * sin], axis=-1)
        key = jax.random.key(seed)
        ks = jax.random.split(key, 10)
        x = jax.random.normal(ks[0], (B, S, HID), jnp.float32)
        Wq = jax.random.normal(ks[1], (HQ * D, HID), jnp.float32) * 0.02
        Wk = jax.random.normal(ks[2], (HK * D, HID), jnp.float32) * 0.02
        Wv = jax.random.normal(ks[3], (HK * D, HID), jnp.float32) * 0.02
        Wo = jax.random.normal(ks[4], (HID, HQ * D), jnp.float32) * 0.02
        q_norm_w = jax.random.uniform(ks[5], (D,), jnp.float32)
        k_norm_w = jax.random.uniform(ks[6], (D,), jnp.float32)
        k_cache = jax.random.normal(ks[7], (PAGES, PSIZE, HK, D), jnp.float32)
        v_cache = jax.random.normal(ks[8], (PAGES, PSIZE, HK, D), jnp.float32)
        block_table = jnp.arange(B * NPP, dtype=jnp.int32).reshape(B, NPP)
        cache_seqlens = jax.random.randint(ks[9], (B,), 0, 475).astype(jnp.int32)
        return dict(x=x, Wq=Wq, Wk=Wk, Wv=Wv, Wo=Wo, q_norm_w=q_norm_w, k_norm_w=k_norm_w, k_cache=k_cache, v_cache=v_cache, block_table=block_table, cache_seqlens=cache_seqlens)
    _L0_cond2_all = _L0_cond2_setup()
    _L0_cond2_in = {k: v for k, v in _L0_cond2_all.items() if k in ('Wq', 'Wk', 'Wv', 'Wo', 'q_norm_w', 'k_norm_w', 'k_cache', 'v_cache')}
    del _L0_cond2_all

    def _L0_ffn_setup():
        import jax, jax.numpy as jnp
        import numpy as np
        BATCH, TOK, DIM, OUT = (4, 256, 512, 512)
        E, R, TOP_K = (8, 16, 2)
        SCALING = 16.0 / R
        key = jax.random.key(seed)
        ks = jax.random.split(key, 6)
        return {'x': jax.random.normal(ks[0], (BATCH, TOK, DIM), dtype=jnp.float32), 'W_base': jax.random.normal(ks[1], (OUT, DIM), dtype=jnp.float32) / np.sqrt(DIM), 'b_base': jax.random.normal(ks[2], (OUT,), dtype=jnp.float32) * 0.01, 'W_gate': jax.random.normal(ks[3], (E, DIM), dtype=jnp.float32) * 0.01, 'A': jax.random.normal(ks[4], (E, R, DIM), dtype=jnp.float32) / np.sqrt(DIM), 'B': jax.random.normal(ks[5], (OUT, OUT // OUT * R * 0 + R), dtype=jnp.float32)[None].repeat(E, 0) * 0.0 + jax.random.normal(ks[5], (E, OUT, R), dtype=jnp.float32) * 0.02}
    _L0_ffn_all = _L0_ffn_setup()
    _L0_ffn_in = {k: v for k, v in _L0_ffn_all.items() if k in ('W_base', 'b_base', 'W_gate', 'A', 'B')}
    del _L0_ffn_all
    return {'x': x, 'itok_B_3_7': itok_B_3_7, 'itok_Bx16_0_63': itok_Bx16_0_63, 'itok_B_207_1644': itok_B_207_1644, 'L0_cond_A': _L0_cond_in['A'], 'L0_cond_B': _L0_cond_in['B'], 'L0_attn_weight_qkv': _L0_attn_in['weight_qkv'], 'L0_attn_weight_proj': _L0_attn_in['weight_proj'], 'L0_cond2_Wq': _L0_cond2_in['Wq'], 'L0_cond2_Wk': _L0_cond2_in['Wk'], 'L0_cond2_Wv': _L0_cond2_in['Wv'], 'L0_cond2_Wo': _L0_cond2_in['Wo'], 'L0_cond2_q_norm_w': _L0_cond2_in['q_norm_w'], 'L0_cond2_k_norm_w': _L0_cond2_in['k_norm_w'], 'L0_cond2_k_cache': _L0_cond2_in['k_cache'], 'L0_cond2_v_cache': _L0_cond2_in['v_cache'], 'L0_ffn_W_base': _L0_ffn_in['W_base'], 'L0_ffn_b_base': _L0_ffn_in['b_base'], 'L0_ffn_W_gate': _L0_ffn_in['W_gate'], 'L0_ffn_A': _L0_ffn_in['A'], 'L0_ffn_B': _L0_ffn_in['B']}

def reference(x, itok_B_3_7, itok_Bx16_0_63, itok_B_207_1644, L0_cond_A, L0_cond_B, L0_attn_weight_qkv, L0_attn_weight_proj, L0_cond2_Wq, L0_cond2_Wk, L0_cond2_Wv, L0_cond2_Wo, L0_cond2_q_norm_w, L0_cond2_k_norm_w, L0_cond2_k_cache, L0_cond2_v_cache, L0_ffn_W_base, L0_ffn_b_base, L0_ffn_W_gate, L0_ffn_A, L0_ffn_B):
    import jax
    import jax.numpy as jnp

    def _L0_cond_ref(x, A, B, adapter_ids):
        import jax, jax.numpy as jnp
        import numpy as np
        RANK = 16
        ALPHA = 16.0
        SCALING = ALPHA / RANK
        N_ADAPTERS = 8
        IN_F = 512
        OUT_F = 512
        BATCH = 4
        SEQ = 256
        B_sel = B[adapter_ids]
        A_sel = A[adapter_ids]
        Bx = jnp.einsum('bni,bri->bnr', x, B_sel)
        out = jnp.einsum('bnr,bor->bno', Bx, A_sel)
        return out * SCALING

    def _L0_attn_ref(tokens, weight_qkv, weight_proj):
        import jax, jax.numpy as jnp
        import numpy as np
        SEQ, BATCH, HIDDEN = (256, 1, 512)
        NUM_HEADS, NUM_KV_HEADS, HEAD_DIM = (32, 8, 128)
        Q_PER_GROUP = NUM_HEADS // NUM_KV_HEADS
        TOTAL_PROJ = NUM_KV_HEADS * (Q_PER_GROUP + 2) * HEAD_DIM
        S, B, H = tokens.shape
        scale = 1.0 / HEAD_DIM ** 0.5
        qkv = jnp.einsum('sbh,ph->sbp', tokens, weight_qkv)
        qkv = qkv.reshape(S, B, NUM_KV_HEADS, Q_PER_GROUP + 2, HEAD_DIM)
        q = qkv[:, :, :, :Q_PER_GROUP, :].reshape(S, B, NUM_HEADS, HEAD_DIM)
        k = qkv[:, :, :, Q_PER_GROUP, :]
        v = qkv[:, :, :, Q_PER_GROUP + 1, :]
        k = jnp.repeat(k, Q_PER_GROUP, axis=2)
        v = jnp.repeat(v, Q_PER_GROUP, axis=2)
        q = q.transpose(1, 2, 0, 3)
        k = k.transpose(1, 2, 0, 3)
        v = v.transpose(1, 2, 0, 3)
        scores = jnp.einsum('bhsd,bhtd->bhst', q, k) * scale
        causal = jnp.tril(jnp.ones((S, S), dtype=bool))
        scores = jnp.where(causal, scores, jnp.finfo(scores.dtype).min)
        attn = jax.nn.softmax(scores, axis=-1)
        out = jnp.einsum('bhst,bhtd->bhsd', attn, v)
        out = out.transpose(2, 0, 1, 3).reshape(S, B, NUM_HEADS * HEAD_DIM)
        return jnp.einsum('sbe,he->sbh', out, weight_proj)

    def _L0_cond2_ref(x, Wq, Wk, Wv, Wo, q_norm_w, k_norm_w, k_cache, v_cache, block_table, cache_seqlens):
        import jax, jax.numpy as jnp
        import numpy as np
        B, S, HID = (4, 128, 512)
        D, HQ, HK = (128, 32, 8)
        PAGES, PSIZE, NPP = (64, 32, 16)
        THETA = 10000.0
        EPS = 1e-06
        SCALE = 1.0 / float(np.sqrt(D))

        def _rmsnorm(t, w):
            var = jnp.mean(t * t, axis=-1, keepdims=True)
            return t * jax.lax.rsqrt(var + EPS) * w

        def _rope(t, pos):
            inv_freq = 1.0 / THETA ** (jnp.arange(0, D, 2, dtype=jnp.float32) / D)
            freqs = pos[..., None].astype(jnp.float32) * inv_freq
            cos = jnp.cos(freqs)[:, :, None, :]
            sin = jnp.sin(freqs)[:, :, None, :]
            t1, t2 = (t[..., :D // 2], t[..., D // 2:])
            return jnp.concatenate([t1 * cos - t2 * sin, t2 * cos + t1 * sin], axis=-1)
        bsz, seqlen, _ = x.shape
        q = jnp.einsum('bsd,ed->bse', x, Wq).reshape(bsz, seqlen, HQ, D)
        k = jnp.einsum('bsd,ed->bse', x, Wk).reshape(bsz, seqlen, HK, D)
        v = jnp.einsum('bsd,ed->bse', x, Wv).reshape(bsz, seqlen, HK, D)
        q = _rmsnorm(q, q_norm_w)
        k = _rmsnorm(k, k_norm_w)
        pos = cache_seqlens[:, None] + jnp.arange(seqlen)[None, :]
        q = _rope(q, pos)
        k = _rope(k, pos)
        L = NPP * PSIZE
        kc = k_cache[block_table].reshape(bsz, L, HK, D)
        vc = v_cache[block_table].reshape(bsz, L, HK, D)
        k_all = jnp.concatenate([kc, k], axis=1)
        v_all = jnp.concatenate([vc, v], axis=1)
        valid_c = jnp.arange(L)[None, :] < cache_seqlens[:, None]
        valid = jnp.concatenate([valid_c, jnp.ones((bsz, seqlen), dtype=bool)], axis=1)
        rep = HQ // HK
        k_all = jnp.repeat(k_all, rep, axis=2)
        v_all = jnp.repeat(v_all, rep, axis=2)
        scores = jnp.einsum('bqhd,bkhd->bhqk', q, k_all) * SCALE
        scores = jnp.where(valid[:, None, None, :], scores, -1e+30)
        probs = jax.nn.softmax(scores, axis=-1)
        o = jnp.einsum('bhqk,bkhd->bqhd', probs, v_all)
        o = o.reshape(bsz, seqlen, HQ * D)
        return jnp.einsum('bse,de->bsd', o, Wo)

    def _L0_ffn_ref(x, W_base, b_base, W_gate, A, B):
        import jax, jax.numpy as jnp
        import numpy as np
        BATCH, TOK, DIM, OUT = (4, 256, 512, 512)
        E, R, TOP_K = (8, 16, 2)
        SCALING = 16.0 / R
        result = jnp.einsum('bnd,od->bno', x, W_base) + b_base
        logits = jnp.einsum('bnd,ed->bne', x, W_gate)
        probs = jax.nn.softmax(logits.astype(jnp.float32), axis=-1)
        top_p, top_i = jax.lax.top_k(probs, TOP_K)
        top_p = top_p / jnp.sum(top_p, axis=-1, keepdims=True)
        top_p = top_p.astype(x.dtype)
        route_w = jnp.sum(jax.nn.one_hot(top_i, E, dtype=x.dtype) * top_p[..., None], axis=-2)
        h = jnp.einsum('bnd,erd->bner', x, A)
        hw = h * route_w[..., None]
        delta = jnp.einsum('bner,eor->bno', hw, B)
        return result + delta * SCALING
    x = x + _L0_attn_ref(_L0_cond_ref(x, L0_cond_A, L0_cond_B, itok_B_3_7), L0_attn_weight_qkv, L0_attn_weight_proj)
    x = x + _L0_ffn_ref(_L0_cond2_ref(x, L0_cond2_Wq, L0_cond2_Wk, L0_cond2_Wv, L0_cond2_Wo, L0_cond2_q_norm_w, L0_cond2_k_norm_w, L0_cond2_k_cache, L0_cond2_v_cache, itok_Bx16_0_63, itok_B_207_1644), L0_ffn_W_base, L0_ffn_b_base, L0_ffn_W_gate, L0_ffn_A, L0_ffn_B)
    return x

_drawn_inputs = setup_inputs


def setup_inputs(seed=0):
    import zlib

    import numpy as np

    out = dict(_drawn_inputs(seed))
    spreads = {}
    factors = {'L0_cond_A': 5.162,
     'L0_cond_B': 4.988,
     'L0_attn_weight_qkv': 5.12,
     'L0_attn_weight_proj': 5.128,
     'L0_cond2_Wk': 8.0,
     'L0_cond2_Wv': 5.676,
     'L0_cond2_q_norm_w': 2.871,
     'L0_cond2_k_norm_w': 8.0,
     'L0_ffn_b_base': 200.0,
     'L0_ffn_W_gate': 8.0,
     'L0_ffn_A': 8.0,
     'L0_ffn_B': 8.0,
     'L0_cond2_k_cache': 8.0,
     'L0_cond2_v_cache': 8.0}
    for name, (base, spread) in spreads.items():
        noise = np.random.default_rng([zlib.crc32(name.encode()), seed]).standard_normal(out[name].shape)
        drawn = base * np.exp(spread * noise) if base else spread * noise
        out[name] = jnp.asarray(drawn.astype(out[name].dtype))
    for name, factor in factors.items():
        out[name] = (out[name] * factor).astype(out[name].dtype)
    return out
```

```python
from contextlib import ExitStack

import numpy as np

import concourse.bass as bass
from concourse import mybir

F32 = mybir.dt.float32
F32R = mybir.dt.float32r
BF16 = mybir.dt.bfloat16
I32 = mybir.dt.int32
U32 = mybir.dt.uint32
ALU = mybir.AluOpType
ACT = mybir.ActivationFunctionType
AX = mybir.AxisListType

P = 128
N = 8
HID = 512
NC_ = HID // P
R = 16
G = 8
HG = 4
NH = G * HG
PAGE = 32
CACHED = 512
KC = CACHED // P
KEYS = CACHED + P
E = 8
SCALE = float(1.0 / np.sqrt(128.0))
EPS_RMS = 1e-6
NEG = -3.0e38
MASKED = -1.0e30
QW = HG * P
PW = QW + 2 * P
TILES_W = 10


def inverse_frequencies():
    return (np.float32(1.0) / np.power(np.float32(10000.0), np.arange(0, P, 2, dtype=np.float32) / np.float32(P))
            ).astype(np.float32)


def block_program(nc, x, ids_adapter, table_pages, cache_len, lora_a, lora_b, w_qkv, w_proj, wq, wk, wv, wo,
                  q_norm, k_norm, k_cache, v_cache, w_base, b_base, w_gate, ex_a, ex_b, out):
    KB = 1024
    base0 = (nc.sbuf_base + 63) // 64 * 64
    ctx = ExitStack()
    with ctx:
        def at(name, shape, dt, kb):
            return nc.alloc_sbuf_tensor_at(name, shape, dt, offset=base0 + int(kb * KB))

        def sem(name):
            return ctx.enter_context(nc.semaphore(name))

        wraw = at("wraw", [P, 2, 6, HID], F32, 0)
        wpraw = at("wpraw", [P, 2, 4, HID], F32, 24)
        fold_v = at("fold_v", [P, 4, G, HID], F32, 40)
        xin = at("xin", [P, N, HID], F32, 40)
        xT = at("xT", [P, NC_, N, P], F32, 56)
        bsel = at("bsel", [P, HID], F32, 72)
        bselT = at("bselT", [P, NC_, P], F32, 74)
        tabs = at("tabs", [P, N, 4, P], F32, 184)
        maskall = at("maskall", [P, N, CACHED], BF16, 174)
        score = at("score", [P, N, NH, N], F32, 104)
        theta = at("theta", [P, N, 64], F32, 136)
        turns = at("turns", [P, N, 64], F32, 138)
        turns2 = at("turns2", [P, N, 64], F32, 140)
        sin_t = at("sin_t", [P, N, 64], F32, 142)
        cos_t = at("cos_t", [P, N, 64], F32, 144)
        keyidx = at("keyidx", [P, CACHED], F32, 202.5)
        freqs = at("freqs", [P, 64], F32, 172.5)
        qn_b = at("qn_b", [P, P], F32, 172.75)
        kn_b = at("kn_b", [P, P], F32, 173.25)
        z_ring = at("z_ring", [P, 2, NH, 2 * R], F32, 112)
        zT_ring = at("zT_ring", [P, 2, G, P], F32, 120)
        xres = at("xres", [P, 2, HID], F32, 128)
        x2sb = at("x2sb", [P, 2, HID], F32, 132)
        wT = at("wT", [P, 6, NC_, P], F32, 136)
        folded = at("folded", [P, 6, P], F32, 148)
        mix = at("mix", [P, HG, P], F32, 151)
        wpT = at("wpT", [P, HG, HID], F32, 153)
        prod = at("prod", [P, 2, HG, P], F32, 161)
        zlT = at("zlT", [P, N, P], F32, 165)
        aall = at("aall", [P, N, NC_, R], F32, 169)
        x2T_hi = at("x2T_hi", [P, NC_, N, P], F32R, 0)
        x2T_lo = at("x2T_lo", [P, NC_, N, P], F32R, 16)
        y = at("y", [P, N, HID], F32, 32)
        wo_hi = at("wo_hi", [P, 2, HG, HID], F32R, 48)
        wo_lo = at("wo_lo", [P, 2, HG, HID], F32R, 64)
        pT_hi = at("pT_hi", [P, KC + 1, QW], F32R, 80)
        pT_lo = at("pT_lo", [P, KC + 1, QW], F32R, 90)
        sm = at("sm", [P, HG, KEYS], F32, 100)
        oT_hi = at("oT_hi", [P, HG, P], F32R, 110)
        oT_lo = at("oT_lo", [P, HG, P], F32R, 112)
        qT_hi = at("qT_hi", [P, QW], F32R, 114)
        qT_lo = at("qT_lo", [P, QW], F32R, 116)
        rope_a = at("rope_a", [P, HG + 1, P], F32, 118)
        rope_b = at("rope_b", [P, HG + 1, P], F32, 120.5)
        kT_hi = at("kT_hi", [P, 2, KEYS], F32R, 123)
        kT_lo = at("kT_lo", [P, 2, KEYS], F32R, 128)
        wa_hi = at("wa_hi", [P, 2, NC_, PW], F32R, 136)
        wa_lo = at("wa_lo", [P, 2, NC_, PW], F32R, 160)
        wtile = at("wtile", [P, 2, HID], F32, 184)
        kraw = at("kraw", [P, 2, KC, P], F32, 188)
        vraw = at("vraw", [P, 2, KC, P], F32, 192)
        tab = at("tab", [P, 2, 4, P], F32, 196)
        mask = at("mask", [P, 2, KEYS], BF16, 200)
        v_hi = at("v_hi", [P, KC + 1, P], F32R, 202.5)
        v_lo = at("v_lo", [P, KC + 1, P], F32R, 133)
        wbraw = at("wbraw", [P, NC_, HID], F32, 136)
        earaw = at("earaw", [P, HID], F32, 144)
        gateraw = at("gateraw", [E, HID], F32, 146)
        ebraw = at("ebraw", [P, E, NC_, R], F32, 148)
        wbT = at("wbT", [P, NC_, HID], F32, 150)
        gaT = at("gaT", [P, NC_, P + E], F32, 158)
        ebT = at("ebT", [P, HID], F32, 161)
        yT = at("yT", [P, 2, NC_, P], F32, 163)
        hw = at("hw", [P, 2, E, R], F32, 167)
        hwT = at("hwT", [P, 2, P], F32, 168)
        bias_b = at("bias_b", [P, HID], F32, 169)
        x2r = at("x2r", [P, 2, HID], F32, 171)
        fin = at("fin", [P, 2, HID], F32, 175)
        routes = at("routes", [P, 2, 8, E], F32, 179)
        pairs = at("pairs", [P, 2, 4, E, E], F32, 179.5)
        route1 = at("route1", [P, 2, 4], F32, 181.5)
        ebj = at("ebj", [P, NC_, E, R], F32, 32 - 16)
        before = at("before", [P, E, E], F32, 182)
        ident = at("ident", [P, P], F32, 205)
        zl = at("zl", [P, N, R], F32, 205.5)
        SM = 206.0
        blockmask = at("blockmask", [P, N], F32, SM)
        pos = at("pos", [P, N], F32, SM + 0.03125)
        len_i = at("len_i", [P, N], I32, SM + 0.0625)
        len_f = at("len_f", [P, N], F32, SM + 0.09375)
        tok = at("tok", [P, 1], F32, SM + 0.125)
        id_sb = at("id_sb", [1, N], I32, SM + 0.15625)
        ss = at("ss", [P, 2, HG + 1], F32, SM + 0.1875)
        ms = at("ms", [P, 2, HG + 1], F32, SM + 0.25)
        rs = at("rs", [P, 2, HG + 1], F32, SM + 0.3125)
        qs = at("qs", [P, 2, HG], F32, SM + 0.375)
        mn = at("mn", [P, HG], F32, SM + 0.40625)
        den = at("den", [P, HG], F32, SM + 0.4375)
        rd = at("rd", [P, HG], F32, SM + 0.46875)
        halfs = at("halfs", [P, HG + 1], F32, SM + 0.5)
        idx_a = at("idx_a", [P, N * KC], I32, SM + 0.53125)
        idx_b = at("idx_b", [P, N * KC], I32, SM + 0.65625)
        slot8 = at("slot8", [P, 1], I32, SM + 0.78125)
        kvown = at("kvown", [P, 2, P], F32, SM + 0.8125)
        rmax = at("rmax", [P, N * NH], F32, 182)
        rden = at("rden", [P, N * NH], F32, 183)
        pages = at("pages", [P, N * 16], I32, 172)

        ps_a = ctx.enter_context(nc.psum_tensor("ps_a", [P, 2 * HID], F32))
        ps_b = ctx.enter_context(nc.psum_tensor("ps_b", [P, 2 * HID], F32))
        ps_t = [ctx.enter_context(nc.psum_tensor(f"ps_t{i}", [P, HID], F32)) for i in range(2)]
        ps_q = ctx.enter_context(nc.psum_tensor("ps_q", [P, HID], F32))
        ps_o = ctx.enter_context(nc.psum_tensor("ps_o", [P, HID], F32))
        ps_s = [ps_a, ps_b]

        x2_d = nc.dram_tensor("x2_scratch", [N, P, HID], F32, kind="Internal").ap()
        tab_d = nc.dram_tensor("tab_scratch", [N, P, 4 * P], F32, kind="Internal").ap()
        mask_d = nc.dram_tensor("mask_scratch", [N, P, CACHED], BF16, kind="Internal").ap()
        freq_d = nc.inline_tensor(inverse_frequencies().reshape(1, 64), "rotary_freqs").ap()

        k_rows = k_cache.rearrange("a s g d -> (a s g) d")
        v_rows = v_cache.rearrange("a s g d -> (a s g) d")

        x_in = [sem(f"x_in{i}") for i in range(2)]
        id_in = sem("id_in")
        lora_in = sem("lora_in")
        small_in = sem("small_in")
        pages_in = sem("pages_in")
        ident_ok = sem("ident_ok")
        bmask_ok = sem("bmask_ok")
        iota_ok = sem("iota_ok")
        xt_full = sem("xt_full")
        xt_act = sem("xt_act")
        xt_dve = sem("xt_dve")
        bt_full = sem("bt_full")
        bt_done = sem("bt_done")
        zT_full = sem("zT_full")
        zT_done = sem("zT_done")
        zl_full = sem("zl_full")
        zl_done = sem("zl_done")
        tb = sem("tb")
        sin_ok = sem("sin_ok")
        tab_out = sem("tab_out")
        idx_ok = sem("idx_ok")
        wq_in = [sem(f"wq_in{i}") for i in range(2)]
        wp_in = [sem(f"wp_in{i}") for i in range(2)]
        t2_full = sem("t2_full")
        t2_done = sem("t2_done")
        fold_full = sem("fold_full")
        fold_done = sem("fold_done")
        mix_full = sem("mix_full")
        mix_done = sem("mix_done")
        y_full = sem("y_full")
        y_done = sem("y_done")
        y_red = sem("y_red")
        fv_full = sem("fv_full")
        fv_act = sem("fv_act")
        fv_dve = sem("fv_dve")
        smx = sem("smx")
        exp2 = sem("exp2")
        prob = sem("prob")
        z_done = sem("z_done")
        zt_full = sem("zt_full")
        zt_done = sem("zt_done")
        out2_full = sem("out2_full")
        out2_done = sem("out2_done")
        xres_in = [sem(f"xres_in{i}") for i in range(2)]
        x2_out = [sem(f"x2_out{i}") for i in range(2)]
        x2t_full = sem("x2t_full")
        x2t_hi = sem("x2t_hi")
        x2t_lo = sem("x2t_lo")
        wt_in = [sem(f"wt_in{i}") for i in range(2)]
        tab_in = [sem(f"tab_in{i}") for i in range(2)]
        kg_in = [sem(f"kg_in{i}") for i in range(2)]
        vg_in = [sem(f"vg_in{i}") for i in range(2)]
        init3 = sem("init3")
        t_full = sem("t_full")
        t_hi = sem("t_hi")
        t_lo = sem("t_lo")
        s_full = sem("s_full")
        s_read = sem("s_read")
        e_done = sem("e_done")
        r_done = sem("r_done")
        p_dve = sem("p_dve")
        p_act = sem("p_act")
        aq_full = sem("aq_full")
        akv_full = sem("akv_full")
        sq_done = sem("sq_done")
        st_pool = sem("st_pool")
        st_done = sem("st_done")
        ro_ab = sem("ro_ab")
        rq_done = sem("rq_done")
        kv_copied = sem("kv_copied")
        sqq_done = sem("sqq_done")
        smx0 = sem("smx0")
        rk_ab = sem("rk_ab")
        rk_done = sem("rk_done")
        vs_hi = sem("vs_hi")
        vs_lo = sem("vs_lo")
        vc_hi = sem("vc_hi")
        vc_lo = sem("vc_lo")
        pv_full = sem("pv_full")
        o_hi = sem("o_hi")
        o_lo = sem("o_lo")
        f_full = sem("f_full")
        f_done = sem("f_done")
        ix_ok = sem("ix_ok")
        lw_in = sem("lw_in")
        lt_full = sem("lt_full")
        lt_done = sem("lt_done")
        x2r_in = [sem(f"x2r_in{i}") for i in range(2)]
        yt_full = sem("yt_full")
        yt_done = sem("yt_done")
        g_full = sem("g_full")
        gm = sem("gm")
        ge = sem("ge")
        rt = sem("rt")
        hw_done = sem("hw_done")
        ht_full = sem("ht_full")
        ht_done = sem("ht_done")
        d_full = sem("d_full")
        fin_done = sem("fin_done")
        fin_out = [sem(f"fin_out{i}") for i in range(2)]
        bias_ok = sem("bias_ok")
        x2b = sem("x2b")
        eb_ok = sem("eb_ok")
        waits_alone = sem("waits_alone")

        W_FIRST = {0: 0, 1: 1, 2: 3, 3: 4, 4: 6, 5: 7, 6: 9}
        W_COUNT = {0: 1, 1: 2, 2: 1, 3: 2, 4: 1, 5: 2, 6: 1, 7: 0}
        PRO = TILES_W + 3

        def groups_of(n, last):
            w = [] if last else [f"W{W_FIRST[n] + i}" for i in range(W_COUNT[n])] if W_COUNT[n] else []
            nxt = not (last and n == N - 1)
            return w + ["K"] * nxt + ["D0", "D1", "D2"] + ["q"] * nxt + ["D3"] + ["k"] * nxt + ["DS"]

        PER_G = sum(len(groups_of(n, False)) for n in range(N))
        assert PER_G % 2 == 0

        def t_index(n, name, last):
            i = sum(len(groups_of(m, last)) for m in range(n)) + groups_of(n, last).index(name)
            return i, (PRO + i) % 2

        LATE_DMAS = 3 + E + 1
        TB_ALL = 32
        TB_ANGLES = 16
        PAIRS = [(s, tp) for s in range(N) for tp in range(s // 2 + 1)]

        def w_dst(wa, wo_t, wpar, t):
            one = bass.ds(wpar, 1)
            if t < 6:
                return wa[:, one, :, t * P:(t + 1) * P].rearrange("p a c m -> p (a c) m")
            return wo_t[:, one, :, (t - 6) * P:(t - 5) * P].rearrange("p a h m -> p (a h) m")

        def hi_lo_target(name, g, kpar1, lo):
            if name == "K":
                return (kT_hi, kT_lo)[lo][:, kpar1, 0:CACHED], HID
            if name == "k":
                return (kT_hi, kT_lo)[lo][:, kpar1, CACHED:KEYS], P
            if name == "q":
                return (qT_hi, qT_lo)[lo][:, :], HID
            pT = (pT_hi, pT_lo)[lo]
            if name == "DS":
                return pT[:, KC, :], HID
            if name[0] == "D":
                h = int(name[1])
                return pT[:, 0:KC, h * P:(h + 1) * P], HID
            return w_dst((wa_hi, wa_lo)[lo], (wo_hi, wo_lo)[lo], (g + 1) % 2, int(name[1:])), HID

        def wait_alone(eng, s, value):
            eng.wait_ge(s, value)
            eng.sem_inc(waits_alone, 1)

        block = ctx.enter_context(nc.Block())

        @block.sync
        def _(sp):
            sp.dma_start(id_sb[:], ids_adapter.rearrange("(o n) -> o n", o=1)).then_inc(id_in, 16)
            sp.dma_start(len_i[:], cache_len.rearrange("(o n) -> o n", o=1).broadcast_to([P, N])).then_inc(small_in, 16)
            sp.dma_start(freqs[:], freq_d.broadcast_to([P, 64])).then_inc(small_in, 16)
            sp.dma_start(qn_b[:], q_norm.rearrange("(o d) -> o d", o=1).broadcast_to([P, P])).then_inc(small_in, 16)
            sp.dma_start(kn_b[:], k_norm.rearrange("(o d) -> o d", o=1).broadcast_to([P, P])).then_inc(small_in, 16)
            sp.dma_start(pages[:], table_pages.rearrange("(o n) k -> o (n k)", o=1).broadcast_to([P, N * 16])
                         ).then_inc(pages_in, 16)
            for h in range(2):
                sp.dma_start(xin[:, 4 * h:4 * h + 4, :], x[4 * h:4 * h + 4].rearrange("n b i -> b n i")
                             ).then_inc(x_in[h], 16)
            sp.wait_ge(id_in, 16)
            for n in range(N):
                a_id = sp.value_load(id_sb[0:1, n:n + 1], min_val=0, max_val=7)
                sp.dma_start(bsel[R * n:R * n + R, :],
                             lora_b[bass.ds(a_id, 1), :, :].rearrange("a r i -> (a r) i")).then_inc(lora_in, 16)
                sp.dma_start(aall[:, n, :, :].rearrange("p j r -> p (j r)"),
                             lora_a[bass.ds(a_id, 1), :, :].rearrange("a (p j) r -> (a p) (j r)", j=NC_)
                             ).then_inc(lora_in, 16)

            def load_weights(g, par):
                sp.dma_start(wraw[:, par, :, :],
                             w_qkv[bass.ds(g * 6 * P, 6 * P), :].rearrange("(t p) o -> p t o", p=P)
                             ).then_inc(wq_in[par], 16)
                sp.dma_start(wpraw[:, par, :, :],
                             w_proj[:, bass.ds(g * QW, QW)].rearrange("(t p) e -> p t e", p=P)
                             ).then_inc(wp_in[par], 16)

            load_weights(0, 0)
            load_weights(1, 1)
            with sp.Fori(0, G // 2 - 1) as gp:
                for par in range(2):
                    wait_alone(sp, t2_full, (gp * 2 + par + 1) * 10)
                    load_weights(gp * 2 + par + 2, par)

            for s in range(2):
                sp.dma_start(xres[:, s, :], x[s]).then_inc(xres_in[s], 16)
            def load_tables(n, par):
                sp.dma_start(tab[:, par, :, :].rearrange("p a d -> p (a d)"), tab_d[n]).then_inc(tab_in[par], 16)
                sp.dma_start(mask[:, par, 0:CACHED], mask_d[n]).then_inc(tab_in[par], 16)

            def load_wtile(g, t, slot):
                if t < HG:
                    src = wq[bass.ds(g * QW + t * P, P), :]
                elif t == HG:
                    src = wk[bass.ds(g * P, P), :]
                elif t == HG + 1:
                    src = wv[bass.ds(g * P, P), :]
                else:
                    src = wo[(t - 6) * P:(t - 5) * P, bass.ds(g * QW, QW)]
                sp.dma_start(wtile[:, slot, :], src).then_inc(wt_in[slot], 16)

            for s in range(N):
                if s == 2:
                    sp.wait_ge(tb, TB_ALL)
                    for n in range(N):
                        sp.dma_start(tab_d[n], tabs[:, n, :, :].rearrange("p a d -> p (a d)")).then_inc(tab_out, 16)
                        sp.dma_start(mask_d[n], maskall[:, n, :]).then_inc(tab_out, 16)
                sp.wait_ge(out2_done, s + 1)
                sp.dma_start(x2_d[s], x2sb[:, s % 2, :]).then_inc(x2_out[s % 2], 16)
                if s + 2 < N:
                    sp.dma_start(xres[:, s % 2, :], x[s + 2]).then_inc(xres_in[s % 2], 16)
                if s == 5:
                    sp.wait_ge(tab_out, 32 * N)
                    load_tables(0, 0)
                    load_tables(1, 1)
                    load_wtile(0, 0, 0)
                    load_wtile(0, 1, 1)

            for t in range(2, TILES_W):
                sp.wait_ge(t_full, t - 1)
                load_wtile(0, t, t % 2)

            def step(g, n, last):
                J = g * N + n
                base = g * PER_G + PRO
                if not last and n == 0:
                    wait_alone(sp, t_full, base)
                    load_wtile(g + 1, 0, 0)
                    load_wtile(g + 1, 1, 1)
                for name in groups_of(n, last):
                    if name[0] == "W" and int(name[1:]) + 2 < TILES_W:
                        t = int(name[1:])
                        wait_alone(sp, t_full, base + t_index(n, name, last)[0] + 1)
                        load_wtile(g + 1, t + 2, t % 2)
                if not (last and n >= N - 2):
                    wait_alone(sp, s_read, J * 4 + 4 + 2)
                    load_tables((n + 2) % N, n % 2)

            with sp.Fori(0, G - 1) as g:
                for n in range(N):
                    step(g, n, False)
            for n in range(N):
                step(G - 1, n, True)

            sp.wait_ge(f_full, N * G)
            sp.dma_start(wbraw[:], w_base.rearrange("(t p) i -> p t i", p=P)).then_inc(lw_in, 16)
            sp.dma_start(earaw[:], ex_a.rearrange("e r i -> (e r) i")).then_inc(lw_in, 16)
            sp.dma_start(gateraw[:], w_gate).then_inc(lw_in, 16)
            for e in range(E):
                sp.dma_start(ebraw[:, e, :, :].rearrange("p j r -> p (j r)"),
                             ex_b[e].rearrange("(p j) r -> p (j r)", j=NC_)).then_inc(lw_in, 16)
            sp.dma_start(bias_b[:], b_base.rearrange("(o i) -> o i", o=1).broadcast_to([P, HID])).then_inc(lw_in, 16)
            for i in range(2):
                sp.wait_ge(x2_out[i], 16 * (N // 2))
            for n in range(2):
                sp.dma_start(x2r[:, n, :], x2_d[n]).then_inc(x2r_in[n], 16)
            for n in range(N):
                sp.wait_ge(fin_done, n + 1)
                sp.dma_start(out[n], fin[:, n % 2, :]).then_inc(fin_out[n % 2], 16)
                if n + 2 < N:
                    sp.dma_start(x2r[:, n % 2, :], x2_d[n + 2]).then_inc(x2r_in[n % 2], 16)
            for i in range(2):
                sp.wait_ge(fin_out[i], 16 * (N // 2))

        @block.gpsimd
        def _(pool):
            pool.memset(ident[:], 0.0).then_inc(ident_ok, 1)
            pool.wait_ge(ident_ok, 1)
            pool.affine_select(out=ident[:], in_=ident[:], compare_op=ALU.not_equal, fill=1.0, base=0,
                               pattern=[[-1, P]], channel_multiplier=1).then_inc(ident_ok, 1)
            pool.memset(blockmask[:], 1.0).then_inc(bmask_ok, 1)
            pool.iota(tok[:], pattern=[[0, 1]], base=0, channel_multiplier=1,
                      allow_small_or_imprecise_dtypes=True).then_inc(iota_ok, 1)
            pool.iota(keyidx[:], pattern=[[1, CACHED]], base=0, channel_multiplier=0,
                      allow_small_or_imprecise_dtypes=True).then_inc(iota_ok, 1)
            pool.iota(slot8[:], pattern=[[0, 1]], base=0, channel_multiplier=8).then_inc(iota_ok, 1)
            pool.wait_ge(bmask_ok, 1)
            pool.affine_select(out=blockmask[:], in_=blockmask[:], compare_op=ALU.is_ge, fill=0.0, base=0,
                               pattern=[[-R, N]], channel_multiplier=1).then_inc(bmask_ok, 1)
            pool.wait_ge(bmask_ok, 2)
            pool.affine_select(out=blockmask[:], in_=blockmask[:], compare_op=ALU.is_ge, fill=0.0, base=R - 1,
                               pattern=[[R, N]], channel_multiplier=-1).then_inc(bmask_ok, 1)
            pool.memset(halfs[:], -0.5).then_inc(iota_ok, 1)
            pool.memset(mask[:, :, CACHED:KEYS], 0.0).then_inc(iota_ok, 1)
            pool.wait_ge(pages_in, 16)
            pool.wait_ge(iota_ok, 5)
            for q in range(4):
                rows = slice(PAGE * q, PAGE * q + PAGE)
                pool.tensor_scalar(idx_a[rows, :], pages[rows, :].rearrange("p (m q) -> p m q", q=4)[:, :, q],
                                   float(PAGE * G), float(-PAGE * G * q), ALU.mult, ALU.add).then_inc(idx_ok, 1)
            pool.wait_ge(idx_ok, 4)
            pool.tensor_tensor(idx_a[:], idx_a[:], slot8[:].broadcast_to([P, N * KC]), ALU.add).then_inc(idx_ok, 1)
            pool.wait_ge(idx_ok, 5)

            def gather(rows_d, raw, arrived, idx, n, par):
                for c in range(KC):
                    k = n * KC + c
                    pool.indirect_dma_start(raw[:, par, c, :], None, rows_d,
                                            bass.IndirectOffsetOnAxis(idx[:, k:k + 1].bitcast(U32), 0)
                                            ).then_inc(arrived[par], 16)

            pool.wait_ge(tab_out, 32 * N)
            for n in range(2):
                gather(k_rows, kraw, kg_in, idx_a, n, n)
                gather(v_rows, vraw, vg_in, idx_a, n, n)

            def stats(J, par):
                wait_alone(pool, sq_done, J + 1)
                pool.tensor_scalar(ms[:, par, :], ss[:, par, :], 1.0 / P, EPS_RMS, ALU.mult, ALU.add
                                   ).then_inc(st_pool, 1)
                wait_alone(pool, st_pool, J * 2 + 1)
                pool.tensor_tensor(rs[:, par, :], ms[:, par, :], halfs[:], ALU.pow).then_inc(st_pool, 1)
                wait_alone(pool, st_pool, J * 2 + 2)
                pool.tensor_scalar(qs[:, par, :], rs[:, par, 0:HG], -SCALE, None, ALU.mult).then_inc(st_done, 1)

            stats(0, 0)
            for i in range(2):
                pool.wait_ge(x2_out[i], 16 * (N // 2))

            def step(g, n, last):
                J = g * N + n
                par = n % 2
                more = not (last and n >= N - 2)
                if n == 0 and not last:
                    pool.tensor_scalar(idx_b[:], idx_a[:], 1.0, None, ALU.add).then_inc(ix_ok, 1)
                    wait_alone(pool, ix_ok, g * 2 + 1)
                idx = idx_a if n < N - 2 else idx_b
                if more:
                    wait_alone(pool, t_full, g * PER_G + PRO + sum(len(groups_of(m, last)) for m in range(n)))
                    gather(k_rows, kraw, kg_in, idx, (n + 2) % N, par)
                wait_alone(pool, vg_in[par], (g * 4 + n // 2 + 1) * 64)
                wait_alone(pool, pv_full, J + 1)
                pool.tensor_copy(v_hi[:, 0:KC, :], vraw[:, par, :, :]).then_inc(vc_hi, 1)
                wait_alone(pool, vc_hi, J + 1)
                pool.tensor_tensor(v_lo[:, 0:KC, :], vraw[:, par, :, :], v_hi[:, 0:KC, :].bitcast(F32),
                                   ALU.subtract).then_inc(vc_lo, 1)
                if more:
                    wait_alone(pool, vc_lo, J + 1)
                    gather(v_rows, vraw, vg_in, idx, (n + 2) % N, par)
                if not (last and n == N - 1):
                    stats(J + 1, 1 - par)
                if n == N - 1 and not last:
                    wait_alone(pool, kg_in[1], (g * 4 + 4) * 64)
                    wait_alone(pool, vg_in[1], (g * 4 + 4) * 64)
                    pool.tensor_copy(idx_a[:], idx_b[:]).then_inc(ix_ok, 1)
                    wait_alone(pool, ix_ok, g * 2 + 2)
                    wait_alone(pool, kg_in[1], (g * 4 + 5) * 64)
                    wait_alone(pool, vg_in[1], (g * 4 + 5) * 64)
                    wait_alone(pool, kg_in[0], (g * 4 + 5) * 64)
                    wait_alone(pool, vg_in[0], (g * 4 + 5) * 64)

            with pool.Fori(0, G - 1) as g:
                for n in range(N):
                    step(g, n, False)
            for n in range(N):
                step(G - 1, n, True)
            pool.wait_ge(f_full, N * G)
            pool.memset(before[:], 1.0).then_inc(bias_ok, 1)
            pool.wait_ge(bias_ok, 1)
            pool.affine_select(out=before[:], in_=before[:], compare_op=ALU.is_gt, fill=0.0, base=0,
                               pattern=[[1, E], [-1, E]], channel_multiplier=0).then_inc(bias_ok, 1)
            pool.wait_ge(lw_in, 16 * LATE_DMAS)
            pool.tensor_copy(ebj[:, :, :, :], ebraw[:, :, :, :].rearrange("p e j r -> p j e r")).then_inc(eb_ok, 1)
            for n in range(N):
                pool.wait_ge(x2r_in[n % 2], 16 * (n // 2 + 1))
                pool.tensor_tensor(x2r[:, n % 2, :], x2r[:, n % 2, :], bias_b[:], ALU.add).then_inc(x2b, 1)

        def mm3(pe, o, l_hi, l_lo, r_hi, r_lo, start, stop):
            pe.matmul(o, l_hi, r_lo, start=start, stop=False)
            pe.matmul(o, l_lo, r_hi, start=False, stop=False)
            return pe.matmul(o, l_hi, r_hi, start=False, stop=stop)

        @block.tensor
        def _(pe):
            pe.wait_ge(ident_ok, 2)
            for n in range(N):
                pe.wait_ge(x_in[n // 4], 16)
                if n >= 2:
                    pe.wait_ge(xt_act if n % 2 == 0 else xt_dve, n // 2)
                for c in range(NC_):
                    mm = pe.transpose(ps_t[n % 2][:, c * P:(c + 1) * P], xin[:, n, c * P:(c + 1) * P], ident[:])
                mm.then_inc(xt_full, 1)
            pe.wait_ge(lora_in, 32 * N)
            for c in range(NC_):
                mm = pe.transpose(ps_q[:, c * P:(c + 1) * P], bsel[:, c * P:(c + 1) * P], ident[:])
            mm.then_inc(bt_full, 1)
            pe.wait_ge(bt_done, 1)
            pe.wait_ge(xt_act, 4)
            pe.wait_ge(xt_dve, 4)
            for h in range(2):
                for c in range(NC_):
                    mm = pe.matmul(ps_a[:, h * HID:(h + 1) * HID], bselT[:, c, :],
                                   xT[:, c, 4 * h:4 * h + 4, :].rearrange("p n b -> p (n b)"),
                                   start=(c == 0), stop=(c == NC_ - 1))
                mm.then_inc(zT_full, 1)
            pe.wait_ge(zT_done, 2)
            for n in range(N):
                mm = pe.matmul(ps_o[:, n * R:(n + 1) * R], zlT[:, n, :], ident[:, n * R:(n + 1) * R],
                               start=True, stop=True)
            mm.then_inc(zl_full, 1)
            pe.wait_ge(zl_done, 1)

            def part_a(gp, par):
                g = gp * 2 + par
                t0 = g * 10

                def transposed(i, srcs):
                    pe.wait_ge(t2_done, t0 + i + 1)
                    for c, src in enumerate(srcs):
                        mm = pe.transpose(ps_t[i % 2][:, c * P:(c + 1) * P], src, ident[:])
                    return mm.then_inc(t2_full, 1)

                def w_group(t):
                    return transposed(t, [wraw[:, par, t, :].rearrange("p (o j) -> p o j", j=NC_)[:, :, j]
                                          for j in range(NC_)])

                def p_group(h):
                    return transposed(6 + h, [wpraw[:, par, ot, h * P:(h + 1) * P] for ot in range(NC_)])

                def fold(t):
                    pe.wait_ge(t2_done, t0 + t + 1 + 2)
                    for j in range(NC_):
                        mm = pe.matmul(ps_a[:, t * P:(t + 1) * P], wT[:, t, j, :], aall[:, :, j, :],
                                       start=(j == 0), stop=(j == NC_ - 1))
                    return mm

                def scores_s(s):
                    if s == 0:
                        pe.wait_ge(mix_done, g + 1)
                    pe.wait_ge(y_done, g * 8 + s + 1)
                    o = (ps_o if s % 2 == 0 else ps_q)[:, 0:HG * R * (s + 1)]
                    pe.matmul(o.rearrange("p (h m) -> p h m", h=HG), zlT[:, s, :], mix[:, :, 0:R * (s + 1)],
                              start=True, stop=True).then_inc(y_full, 1)

                def fold_out(h):
                    pe.wait_ge(t2_done, t0 + 6 + h + 1 + 2)
                    done = fv_act if h % 2 == 0 else fv_dve
                    pe.wait_ge(done, g * 2 + h // 2 + 1)
                    pe.matmul(ps_b[:, (h % 2) * HID:(h % 2 + 1) * HID], folded[:, 5, :], wpT[:, h, :],
                              start=True, stop=True).then_inc(fv_full, 1)

                pe.wait_ge(wq_in[par], (gp + 1) * 16)
                w_group(0)
                w_group(1)
                for t in range(2, 6):
                    fold(t - 2)
                    w_group(t)
                fold(4)
                pe.wait_ge(wp_in[par], (gp + 1) * 16)
                p_group(0)
                fold(5).then_inc(fold_full, 1)
                p_group(1)
                pe.wait_ge(fold_done, g + 1)
                pe.wait_ge(y_done, g * 8 + 2)
                for h in range(HG):
                    mm = pe.matmul(ps_q[:, h * P:(h + 1) * P], folded[:, h, :], folded[:, 4, :], start=True, stop=True)
                mm.then_inc(mix_full, 1)
                p_group(2)
                fold_out(0)
                p_group(3)
                scores_s(0)
                fold_out(1)
                scores_s(1)
                scores_s(2)
                fold_out(2)
                scores_s(3)
                scores_s(4)
                fold_out(3)
                for s in range(5, N):
                    scores_s(s)

            with pe.Fori(0, G // 2) as gp:
                for par in range(2):
                    part_a(gp, par)

            pe.wait_ge(t2_done, 10 * G + 2)
            pe.wait_ge(fv_act, 2 * G + 1)
            pe.wait_ge(fv_dve, 2 * G + 1)
            pe.wait_ge(y_done, 8 * G + 2)

            def z_transposes(k):
                pe.wait_ge(z_done, k + 1)
                for half in range(2):
                    if k >= 1:
                        pe.wait_ge(zt_done, 2 * (k - 1) + half + 1)
                    for i in range(4):
                        g = 4 * half + i
                        mm = pe.transpose(ps_t[half][:, i * P:(i + 1) * P],
                                          z_ring[:, k % 2, g * HG:(g + 1) * HG, :].rearrange("p h m -> p (h m)"),
                                          ident[:])
                    mm.then_inc(zt_full, 1)

            def z_products(k):
                s, tp = PAIRS[k]
                o = ps_o if s % 2 == 0 else ps_q
                if tp == 0 and s >= 2:
                    pe.wait_ge(out2_done, s - 1)
                for g in range(G):
                    if g % 4 == 0:
                        pe.wait_ge(zt_done, 2 * k + g // 4 + 1)
                    mm = pe.matmul(o[:, :], zT_ring[:, k % 2, g, :], fold_v[:, tp, g, :],
                                   start=(tp == 0 and g == 0), stop=(tp == s // 2 and g == G - 1))
                if tp == s // 2:
                    mm.then_inc(out2_full, 1)

            def x2_transposes(s):
                pe.wait_ge(out2_done, s + 1)
                if s >= 2:
                    pe.wait_ge(x2t_lo, s - 1)
                for c in range(NC_):
                    mm = pe.transpose(ps_b[:, (s % 2) * HID + c * P:(s % 2) * HID + (c + 1) * P],
                                      x2sb[:, s % 2, c * P:(c + 1) * P], ident[:])
                mm.then_inc(x2t_full, 1)

            z_transposes(0)
            for k in range(len(PAIRS)):
                if k + 1 < len(PAIRS):
                    z_transposes(k + 1)
                z_products(k)
                s, tp = PAIRS[k]
                if tp == 0 and s >= 1:
                    x2_transposes(s - 1)
            x2_transposes(N - 1)

            pe.sem_inc(pv_full, 1)

            def transposed(idx, bank, outs_ins):
                pe.wait_ge(t_lo, idx + 1)
                for o, i in outs_ins:
                    mm = pe.transpose(ps_t[bank][:, o * P:(o + 1) * P], i, ident[:])
                return mm.then_inc(t_full, 1)

            def w_tile(idx, bank, t, arrivals):
                pe.wait_ge(wt_in[t % 2], arrivals)
                transposed(idx, bank, [(c, wtile[:, t % 2, c * P:(c + 1) * P]) for c in range(NC_)])

            def k_group(idx, bank, g, n):
                pe.wait_ge(kg_in[n % 2], (g * 4 + n // 2 + 1) * 64)
                transposed(idx, bank, [(c, kraw[:, n % 2, c, :]) for c in range(KC)])

            def project_q(n, wpar, cs):
                for c in cs:
                    wh, wl = (w[:, bass.ds(wpar, 1), c, 0:QW].rearrange("p a m -> p (a m)") for w in (wa_hi, wa_lo))
                    mm = mm3(pe, ps_q[:, :], x2T_hi[:, c, n, :], x2T_lo[:, c, n, :], wh, wl, c == 0, c == NC_ - 1)
                if cs[-1] == NC_ - 1:
                    mm.then_inc(aq_full, 1)

            def project_kv(n, wpar):
                for c in range(NC_):
                    wh, wl = (w[:, bass.ds(wpar, 1), c, QW:PW].rearrange("p a m -> p (a m)") for w in (wa_hi, wa_lo))
                    mm = mm3(pe, ps_o[:, 0:2 * P], x2T_hi[:, c, n, :], x2T_lo[:, c, n, :], wh, wl,
                             c == 0, c == NC_ - 1)
                mm.then_inc(akv_full, 1)

            pe.wait_ge(zt_done, 2 * len(PAIRS))
            for t in range(TILES_W):
                w_tile(t, t % 2, t, 16 * (t // 2 + 1))
            pe.wait_ge(x2t_lo, N)
            pe.wait_ge(t_lo, 2 + TILES_W)
            project_q(0, 0, range(NC_))
            project_kv(0, 0)
            k_group(TILES_W, TILES_W % 2, 0, 0)
            pe.wait_ge(rq_done, 1)
            transposed(TILES_W + 1, (TILES_W + 1) % 2, [(h, rope_a[:, h, :]) for h in range(HG)])
            pe.wait_ge(rk_done, 1)
            transposed(TILES_W + 2, TILES_W % 2, [(0, rope_a[:, HG, :])])

            def values(cs, own_group, last_head_group):
                for c in cs:
                    if c == 0:
                        pe.wait_ge(t_lo, last_head_group + 1 + 2)
                    if c == KC:
                        pe.wait_ge(t_lo, own_group + 1 + 2)
                    mm = mm3(pe, ps_o[:, :], v_hi[:, c, :], v_lo[:, c, :], pT_hi[:, c, :], pT_lo[:, c, :],
                             c == 0, c == KC)
                if cs[-1] == KC:
                    mm.then_inc(pv_full, 1)

            def out_proj(wpar, heads):
                for h in heads:
                    wh, wl = (w[:, bass.ds(wpar, 1), h, :].rearrange("p a m -> p (a m)") for w in (wo_hi, wo_lo))
                    mm = mm3(pe, ps_o[:, :], oT_hi[:, h, :], oT_lo[:, h, :], wh, wl, h == 0, h == HG - 1)
                if heads[-1] == HG - 1:
                    mm.then_inc(f_full, 1)

            def step(g, n, first, last):
                J = g * N + n
                base = g * PER_G + PRO
                par = n % 2
                names = groups_of(n, last)
                first = first and n == 0
                nxt = not (last and n == N - 1)
                n1 = (n + 1) % N
                wpar1 = (g + (n == N - 1)) % 2
                wpar0 = (g + (n == 0)) % 2
                start = base + t_index(n, names[0], last)[0]

                def idx(name):
                    i, bank = t_index(n, name, last)
                    return base + i, bank

                def scores(h):
                    pe.wait_ge(s_read, J * 4 + h + 1)
                    s, q = ps_s[h % 2], slice(h * P, (h + 1) * P)
                    mm3(pe, s[:, 0:CACHED], qT_hi[:, q], qT_lo[:, q], kT_hi[:, par, 0:CACHED],
                        kT_lo[:, par, 0:CACHED], True, True)
                    mm3(pe, s[:, CACHED:KEYS], qT_hi[:, q], qT_lo[:, q], kT_hi[:, par, CACHED:KEYS],
                        kT_lo[:, par, CACHED:KEYS], True, True).then_inc(s_full, 1)

                def probs_group(h):
                    pe.wait_ge(p_dve if h < 2 else p_act, J * 2 + h % 2 + 1)
                    transposed(*idx(f"D{h}"), [(c, sm[:, h, c * P:(c + 1) * P]) for c in range(KC)])

                pe.wait_ge(t_lo, start + (2 if first else 1))
                scores(0)
                scores(1)
                for name in names:
                    if name[0] == "W":
                        t = int(name[1:])
                        w_tile(*idx(name), t, (g + 1) * (16 * TILES_W // 2) + 16 * (t // 2 + 1))
                if not first:
                    pe.wait_ge(f_done, J)
                    pe.wait_ge(vc_lo, J)
                    values(range(KC + 1), start - 1, start - 3)
                if nxt:
                    k_group(*idx("K"), g + (n == N - 1), n1)
                    pe.wait_ge(rq_done, J + 1)
                    pe.wait_ge(sq_done, J + 1)
                    if n == N - 1:
                        pe.wait_ge(t_lo, base + t_index(6, "W9", last)[0] + 1 + 2)
                    project_q(n1, wpar1, [0, 1])
                probs_group(0)
                scores(2)
                if nxt:
                    project_q(n1, wpar1, [2, 3])
                probs_group(1)
                scores(3)
                if not first:
                    pe.wait_ge(o_lo, J)
                if nxt:
                    pe.wait_ge(vs_lo, J + 1)
                    project_kv(n1, wpar1)
                probs_group(2)
                if not first:
                    if nxt:
                        pe.wait_ge(kv_copied, J + 2)
                    out_proj(wpar0, [0])
                if nxt:
                    pe.wait_ge(rq_done, J + 2)
                    transposed(*idx("q"), [(h, rope_a[:, h, :]) for h in range(HG)])
                if not first:
                    out_proj(wpar0, [1])
                probs_group(3)
                if not first:
                    out_proj(wpar0, [2])
                if nxt:
                    pe.wait_ge(rk_done, J + 2)
                    transposed(*idx("k"), [(0, rope_a[:, HG, :])])
                if not first:
                    out_proj(wpar0, [3])
                transposed(*idx("DS"), [(h, sm[:, h, CACHED:KEYS]) for h in range(HG)])

            for n in range(N):
                step(0, n, True, False)
            with pe.Fori(1, G - 1) as g:
                for n in range(N):
                    step(g, n, False, False)
            for n in range(N):
                step(G - 1, n, False, True)
            end = (G - 1) * PER_G + PRO + sum(len(groups_of(n, True)) for n in range(N))
            pe.wait_ge(f_done, G * N)
            pe.wait_ge(vc_lo, G * N)
            values(range(KC + 1), end - 1, end - 2)
            pe.wait_ge(o_lo, G * N)
            out_proj((G - 1) % 2, range(HG))

            pe.wait_ge(lw_in, 16 * (3 + E + 1))
            pe.wait_ge(t_lo, 2 + PRO + PER_G * (G - 1) + sum(len(groups_of(n, True)) for n in range(N)))

            def late(i, outs_ins, k=P, m=P):
                if i >= 2:
                    pe.wait_ge(lt_done, i - 1)
                for o, src in outs_ins:
                    mm = pe.transpose(ps_t[i % 2][0:m, o * P:o * P + k], src, ident[0:k, 0:k])
                mm.then_inc(lt_full, 1)

            for ot in range(NC_):
                late(ot, [(c, wbraw[:, ot, c * P:(c + 1) * P]) for c in range(NC_)])
            late(4, [(c, earaw[:, c * P:(c + 1) * P]) for c in range(NC_)])
            late(5, [(c, gateraw[:, c * P:(c + 1) * P]) for c in range(NC_)], k=E)
            pe.wait_ge(eb_ok, 1)
            late(6, [(j, ebj[:, j, :, :].rearrange("p e r -> p (e r)")) for j in range(NC_)])
            pe.wait_ge(lt_done, 7)
            pe.wait_ge(f_done, N * G + 1)

            def y_transposes(n):
                if n >= 2:
                    pe.wait_ge(yt_done, n - 1)
                for c in range(NC_):
                    mm = pe.transpose(ps_t[n % 2][:, c * P:(c + 1) * P], y[:, n, c * P:(c + 1) * P], ident[:])
                mm.then_inc(yt_full, 1)

            def base_and_gate(n):
                pe.wait_ge(yt_done, n + 1)
                if n >= 2:
                    pe.wait_ge(fin_done, n - 1)
                    pe.wait_ge(hw_done, n - 1)
                for c in range(NC_):
                    pe.matmul(ps_b[:, (n % 2) * HID:(n % 2) * HID + P + E], yT[:, n % 2, c, :], gaT[:, c, :],
                              start=(c == 0), stop=(c == NC_ - 1)).then_inc(g_full, 1)
                for c in range(NC_):
                    pe.matmul(ps_a[:, (n % 2) * HID:(n % 2 + 1) * HID], yT[:, n % 2, c, :], wbT[:, c, :],
                              start=(c == 0), stop=False)

            def experts(n):
                pe.wait_ge(hw_done, n + 1)
                if n >= 1:
                    pe.wait_ge(ht_done, n)
                pe.transpose(ps_q[:, 0:P], hw[:, n % 2, :, :].rearrange("p e r -> p (e r)"), ident[:]
                             ).then_inc(ht_full, 1)
                pe.wait_ge(ht_done, n + 1)
                pe.matmul(ps_a[:, (n % 2) * HID:(n % 2 + 1) * HID], hwT[:, n % 2, :], ebT[:, :],
                          start=False, stop=True).then_inc(d_full, 1)

            y_transposes(0)
            for n in range(N):
                if n + 1 < N:
                    y_transposes(n + 1)
                base_and_gate(n)
                if n >= 1:
                    experts(n - 1)
            experts(N - 1)

        @block.scalar
        def _(act):
            for n in range(0, N, 2):
                act.wait_ge(xt_full, n + 1)
                act.activation(xT[:, :, n, :], ps_t[0][:, :].rearrange("p (c b) -> p c b", c=NC_), ACT.Copy
                               ).then_inc(xt_act, 1)
            act.wait_ge(xt_dve, N // 2)
            act.sem_inc(t2_done, 2)
            act.sem_inc(fv_act, 1)

            def part_a(gp, par):
                g = gp * 2 + par

                def copy_group(i):
                    act.wait_ge(t2_full, g * 10 + i + 1)
                    if i < 6:
                        dst, src = wT[:, i, :, :], ps_t[i % 2][:, :].rearrange("p (c b) -> p c b", c=NC_)
                    else:
                        dst, src = wpT[:, i - 6, :], ps_t[i % 2][:, :]
                    act.activation(dst, src, ACT.Copy).then_inc(t2_done, 1)

                def fold_v_copy(h):
                    act.wait_ge(fv_full, g * 4 + h + 1)
                    for tp in range(4):
                        ins = act.activation(
                            fold_v[2 * R * h:2 * R * h + 2 * R, tp, bass.ds(g, 1), :].rearrange("p a m -> p (a m)"),
                            ps_b[2 * R * tp:2 * R * tp + 2 * R, (h % 2) * HID:(h % 2 + 1) * HID], ACT.Copy)
                    ins.then_inc(fv_act, 1)

                for i in range(8):
                    copy_group(i)
                act.wait_ge(fold_full, g + 1)
                act.activation(folded[:, :, :].rearrange("p a m -> p (a m)"), ps_a[:, 0:6 * P], ACT.Copy
                               ).then_inc(fold_done, 1)
                copy_group(8)
                copy_group(9)
                fold_v_copy(0)
                fold_v_copy(2)

            with act.Fori(0, G // 2) as gp:
                for par in range(2):
                    part_a(gp, par)

            for half in range(2):
                act.wait_ge(smx, 4 * half + 2)
                sc = score[:, 4 * half:4 * half + 4, :, :].rearrange("p s h t -> p (s h t)")
                act.activation(sc, sc, ACT.Exp, scale=SCALE).then_inc(exp2, 1)

            def zt_copy(k):
                for half in range(2):
                    act.wait_ge(zt_full, 2 * k + half + 1)
                    if k >= 2 and half == 0:
                        pass
                    act.activation(zT_ring[:, k % 2, 4 * half:4 * half + 4, :].rearrange("p g m -> p (g m)"),
                                   ps_t[half][:, :], ACT.Copy).then_inc(zt_done, 1)

            def x2_hi(s):
                act.wait_ge(x2t_full, s + 1)
                act.activation(x2T_hi[:, :, s, :],
                               ps_b[:, (s % 2) * HID:(s % 2 + 1) * HID].rearrange("p (c b) -> p c b", c=NC_),
                               ACT.Copy).then_inc(x2t_hi, 1)

            for k in range(len(PAIRS)):
                zt_copy(k)
                s, tp = PAIRS[k]
                if tp == 0 and s >= 2:
                    x2_hi(s - 2)
                if k == 1:
                    act.wait_ge(tb, TB_ANGLES)
                    act.activation(sin_t[:], sin_t[:], ACT.Sin).then_inc(sin_ok, 1)
                    act.activation(cos_t[:], cos_t[:], ACT.Sin).then_inc(sin_ok, 1)
            x2_hi(N - 2)
            x2_hi(N - 1)

            def copy_hi(idx, bank, dst, width=HID):
                act.wait_ge(t_full, idx + 1)
                src = ps_t[bank][:, 0:width]
                if len(dst.shape) == 3:
                    src = src.rearrange("p (c m) -> p c m", c=dst.shape[1])
                act.activation(dst, src, ACT.Copy).then_inc(t_hi, 1)

            def squares(J, heads):
                if heads[0] < HG:
                    act.wait_ge(aq_full, J + 1)
                else:
                    act.wait_ge(akv_full, J + 1)
                    act.activation(kvown[:, :, :].rearrange("p a d -> p (a d)"), ps_o[:, 0:2 * P], ACT.Copy
                                   ).then_inc(kv_copied, 1)
                    act.wait_ge(kv_copied, J + 1)
                for h in heads:
                    src = ps_q[:, h * P:(h + 1) * P] if h < HG else kvown[:, 0, :]
                    ins = act.activation(rope_b[:, h, :], src, ACT.Square, accum_out=ss_of(J)[:, h:h + 1])
                ins.then_inc(sq_done if heads[0] == HG else sqq_done, 1)

            ss_par = [0]

            def ss_of(J):
                return ss[:, ss_par[0], :]

            for t in range(TILES_W):
                copy_hi(t, t % 2, w_dst(wa_hi, wo_hi, 0, t))
            squares(0, range(HG))
            squares(0, [HG])
            copy_hi(TILES_W, TILES_W % 2, kT_hi[:, 0, 0:CACHED])
            copy_hi(TILES_W + 1, (TILES_W + 1) % 2, qT_hi[:, :])
            copy_hi(TILES_W + 2, TILES_W % 2, kT_hi[:, 0, CACHED:KEYS], P)

            def output_hi(count):
                act.wait_ge(pv_full, count + 1)
                act.activation(oT_hi[:, :, :].rearrange("p h m -> p (h m)"), ps_o[:, :], ACT.Copy).then_inc(o_hi, 1)

            def step(g, n, first, last):
                first = first and n == 0
                J = g * N + n
                base = g * PER_G + PRO
                names = groups_of(n, last)
                nxt = not (last and n == N - 1)
                kpar1 = 1 - n % 2

                def group(name):
                    i, bank = t_index(n, name, last)
                    dst, width = hi_lo_target(name, g, kpar1, 0)
                    copy_hi(base + i, bank, dst, width)

                def exponentials(h):
                    act.wait_ge(s_read, J * 4 + h + 1 + 2)
                    act.activation(sm[:, h, :], sm[:, h, :], ACT.Exp, bias=mn[:, h:h + 1], scale=-1.0,
                                   accum_out=den[:, h:h + 1]).then_inc(e_done, 1)

                def own_v_hi():
                    act.wait_ge(kv_copied, J + 1)
                    act.wait_ge(pv_full, J + 1)
                    act.activation(v_hi[:, KC, :], kvown[:, 1, :], ACT.Copy).then_inc(vs_hi, 1)

                def normalise(h):
                    act.wait_ge(r_done, J * 4 + h + 1)
                    act.activation(sm[:, h, :], sm[:, h, :], ACT.Copy, scale=rd[:, h:h + 1]).then_inc(p_act, 1)

                w = [m for m in names if m[0] == "W"]
                exponentials(0)
                if w:
                    group(w[0])
                exponentials(1)
                if len(w) > 1:
                    group(w[1])
                if not first:
                    output_hi(J)
                own_v_hi()
                if nxt:
                    group("K")
                group("D0")
                exponentials(2)
                ss_par[0] = 1 - n % 2
                if nxt:
                    squares(J + 1, range(HG))
                group("D1")
                normalise(2)
                exponentials(3)
                if nxt:
                    squares(J + 1, [HG])
                group("D2")
                normalise(3)
                if nxt:
                    group("q")
                group("D3")
                if nxt:
                    group("k")
                group("DS")

            for n in range(N):
                step(0, n, True, False)
            with act.Fori(1, G - 1) as g:
                for n in range(N):
                    step(g, n, False, False)
            for n in range(N):
                step(G - 1, n, False, True)
            output_hi(G * N)

            for i in range(7):
                act.wait_ge(lt_full, i + 1)
                b = ps_t[i % 2]
                if i < 4:
                    dst, src = wbT[:, :, i * P:(i + 1) * P], b[:, :].rearrange("p (c m) -> p c m", c=NC_)
                elif i == 4:
                    dst, src = gaT[:, :, 0:P], b[:, :].rearrange("p (c m) -> p c m", c=NC_)
                elif i == 5:
                    dst = gaT[:, :, P:P + E]
                    src = b[:, :].rearrange("p (c m) -> p c m", c=NC_)[:, :, 0:E]
                else:
                    dst = ebT[:, :].rearrange("p (o j) -> p j o", j=NC_)
                    src = b[:, :].rearrange("p (j o) -> p j o", j=NC_)
                act.activation(dst, src, ACT.Copy).then_inc(lt_done, 1)

            def y_copy(n):
                act.wait_ge(yt_full, n + 1)
                if n >= 2:
                    act.wait_ge(g_full, NC_ * (n - 1))
                    act.wait_ge(ht_full, n - 1)
                act.activation(yT[:, n % 2, :, :].rearrange("p c m -> p (c m)"), ps_t[n % 2][:, :], ACT.Copy
                               ).then_inc(yt_done, 1)

            def gate_exp(n):
                act.wait_ge(gm, n + 1)
                act.activation(routes[:, n % 2, 0, :], ps_b[:, (n % 2) * HID + P:(n % 2) * HID + P + E], ACT.Exp,
                               bias=route1[:, n % 2, 0:1], accum_out=route1[:, n % 2, 1:2]).then_inc(ge, 1)

            def hw_copy(n):
                act.wait_ge(ht_full, n + 1)
                act.activation(hwT[:, n % 2, :], ps_q[:, 0:P], ACT.Copy).then_inc(ht_done, 1)

            y_copy(0)
            for n in range(N):
                if n + 1 < N:
                    y_copy(n + 1)
                gate_exp(n)
                if n >= 1:
                    hw_copy(n - 1)
            hw_copy(N - 1)

        @block.vector
        def _(dve):
            for n in range(1, N, 2):
                dve.wait_ge(xt_full, n + 1)
                dve.tensor_copy(xT[:, :, n, :], ps_t[1][:, :].rearrange("p (c b) -> p c b", c=NC_)
                                ).then_inc(xt_dve, 1)
            dve.wait_ge(bt_full, 1)
            dve.tensor_copy(bselT[:, :, :].rearrange("p c m -> p (c m)"), ps_q[:, :]).then_inc(bt_done, 1)
            dve.memset(score[:], NEG).then_inc(smx0, 1)
            dve.wait_ge(bmask_ok, 3)
            for h in range(2):
                dve.wait_ge(zT_full, h + 1)
                dve.tensor_tensor(zlT[:, 4 * h:4 * h + 4, :],
                                  ps_a[:, h * HID:(h + 1) * HID].rearrange("p (n b) -> p n b", n=4),
                                  blockmask[:, 4 * h:4 * h + 4].unsqueeze(2).broadcast_to([P, 4, P]), ALU.mult
                                  ).then_inc(zT_done, 1)
            dve.wait_ge(zl_full, 1)
            dve.tensor_copy(zl[:, :, :].rearrange("p n r -> p (n r)"), ps_o[:, 0:P]).then_inc(zl_done, 1)
            dve.wait_ge(zl_done, 1)
            dve.wait_ge(smx0, 1)
            dve.sem_inc(y_done, 2)
            dve.sem_inc(fv_dve, 1)

            def part_a(gp, par):
                g = gp * 2 + par

                def scores_s(s):
                    w = R * (s + 1)
                    dve.wait_ge(y_full, g * 8 + s + 1)
                    dve.wait_ge(y_red, g * 8 + s + 1)
                    src = (ps_o if s % 2 == 0 else ps_q)[:, 0:HG * w].rearrange("p (h m) -> p h m", h=HG)
                    zz = zl[:, 0:s + 1, :].rearrange("p n r -> p (n r)").unsqueeze(1).broadcast_to([P, HG, w])
                    dve.tensor_tensor(prod[:, s % 2, :, 0:w], src, zz, ALU.mult).then_inc(y_done, 1)

                def sums_s(s):
                    dve.wait_ge(y_done, g * 8 + s + 1 + 2)
                    dve.tensor_reduce(score[:, s, bass.ds(g * HG, HG), 0:s + 1],
                                      prod[:, s % 2, :, 0:R * (s + 1)].rearrange("p h (t r) -> p h t r", r=R),
                                      AX.X, ALU.add).then_inc(y_red, 1)

                def fold_v_copy(h):
                    dve.wait_ge(fv_full, g * 4 + h + 1)
                    for tp in range(4):
                        ins = dve.tensor_copy(
                            fold_v[2 * R * h:2 * R * h + 2 * R, tp, bass.ds(g, 1), :].rearrange("p a m -> p (a m)"),
                            ps_b[2 * R * tp:2 * R * tp + 2 * R, (h % 2) * HID:(h % 2 + 1) * HID])
                    ins.then_inc(fv_dve, 1)

                dve.wait_ge(mix_full, g + 1)
                dve.tensor_copy(mix[:, :, :].rearrange("p h m -> p (h m)"), ps_q[:, :]).then_inc(mix_done, 1)
                scores_s(0)
                scores_s(1)
                sums_s(0)
                sums_s(1)
                fold_v_copy(1)
                scores_s(2)
                scores_s(3)
                sums_s(2)
                sums_s(3)
                scores_s(4)
                fold_v_copy(3)
                scores_s(5)
                sums_s(4)
                scores_s(6)
                sums_s(5)
                scores_s(7)
                sums_s(6)
                sums_s(7)

            dve.sem_inc(y_red, 2)
            with dve.Fori(0, G // 2) as gp:
                for par in range(2):
                    part_a(gp, par)

            dve.wait_ge(y_red, 8 * G + 2)
            for half in range(2):
                sc = score[:, 4 * half:4 * half + 4, :, :].rearrange("p s h t -> p (s h) t")
                rm = rmax[:, 4 * NH * half:4 * NH * (half + 1)]
                dve.tensor_reduce(rm, sc, AX.X, ALU.max).then_inc(smx, 1)
                dve.wait_ge(smx, 4 * half + 1)
                dve.tensor_tensor(sc, sc, rm.unsqueeze(2).broadcast_to([P, 4 * NH, N]), ALU.subtract).then_inc(smx, 1)
                dve.wait_ge(exp2, half + 1)
                rr = rden[:, 4 * NH * half:4 * NH * (half + 1)]
                dve.tensor_reduce(rr, sc, AX.X, ALU.add).then_inc(smx, 1)
                dve.wait_ge(smx, 4 * half + 3)
                dve.reciprocal(rr, rr).then_inc(smx, 1)
                dve.wait_ge(smx, 4 * half + 4)
                dve.tensor_tensor(sc, sc, rr.unsqueeze(2).broadcast_to([P, 4 * NH, N]), ALU.mult).then_inc(prob, 1)

            def z_pair(k):
                s, tp = PAIRS[k]
                dve.wait_ge(prob, s // 4 + 1)
                if k >= 2:
                    dve.wait_ge(zt_full, 2 * (k - 1))
                pr = score[:, s, :, 2 * tp:2 * tp + 2].unsqueeze(3).broadcast_to([P, NH, 2, R])
                zz = zl[:, 2 * tp:2 * tp + 2, :].unsqueeze(1).broadcast_to([P, NH, 2, R])
                dve.tensor_tensor(z_ring[:, k % 2, :, :].rearrange("p h (t r) -> p h t r", r=R), pr, zz, ALU.mult
                                  ).then_inc(z_done, 1)

            def x2_sum(s):
                dve.wait_ge(out2_full, s + 1)
                dve.wait_ge(xres_in[s % 2], 16 * (s // 2 + 1))
                if s >= 2:
                    dve.wait_ge(x2_out[s % 2], 16 * (s // 2))
                    dve.wait_ge(x2t_full, s - 1)
                dve.tensor_tensor(x2sb[:, s % 2, :], ps_o[:, :] if s % 2 == 0 else ps_q[:, :],
                                  xres[:, s % 2, :], ALU.add).then_inc(out2_done, 1)

            def x2_low(s):
                dve.wait_ge(x2t_hi, s + 1)
                dve.tensor_tensor(x2T_lo[:, :, s, :],
                                  ps_b[:, (s % 2) * HID:(s % 2 + 1) * HID].rearrange("p (c b) -> p c b", c=NC_),
                                  x2T_hi[:, :, s, :].bitcast(F32), ALU.subtract).then_inc(x2t_lo, 1)

            def angles():
                dve.wait_ge(small_in, 64)
                dve.wait_ge(iota_ok, 5)
                dve.wait_ge(y_full, 8 * G)
                c1 = 6.28125
                c2 = float(2 * np.pi - c1)
                magic = 1.5 * 2.0 ** 23
                dve.tensor_copy(len_f[:], len_i[:]).then_inc(tb, 1)
                dve.wait_ge(tb, 1)
                dve.tensor_scalar(pos[:], len_f[:], tok[:, 0:1], None, ALU.add).then_inc(tb, 1)
                dve.wait_ge(tb, 2)
                dve.tensor_tensor(theta[:], pos[:].unsqueeze(2).broadcast_to([P, N, 64]),
                                  freqs[:].unsqueeze(1).broadcast_to([P, N, 64]), ALU.mult).then_inc(tb, 1)
                dve.wait_ge(tb, 3)
                i = 3
                for dst, quarter in ((sin_t, 0.0), (cos_t, 0.25)):
                    dve.tensor_scalar(turns[:], theta[:], float(1 / (2 * np.pi)), quarter, ALU.mult, ALU.add
                                      ).then_inc(tb, 1)
                    dve.wait_ge(tb, i + 1)
                    dve.tensor_scalar(turns2[:], turns[:], magic, None, ALU.add).then_inc(tb, 1)
                    dve.wait_ge(tb, i + 2)
                    dve.tensor_scalar(turns[:], turns2[:], -magic, None, ALU.add).then_inc(tb, 1)
                    dve.wait_ge(tb, i + 3)
                    dve.scalar_tensor_tensor(out=turns2[:], in0=turns[:], scalar=-c1, in1=theta[:],
                                             op0=ALU.mult, op1=ALU.add).then_inc(tb, 1)
                    dve.wait_ge(tb, i + 4)
                    dve.scalar_tensor_tensor(out=dst[:], in0=turns[:], scalar=-c2, in1=turns2[:],
                                             op0=ALU.mult, op1=ALU.add).then_inc(tb, 1)
                    dve.wait_ge(tb, i + 5)
                    i += 5
                dve.tensor_scalar(cos_t[:], cos_t[:], float(np.pi / 2), None, ALU.add).then_inc(tb, 1)
                dve.wait_ge(tb, i + 1)
                for dst in (sin_t, cos_t):
                    dve.tensor_scalar(dst[:], dst[:], 3.1415925, -3.1415925, ALU.min, ALU.max).then_inc(tb, 1)
                assert i + 3 == TB_ANGLES

            def tables():
                dve.wait_ge(sin_ok, 2)
                for which, w in ((0, qn_b), (2, kn_b)):
                    for half in range(2):
                        wh = w[:, 64 * half:64 * half + 64].unsqueeze(1).broadcast_to([P, N, 64])
                        dve.tensor_tensor(tabs[:, :, which, 64 * half:64 * half + 64], cos_t[:], wh, ALU.mult
                                          ).then_inc(tb, 1)
                    dve.scalar_tensor_tensor(out=tabs[:, :, which + 1, 0:64], in0=sin_t[:], scalar=-1.0,
                                             in1=w[:, 64:128].unsqueeze(1).broadcast_to([P, N, 64]),
                                             op0=ALU.mult, op1=ALU.mult).then_inc(tb, 1)
                    dve.tensor_tensor(tabs[:, :, which + 1, 64:128], sin_t[:],
                                      w[:, 0:64].unsqueeze(1).broadcast_to([P, N, 64]), ALU.mult).then_inc(tb, 1)
                for n in range(N):
                    dve.tensor_scalar(maskall[:, n, :], keyidx[:], len_f[:, n:n + 1], MASKED, ALU.is_ge, ALU.mult
                                      ).then_inc(tb, 1)
                assert TB_ANGLES + 8 + N == TB_ALL

            z_pair(0)
            z_pair(1)
            for k in range(len(PAIRS)):
                if k + 2 < len(PAIRS):
                    z_pair(k + 2)
                if k == 0:
                    angles()
                if k == 1:
                    tables()
                s, tp = PAIRS[k]
                if tp == 0 and s >= 2:
                    x2_low(s - 2)
                if tp == s // 2:
                    x2_sum(s)
            x2_low(N - 2)
            x2_low(N - 1)

            for i in range(2):
                dve.wait_ge(x2_out[i], 16 * (N // 2))
            dve.wait_ge(x2t_full, N)
            dve.memset(y[:], 0.0).then_inc(init3, 1)
            dve.wait_ge(init3, 1)
            dve.wait_ge(zt_done, 2 * len(PAIRS))
            dve.sem_inc(t_lo, 2)
            dve.sem_inc(s_read, 2)
            dve.sem_inc(f_done, 1)

            def copy_lo(idx, bank, hi, lo, width=HID):
                dve.wait_ge(t_hi, idx + 1)
                src = ps_t[bank][:, 0:width]
                if len(hi.shape) == 3:
                    src = src.rearrange("p (c m) -> p c m", c=hi.shape[1])
                dve.tensor_tensor(lo, src, hi.bitcast(F32), ALU.subtract).then_inc(t_lo, 1)

            def rope_q(J, par):
                q = ps_q[:, :].rearrange("p (h d) -> p h d", h=HG)
                dve.wait_ge(aq_full, J + 1)
                dve.wait_ge(tab_in[par], tab_count(J, par))
                dve.wait_ge(sqq_done, J + 1)
                ta = tab[:, par, 0, :].unsqueeze(1).broadcast_to([P, HG, P])
                dve.tensor_tensor(rope_a[:, 0:HG, :], q, ta, ALU.mult).then_inc(ro_ab, 1)
                for half in range(2):
                    a, b = 64 * half, 64 * (1 - half)
                    ins = dve.tensor_tensor(rope_b[:, 0:HG, a:a + 64], q[:, :, b:b + 64],
                                            tab[:, par, 1, a:a + 64].unsqueeze(1).broadcast_to([P, HG, 64]), ALU.mult)
                    ins.then_inc(ro_ab, 1)
                dve.wait_ge(ro_ab, (J + 1) * 3)
                dve.tensor_tensor(rope_a[:, 0:HG, :], rope_a[:, 0:HG, :], rope_b[:, 0:HG, :], ALU.add
                                  ).then_inc(rq_done, 1)

            def rope_k(J, par):
                k = kvown[:, 0, :]
                dve.wait_ge(st_done, J + 1)
                r = rs[:, par, HG:HG + 1]
                dve.scalar_tensor_tensor(out=rope_a[:, HG, :], in0=k, scalar=r, in1=tab[:, par, 2, :],
                                         op0=ALU.mult, op1=ALU.mult).then_inc(rk_ab, 1)
                for half in range(2):
                    a, b = 64 * half, 64 * (1 - half)
                    dve.scalar_tensor_tensor(out=rope_b[:, HG, a:a + 64], in0=k[:, b:b + 64], scalar=r,
                                             in1=tab[:, par, 3, a:a + 64], op0=ALU.mult, op1=ALU.mult
                                             ).then_inc(rk_ab, 1)
                dve.wait_ge(rk_ab, (J + 1) * 3)
                dve.tensor_tensor(rope_a[:, HG, :], rope_a[:, HG, :], rope_b[:, HG, :], ALU.add).then_inc(rk_done, 1)

            tab_g = [0, 0]

            def tab_count(J, par):
                g, n = tab_g
                return (g * 4 + n // 2 + 1) * 32

            for t in range(TILES_W):
                copy_lo(t, t % 2, w_dst(wa_hi, wo_hi, 0, t), w_dst(wa_lo, wo_lo, 0, t))
            rope_q(0, 0)
            rope_k(0, 0)
            copy_lo(TILES_W, TILES_W % 2, kT_hi[:, 0, 0:CACHED], kT_lo[:, 0, 0:CACHED])
            copy_lo(TILES_W + 1, (TILES_W + 1) % 2, qT_hi[:, :], qT_lo[:, :])
            copy_lo(TILES_W + 2, TILES_W % 2, kT_hi[:, 0, CACHED:KEYS], kT_lo[:, 0, CACHED:KEYS], P)

            def output_lo(count):
                dve.wait_ge(o_hi, count)
                dve.tensor_tensor(oT_lo[:, :, :].rearrange("p h m -> p (h m)"), ps_o[:, :],
                                  oT_hi[:, :, :].rearrange("p h m -> p (h m)").bitcast(F32), ALU.subtract
                                  ).then_inc(o_lo, 1)

            def add_output(count, m):
                dve.wait_ge(f_full, count)
                dve.tensor_tensor(y[:, m, :], ps_o[:, :], y[:, m, :], ALU.add).then_inc(f_done, 1)

            def step(g, n, first, last):
                J = g * N + n
                base = g * PER_G + PRO
                par = n % 2
                names = groups_of(n, last)
                nxt = not (last and n == N - 1)
                w = [m for m in names if m[0] == "W"]

                def group(name):
                    i, bank = t_index(n, name, last)
                    hi, width = hi_lo_target(name, g, 1 - par, 0)
                    lo, _ = hi_lo_target(name, g, 1 - par, 1)
                    copy_lo(base + i, bank, hi, lo, width)

                def least(h):
                    wait_alone(dve, s_full, J * 4 + h + 1)
                    if h == 0:
                        wait_alone(dve, st_done, J + 1)
                        wait_alone(dve, tab_in[par], (g * 4 + n // 2 + 1) * 32)
                    dve.tensor_tensor_reduce(out=sm[:, h, :], in0=ps_s[h % 2][:, 0:KEYS], in1=mask[:, par, :],
                                             scale=qs[:, par, h:h + 1], scalar=3.0e38, op0=ALU.add, op1=ALU.min,
                                             accum_out=mn[:, h:h + 1]).then_inc(s_read, 1)

                def reciprocal(h):
                    dve.wait_ge(e_done, J * 4 + h + 1)
                    dve.reciprocal(rd[:, h:h + 1], den[:, h:h + 1]).then_inc(r_done, 1)

                def normalise(h):
                    reciprocal(h)
                    dve.wait_ge(r_done, J * 4 + h + 1)
                    dve.tensor_scalar(sm[:, h, :], sm[:, h, :], rd[:, h:h + 1], None, ALU.mult).then_inc(p_dve, 1)

                if not (first and n < 2):
                    add_output(J - 1, (n - 2) % N)
                least(0)
                least(1)
                if w:
                    group(w[0])
                normalise(0)
                normalise(1)
                if len(w) > 1:
                    group(w[1])
                if not (first and n < 1):
                    output_lo(J)
                dve.wait_ge(vs_hi, J + 1)
                dve.tensor_tensor(v_lo[:, KC, :], kvown[:, 1, :], v_hi[:, KC, :].bitcast(F32), ALU.subtract
                                  ).then_inc(vs_lo, 1)
                if nxt:
                    group("K")
                group("D0")
                least(2)
                reciprocal(2)
                group("D1")
                least(3)
                tab_g[:] = [g + (n == N - 1), (n + 1) % N]
                if nxt:
                    rope_q(J + 1, 1 - par)
                reciprocal(3)
                group("D2")
                if nxt:
                    rope_k(J + 1, 1 - par)
                    group("q")
                group("D3")
                if nxt:
                    group("k")
                group("DS")

            for n in range(N):
                step(0, n, True, False)
            with dve.Fori(1, G - 1) as g:
                for n in range(N):
                    step(g, n, False, False)
            for n in range(N):
                step(G - 1, n, False, True)
            add_output(G * N - 1, N - 2)
            output_lo(G * N)
            add_output(G * N, N - 1)

            dve.wait_ge(bias_ok, 2)
            RT = 11

            def route(n):
                i = n % 2
                g_ps = ps_b[:, i * HID:i * HID + P + E]
                e, p, sel, keep, wgt = (routes[:, i, m, :] for m in range(5))
                neg_max, total, inv, s2 = (route1[:, i, m:m + 1] for m in range(4))
                gt, eq = pairs[:, i, 0, :, :], pairs[:, i, 1, :, :]
                c = [n * RT]

                def after_last():
                    dve.wait_ge(rt, c[0])

                def chained(ins):
                    c[0] += 1
                    ins.then_inc(rt, 1)

                dve.wait_ge(g_full, NC_ * (n + 1))
                dve.tensor_reduce(neg_max, g_ps[:, P:P + E], AX.X, ALU.max, negate=True).then_inc(gm, 1)
                dve.wait_ge(ge, n + 1)
                chained(dve.reciprocal(inv, total))
                after_last()
                chained(dve.tensor_scalar(p, e, inv, None, ALU.mult))
                after_last()
                later = p.unsqueeze(1).broadcast_to([P, E, E])
                mine = p.unsqueeze(2).broadcast_to([P, E, E])
                chained(dve.tensor_tensor(gt, later, mine, ALU.is_gt))
                chained(dve.tensor_tensor(eq, later, mine, ALU.is_equal))
                after_last()
                chained(dve.tensor_tensor(eq, eq, before[:], ALU.mult))
                after_last()
                chained(dve.tensor_tensor(gt, gt, eq, ALU.add))
                after_last()
                chained(dve.tensor_reduce(sel, gt, AX.X, ALU.add))
                after_last()
                chained(dve.tensor_scalar(keep, sel, 1.5, None, ALU.is_lt))
                after_last()
                chained(dve.tensor_tensor(wgt, keep, p, ALU.mult))
                after_last()
                chained(dve.tensor_reduce(s2, wgt, AX.X, ALU.add))
                after_last()
                chained(dve.reciprocal(inv, s2))
                after_last()
                assert c[0] == (n + 1) * RT
                if n >= 2:
                    dve.wait_ge(ht_full, n - 1)
                dve.scalar_tensor_tensor(out=hw[:, i, :, :], in0=g_ps[:, 0:P].rearrange("p (e r) -> p e r", r=R),
                                         scalar=inv, in1=wgt.unsqueeze(2).broadcast_to([P, E, R]),
                                         op0=ALU.mult, op1=ALU.mult).then_inc(hw_done, 1)

            def finish(n):
                dve.wait_ge(d_full, n + 1)
                dve.wait_ge(x2b, n + 1)
                if n >= 2:
                    dve.wait_ge(fin_out[n % 2], 16 * (n // 2))
                dve.tensor_tensor(fin[:, n % 2, :], ps_a[:, (n % 2) * HID:(n % 2 + 1) * HID], x2r[:, n % 2, :],
                                  ALU.add).then_inc(fin_done, 1)

            for n in range(N):
                route(n)
                if n >= 1:
                    finish(n - 1)
            finish(N - 1)


_INS = ['x', 'itok_B_3_7', 'itok_Bx16_0_63', 'itok_B_207_1644', 'L0_cond_A', 'L0_cond_B', 'L0_attn_weight_qkv',
        'L0_attn_weight_proj', 'L0_cond2_Wq', 'L0_cond2_Wk', 'L0_cond2_Wv', 'L0_cond2_Wo', 'L0_cond2_q_norm_w',
        'L0_cond2_k_norm_w', 'L0_cond2_k_cache', 'L0_cond2_v_cache', 'L0_ffn_W_base', 'L0_ffn_b_base',
        'L0_ffn_W_gate', 'L0_ffn_A', 'L0_ffn_B']
_OUTS = [((8, 128, 512), 'float32')]


def kernel(**inputs):
    import numpy as _np
    import concourse.bacc as _bacc
    from concourse import mybir as _mybir
    from concourse.bass_utils import run_bass_kernel_spmd as _run

    nc = _bacc.Bacc("TRN2", target_bir_lowering=False, num_devices=1)
    arrays, args = {}, []
    for name in _INS:
        a = _np.ascontiguousarray(inputs[name])
        arrays[f"in_{name}_dram"] = a
        args.append(nc.dram_tensor(f"in_{name}_dram", a.shape, _mybir.dt.from_np(a.dtype), kind="ExternalInput").ap())
    for i, (shape, dtype) in enumerate(_OUTS):
        dt = _mybir.dt.from_np(_np.dtype(dtype))
        args.append(nc.dram_tensor(f"out_{i}_dram", shape, dt, kind="ExternalOutput").ap())
    block_program(nc, *args)
    r = _run(nc, [arrays], core_ids=[0])
    got = tuple(r.results[0][f"out_{i}_dram"] for i in range(len(_OUTS)))
    return got[0]
```

```python
from contextlib import ExitStack

import numpy as np

import concourse.bass as bass
from concourse import mybir

F32 = mybir.dt.float32
F32R = mybir.dt.float32r
BF16 = mybir.dt.bfloat16
I32 = mybir.dt.int32
U32 = mybir.dt.uint32
ALU = mybir.AluOpType
ACT = mybir.ActivationFunctionType
AX = mybir.AxisListType

P = 128
N = 8
HID = 512
NC_ = HID // P
R = 16
G = 8
HG = 4
NH = G * HG
PAGE = 32
CACHED = 512
KC = CACHED // P
KEYS = CACHED + P
E = 8
SCALE = float(1.0 / np.sqrt(128.0))
EPS_RMS = 1e-6
NEG = -3.0e38
MASKED = -1.0e30
QW = HG * P
PW = QW + 2 * P
TILES_W = 10


def inverse_frequencies():
    return (np.float32(1.0) / np.power(np.float32(10000.0), np.arange(0, P, 2, dtype=np.float32) / np.float32(P))
            ).astype(np.float32)


def block_program(nc, x, ids_adapter, table_pages, cache_len, lora_a, lora_b, w_qkv, w_proj, wq, wk, wv, wo,
                  q_norm, k_norm, k_cache, v_cache, w_base, b_base, w_gate, ex_a, ex_b, out):
    KB = 1024
    base0 = (nc.sbuf_base + 63) // 64 * 64
    ctx = ExitStack()
    with ctx:
        def at(name, shape, dt, kb):
            return nc.alloc_sbuf_tensor_at(name, shape, dt, offset=base0 + int(kb * KB))

        def sem(name):
            return ctx.enter_context(nc.semaphore(name))

        wraw = at("wraw", [P, 2, 6, HID], F32, 0)
        wpraw = at("wpraw", [P, 2, 4, HID], F32, 24)
        fold_v = at("fold_v", [P, 4, G, HID], F32, 40)
        xin = at("xin", [P, N, HID], F32, 40)
        xT = at("xT", [P, NC_, N, P], F32, 56)
        bsel = at("bsel", [P, HID], F32, 72)
        bselT = at("bselT", [P, NC_, P], F32, 74)
        tabs = at("tabs", [P, N, 4, P], F32, 184)
        maskall = at("maskall", [P, N, CACHED], BF16, 174)
        score = at("score", [P, N, NH, N], F32, 104)
        theta = at("theta", [P, N, 64], F32, 136)
        turns = at("turns", [P, N, 64], F32, 138)
        turns2 = at("turns2", [P, N, 64], F32, 140)
        sin_t = at("sin_t", [P, N, 64], F32, 142)
        cos_t = at("cos_t", [P, N, 64], F32, 144)
        keyidx = at("keyidx", [P, CACHED], F32, 202.5)
        freqs = at("freqs", [P, 64], F32, 172.5)
        qn_b = at("qn_b", [P, P], F32, 172.75)
        kn_b = at("kn_b", [P, P], F32, 173.25)
        z_ring = at("z_ring", [P, 2, NH, 2 * R], F32, 112)
        zT_ring = at("zT_ring", [P, 2, G, P], F32, 120)
        xres = at("xres", [P, 2, HID], F32, 128)
        x2sb = at("x2sb", [P, 2, HID], F32, 132)
        wT = at("wT", [P, 6, NC_, P], F32, 136)
        folded = at("folded", [P, 6, P], F32, 148)
        mix = at("mix", [P, HG, P], F32, 151)
        wpT = at("wpT", [P, HG, HID], F32, 153)
        prod = at("prod", [P, 2, HG, P], F32, 161)
        zlT = at("zlT", [P, N, P], F32, 165)
        aall = at("aall", [P, N, NC_, R], F32, 169)
        x2T_hi = at("x2T_hi", [P, NC_, N, P], F32R, 0)
        x2T_lo = at("x2T_lo", [P, NC_, N, P], F32R, 16)
        y = at("y", [P, N, HID], F32, 32)
        wo_hi = at("wo_hi", [P, 2, HG, HID], F32R, 48)
        wo_lo = at("wo_lo", [P, 2, HG, HID], F32R, 64)
        pT_hi = at("pT_hi", [P, KC + 1, QW], F32R, 80)
        pT_lo = at("pT_lo", [P, KC + 1, QW], F32R, 90)
        sm = at("sm", [P, HG, KEYS], F32, 100)
        oT_hi = at("oT_hi", [P, HG, P], F32R, 110)
        oT_lo = at("oT_lo", [P, HG, P], F32R, 112)
        qT_hi = at("qT_hi", [P, QW], F32R, 114)
        qT_lo = at("qT_lo", [P, QW], F32R, 116)
        rope_a = at("rope_a", [P, HG + 1, P], F32, 118)
        rope_b = at("rope_b", [P, HG + 1, P], F32, 120.5)
        kT_hi = at("kT_hi", [P, 2, KEYS], F32R, 123)
        kT_lo = at("kT_lo", [P, 2, KEYS], F32R, 128)
        wa_hi = at("wa_hi", [P, 2, NC_, PW], F32R, 136)
        wa_lo = at("wa_lo", [P, 2, NC_, PW], F32R, 160)
        wtile = at("wtile", [P, 2, HID], F32, 184)
        kraw = at("kraw", [P, 2, KC, P], F32, 188)
        vraw = at("vraw", [P, 2, KC, P], F32, 192)
        tab = at("tab", [P, 2, 4, P], F32, 196)
        mask = at("mask", [P, 2, KEYS], BF16, 200)
        v_hi = at("v_hi", [P, KC + 1, P], F32R, 202.5)
        v_lo = at("v_lo", [P, KC + 1, P], F32R, 133)
        squares = at("squares", [P, P], F32, 135.5)
        wbraw = at("wbraw", [P, NC_, HID], F32, 136)
        earaw = at("earaw", [P, HID], F32, 144)
        gateraw = at("gateraw", [E, HID], F32, 146)
        ebraw = at("ebraw", [P, E, NC_, R], F32, 148)
        wbT = at("wbT", [P, NC_, HID], F32, 150)
        gaT = at("gaT", [P, NC_, P + E], F32, 158)
        ebT = at("ebT", [P, HID], F32, 161)
        yT = at("yT", [P, 2, NC_, P], F32, 163)
        hw = at("hw", [P, 2, E, R], F32, 167)
        hwT = at("hwT", [P, 2, P], F32, 168)
        bias_b = at("bias_b", [P, HID], F32, 169)
        x2r = at("x2r", [P, 2, HID], F32, 171)
        fin = at("fin", [P, 2, HID], F32, 175)
        routes = at("routes", [P, 2, 8, E], F32, 179)
        pairs = at("pairs", [P, 2, 4, E, E], F32, 179.5)
        route1 = at("route1", [P, 2, 4], F32, 181.5)
        ebj = at("ebj", [P, NC_, E, R], F32, 32 - 16)
        before = at("before", [P, E, E], F32, 182)
        ident = at("ident", [P, P], F32, 205)
        zl = at("zl", [P, N, R], F32, 205.5)
        SM = 206.0
        blockmask = at("blockmask", [P, N], F32, SM)
        pos = at("pos", [P, N], F32, SM + 0.03125)
        len_i = at("len_i", [P, N], I32, SM + 0.0625)
        len_f = at("len_f", [P, N], F32, SM + 0.09375)
        tok = at("tok", [P, 1], F32, SM + 0.125)
        id_sb = at("id_sb", [1, N], I32, SM + 0.15625)
        ss = at("ss", [P, 2, HG + 1], F32, SM + 0.1875)
        ms = at("ms", [P, 2, HG + 1], F32, SM + 0.25)
        rs = at("rs", [P, 2, HG + 1], F32, SM + 0.3125)
        qs = at("qs", [P, 2, HG], F32, SM + 0.375)
        mn = at("mn", [P, HG], F32, SM + 0.40625)
        den = at("den", [P, HG], F32, SM + 0.4375)
        rd = at("rd", [P, HG], F32, SM + 0.46875)
        halfs = at("halfs", [P, HG + 1], F32, SM + 0.5)
        idx_a = at("idx_a", [P, N * KC], I32, SM + 0.53125)
        idx_b = at("idx_b", [P, N * KC], I32, SM + 0.65625)
        slot8 = at("slot8", [P, 1], I32, SM + 0.78125)
        kvown = at("kvown", [P, 2, P], F32, SM + 0.8125)
        rmax = at("rmax", [P, N * NH], F32, 182)
        rden = at("rden", [P, N * NH], F32, 183)
        pages = at("pages", [P, N * 16], I32, 172)

        ps_a = ctx.enter_context(nc.psum_tensor("ps_a", [P, 2 * HID], F32))
        ps_b = ctx.enter_context(nc.psum_tensor("ps_b", [P, 2 * HID], F32))
        ps_t = [ctx.enter_context(nc.psum_tensor(f"ps_t{i}", [P, HID], F32)) for i in range(2)]
        ps_q = ctx.enter_context(nc.psum_tensor("ps_q", [P, HID], F32))
        ps_o = ctx.enter_context(nc.psum_tensor("ps_o", [P, HID], F32))
        ps_s = [ps_a, ps_b]
        ps_k = ps_b[:, KEYS:KEYS + P]

        x2_d = nc.dram_tensor("x2_scratch", [N, P, HID], F32, kind="Internal").ap()
        tab_d = nc.dram_tensor("tab_scratch", [N, P, 4 * P], F32, kind="Internal").ap()
        mask_d = nc.dram_tensor("mask_scratch", [N, P, CACHED], BF16, kind="Internal").ap()
        freq_d = nc.inline_tensor(inverse_frequencies().reshape(1, 64), "rotary_freqs").ap()

        k_rows = k_cache.rearrange("a s g d -> (a s g) d")
        v_rows = v_cache.rearrange("a s g d -> (a s g) d")

        x_in = [sem(f"x_in{i}") for i in range(2)]
        id_in = sem("id_in")
        lora_in = sem("lora_in")
        small_in = sem("small_in")
        pages_in = sem("pages_in")
        ident_ok = sem("ident_ok")
        bmask_ok = sem("bmask_ok")
        iota_ok = sem("iota_ok")
        xt_full = sem("xt_full")
        xt_act = sem("xt_act")
        xt_dve = sem("xt_dve")
        bt_full = sem("bt_full")
        bt_done = sem("bt_done")
        zT_full = sem("zT_full")
        zT_done = sem("zT_done")
        zl_full = sem("zl_full")
        zl_done = sem("zl_done")
        tb = sem("tb")
        sin_ok = sem("sin_ok")
        tab_out = sem("tab_out")
        idx_ok = sem("idx_ok")
        wq_in = [sem(f"wq_in{i}") for i in range(2)]
        wp_in = [sem(f"wp_in{i}") for i in range(2)]
        t2_full = sem("t2_full")
        t2_done = sem("t2_done")
        fold_full = sem("fold_full")
        fold_done = sem("fold_done")
        mix_full = sem("mix_full")
        mix_done = sem("mix_done")
        y_full = sem("y_full")
        y_done = sem("y_done")
        y_red = sem("y_red")
        fv_full = sem("fv_full")
        fv_even = sem("fv_even")
        fv_odd = sem("fv_odd")
        smx = sem("smx")
        exp2 = sem("exp2")
        prob = sem("prob")
        z_done = sem("z_done")
        zt_full = sem("zt_full")
        zt_done = sem("zt_done")
        out2_full = sem("out2_full")
        out2_done = sem("out2_done")
        xres_in = [sem(f"xres_in{i}") for i in range(2)]
        x2_out = [sem(f"x2_out{i}") for i in range(2)]
        x2t_full = sem("x2t_full")
        x2t_hi = sem("x2t_hi")
        x2t_lo = sem("x2t_lo")
        wt_in = [sem(f"wt_in{i}") for i in range(2)]
        tab_in = [sem(f"tab_in{i}") for i in range(2)]
        kg_in = [sem(f"kg_in{i}") for i in range(2)]
        vg_in = [sem(f"vg_in{i}") for i in range(2)]
        init3 = sem("init3")
        t_full = sem("t_full")
        t_hi = sem("t_hi")
        t_lo = sem("t_lo")
        s_full = sem("s_full")
        s_read = sem("s_read")
        e_done = sem("e_done")
        r_done = sem("r_done")
        p_dve = sem("p_dve")
        p_act = sem("p_act")
        aq_full = sem("aq_full")
        akv_full = sem("akv_full")
        sq_done = sem("sq_done")
        st_pool = sem("st_pool")
        st_done = sem("st_done")
        kt_full = sem("kt_full")
        kt_hi = sem("kt_hi")
        kt_lo = sem("kt_lo")
        rms_k = sem("rms_k")
        ro_ab = sem("ro_ab")
        rq_done = sem("rq_done")
        kv_copied = sem("kv_copied")
        sqq_done = sem("sqq_done")
        smx0 = sem("smx0")
        rk_ab = sem("rk_ab")
        rk_done = sem("rk_done")
        vs_hi = sem("vs_hi")
        vs_lo = sem("vs_lo")
        vc_hi = sem("vc_hi")
        vc_lo = sem("vc_lo")
        pv_full = sem("pv_full")
        o_hi = sem("o_hi")
        o_lo = sem("o_lo")
        f_full = sem("f_full")
        f_done = sem("f_done")
        ix_ok = sem("ix_ok")
        lw_in = sem("lw_in")
        lt_full = sem("lt_full")
        lt_done = sem("lt_done")
        x2r_in = [sem(f"x2r_in{i}") for i in range(2)]
        yt_full = sem("yt_full")
        yt_done = sem("yt_done")
        g_full = sem("g_full")
        gm = sem("gm")
        ge = sem("ge")
        rt = sem("rt")
        hw_done = sem("hw_done")
        ht_full = sem("ht_full")
        ht_done = sem("ht_done")
        d_full = sem("d_full")
        fin_done = sem("fin_done")
        fin_out = [sem(f"fin_out{i}") for i in range(2)]
        bias_ok = sem("bias_ok")
        x2b = sem("x2b")
        eb_ok = sem("eb_ok")
        waits_alone = sem("waits_alone")

        W_FIRST = {0: 0, 1: 1, 2: 3, 3: 4, 4: 6, 5: 7, 6: 9}
        W_COUNT = {0: 1, 1: 2, 2: 1, 3: 2, 4: 1, 5: 2, 6: 1, 7: 0}
        PRO = TILES_W + 2

        def groups_of(n, last):
            w = [] if last else [f"W{W_FIRST[n] + i}" for i in range(W_COUNT[n])] if W_COUNT[n] else []
            nxt = not (last and n == N - 1)
            return w + ["K"] * nxt + ["D0", "D1", "D2"] + ["q"] * nxt + ["D3", "DS"]

        PER_G = sum(len(groups_of(n, False)) for n in range(N))
        assert PER_G % 2 == 0

        def t_index(n, name, last):
            i = sum(len(groups_of(m, last)) for m in range(n)) + groups_of(n, last).index(name)
            return i, (PRO + i) % 2

        LATE_DMAS = 3 + E + 1
        TB_ALL = 32
        TB_ANGLES = 16
        SOFT = [(0, 2), (2, 2), (4, 4)]
        PAIRS = [(s, tp) for s in range(N) for tp in range(s // 2 + 1)]

        def y_bank(s, end):
            if end:
                return ps_a[:, (s % 2) * HID:(s % 2 + 1) * HID]
            return ps_o if s % 2 == 0 else ps_q

        def w_dst(wa, wo_t, wpar, t):
            one = bass.ds(wpar, 1)
            if t < 6:
                return wa[:, one, :, t * P:(t + 1) * P].rearrange("p a c m -> p (a c) m")
            return wo_t[:, one, :, (t - 6) * P:(t - 5) * P].rearrange("p a h m -> p (a h) m")

        def hi_lo_target(name, g, kpar1, lo):
            if name == "K":
                return (kT_hi, kT_lo)[lo][:, kpar1, 0:CACHED], HID
            if name == "q":
                return (qT_hi, qT_lo)[lo][:, :], HID
            pT = (pT_hi, pT_lo)[lo]
            if name == "DS":
                return pT[:, KC, :], HID
            if name[0] == "D":
                h = int(name[1])
                return pT[:, 0:KC, h * P:(h + 1) * P], HID
            return w_dst((wa_hi, wa_lo)[lo], (wo_hi, wo_lo)[lo], (g + 1) % 2, int(name[1:])), HID

        def wait_alone(eng, s, value):
            eng.wait_ge(s, value)
            eng.sem_inc(waits_alone, 1)

        block = ctx.enter_context(nc.Block())

        @block.sync
        def _(sp):
            sp.dma_start(id_sb[:], ids_adapter.rearrange("(o n) -> o n", o=1)).then_inc(id_in, 16)
            sp.dma_start(len_i[:], cache_len.rearrange("(o n) -> o n", o=1).broadcast_to([P, N])).then_inc(small_in, 16)
            sp.dma_start(freqs[:], freq_d.broadcast_to([P, 64])).then_inc(small_in, 16)
            sp.dma_start(qn_b[:], q_norm.rearrange("(o d) -> o d", o=1).broadcast_to([P, P])).then_inc(small_in, 16)
            sp.dma_start(kn_b[:], k_norm.rearrange("(o d) -> o d", o=1).broadcast_to([P, P])).then_inc(small_in, 16)
            sp.dma_start(pages[:], table_pages.rearrange("(o n) k -> o (n k)", o=1).broadcast_to([P, N * 16])
                         ).then_inc(pages_in, 16)
            for h in range(2):
                sp.dma_start(xin[:, 4 * h:4 * h + 4, :], x[4 * h:4 * h + 4].rearrange("n b i -> b n i")
                             ).then_inc(x_in[h], 16)
            sp.wait_ge(id_in, 16)
            for n in range(N):
                a_id = sp.value_load(id_sb[0:1, n:n + 1], min_val=0, max_val=7)
                sp.dma_start(bsel[R * n:R * n + R, :],
                             lora_b[bass.ds(a_id, 1), :, :].rearrange("a r i -> (a r) i")).then_inc(lora_in, 16)
                sp.dma_start(aall[:, n, :, :].rearrange("p j r -> p (j r)"),
                             lora_a[bass.ds(a_id, 1), :, :].rearrange("a (p j) r -> (a p) (j r)", j=NC_)
                             ).then_inc(lora_in, 16)

            def load_weights(g, par):
                sp.dma_start(wraw[:, par, :, :],
                             w_qkv[bass.ds(g * 6 * P, 6 * P), :].rearrange("(t p) o -> p t o", p=P)
                             ).then_inc(wq_in[par], 16)
                sp.dma_start(wpraw[:, par, :, :],
                             w_proj[:, bass.ds(g * QW, QW)].rearrange("(t p) e -> p t e", p=P)
                             ).then_inc(wp_in[par], 16)

            load_weights(0, 0)
            load_weights(1, 1)
            with sp.Fori(0, G // 2 - 1) as gp:
                for par in range(2):
                    wait_alone(sp, t2_full, (gp * 2 + par + 1) * 10)
                    load_weights(gp * 2 + par + 2, par)

            for s in range(2):
                sp.dma_start(xres[:, s, :], x[s]).then_inc(xres_in[s], 16)
            def load_tables(n, par):
                sp.dma_start(tab[:, par, :, :].rearrange("p a d -> p (a d)"), tab_d[n]).then_inc(tab_in[par], 16)
                sp.dma_start(mask[:, par, 0:CACHED], mask_d[n]).then_inc(tab_in[par], 16)

            def load_wtile(g, t, slot):
                if t < HG:
                    src = wq[bass.ds(g * QW + t * P, P), :]
                elif t == HG:
                    src = wk[bass.ds(g * P, P), :]
                elif t == HG + 1:
                    src = wv[bass.ds(g * P, P), :]
                else:
                    src = wo[(t - 6) * P:(t - 5) * P, bass.ds(g * QW, QW)]
                sp.dma_start(wtile[:, slot, :], src).then_inc(wt_in[slot], 16)

            for s in range(N):
                if s == 2:
                    sp.wait_ge(tb, TB_ALL)
                    for n in range(N):
                        sp.dma_start(tab_d[n], tabs[:, n, :, :].rearrange("p a d -> p (a d)")).then_inc(tab_out, 16)
                        sp.dma_start(mask_d[n], maskall[:, n, :]).then_inc(tab_out, 16)
                sp.wait_ge(out2_done, s + 1)
                sp.dma_start(x2_d[s], x2sb[:, s % 2, :]).then_inc(x2_out[s % 2], 16)
                if s + 2 < N:
                    sp.dma_start(xres[:, s % 2, :], x[s + 2]).then_inc(xres_in[s % 2], 16)
                if s == 5:
                    sp.wait_ge(tab_out, 32 * N)
                    load_tables(0, 0)
                    load_tables(1, 1)
                    load_wtile(0, 0, 0)
                    load_wtile(0, 1, 1)

            for t in range(2, TILES_W):
                sp.wait_ge(t_full, t - 1)
                load_wtile(0, t, t % 2)

            def step(g, n, last):
                J = g * N + n
                base = g * PER_G + PRO
                if not last and n == 0:
                    wait_alone(sp, t_full, base)
                    load_wtile(g + 1, 0, 0)
                    load_wtile(g + 1, 1, 1)
                for name in groups_of(n, last):
                    if name[0] == "W" and int(name[1:]) + 2 < TILES_W:
                        t = int(name[1:])
                        wait_alone(sp, t_full, base + t_index(n, name, last)[0] + 1)
                        load_wtile(g + 1, t + 2, t % 2)
                if not (last and n >= N - 2):
                    wait_alone(sp, s_read, J * 4 + 4 + 2)
                    load_tables((n + 2) % N, n % 2)

            with sp.Fori(0, G - 1) as g:
                for n in range(N):
                    step(g, n, False)
            for n in range(N):
                step(G - 1, n, True)

            sp.wait_ge(f_full, N * G)
            sp.dma_start(wbraw[:], w_base.rearrange("(t p) i -> p t i", p=P)).then_inc(lw_in, 16)
            sp.dma_start(earaw[:], ex_a.rearrange("e r i -> (e r) i")).then_inc(lw_in, 16)
            sp.dma_start(gateraw[:], w_gate).then_inc(lw_in, 16)
            for e in range(E):
                sp.dma_start(ebraw[:, e, :, :].rearrange("p j r -> p (j r)"),
                             ex_b[e].rearrange("(p j) r -> p (j r)", j=NC_)).then_inc(lw_in, 16)
            sp.dma_start(bias_b[:], b_base.rearrange("(o i) -> o i", o=1).broadcast_to([P, HID])).then_inc(lw_in, 16)
            for i in range(2):
                sp.wait_ge(x2_out[i], 16 * (N // 2))
            for n in range(2):
                sp.dma_start(x2r[:, n, :], x2_d[n]).then_inc(x2r_in[n], 16)
            for n in range(N):
                sp.wait_ge(fin_done, n + 1)
                sp.dma_start(out[n], fin[:, n % 2, :]).then_inc(fin_out[n % 2], 16)
                if n + 2 < N:
                    sp.dma_start(x2r[:, n % 2, :], x2_d[n + 2]).then_inc(x2r_in[n % 2], 16)
            for i in range(2):
                sp.wait_ge(fin_out[i], 16 * (N // 2))

        @block.gpsimd
        def _(pool):
            pool.memset(ident[:], 0.0).then_inc(ident_ok, 1)
            pool.wait_ge(ident_ok, 1)
            pool.affine_select(out=ident[:], in_=ident[:], compare_op=ALU.not_equal, fill=1.0, base=0,
                               pattern=[[-1, P]], channel_multiplier=1).then_inc(ident_ok, 1)
            pool.memset(blockmask[:], 1.0).then_inc(bmask_ok, 1)
            pool.iota(tok[:], pattern=[[0, 1]], base=0, channel_multiplier=1,
                      allow_small_or_imprecise_dtypes=True).then_inc(iota_ok, 1)
            pool.iota(keyidx[:], pattern=[[1, CACHED]], base=0, channel_multiplier=0,
                      allow_small_or_imprecise_dtypes=True).then_inc(iota_ok, 1)
            pool.iota(slot8[:], pattern=[[0, 1]], base=0, channel_multiplier=8).then_inc(iota_ok, 1)
            pool.wait_ge(bmask_ok, 1)
            pool.affine_select(out=blockmask[:], in_=blockmask[:], compare_op=ALU.is_ge, fill=0.0, base=0,
                               pattern=[[-R, N]], channel_multiplier=1).then_inc(bmask_ok, 1)
            pool.wait_ge(bmask_ok, 2)
            pool.affine_select(out=blockmask[:], in_=blockmask[:], compare_op=ALU.is_ge, fill=0.0, base=R - 1,
                               pattern=[[R, N]], channel_multiplier=-1).then_inc(bmask_ok, 1)
            pool.memset(halfs[:], -0.5).then_inc(iota_ok, 1)
            pool.memset(mask[:, :, CACHED:KEYS], 0.0).then_inc(iota_ok, 1)
            pool.wait_ge(pages_in, 16)
            pool.wait_ge(iota_ok, 5)
            for q in range(4):
                rows = slice(PAGE * q, PAGE * q + PAGE)
                pool.tensor_scalar(idx_a[rows, :], pages[rows, :].rearrange("p (m q) -> p m q", q=4)[:, :, q],
                                   float(PAGE * G), float(-PAGE * G * q), ALU.mult, ALU.add).then_inc(idx_ok, 1)
            pool.wait_ge(idx_ok, 4)
            pool.tensor_tensor(idx_a[:], idx_a[:], slot8[:].broadcast_to([P, N * KC]), ALU.add).then_inc(idx_ok, 1)
            pool.wait_ge(idx_ok, 5)

            def gather(rows_d, raw, arrived, idx, n, par):
                for c in range(KC):
                    k = n * KC + c
                    pool.indirect_dma_start(raw[:, par, c, :], None, rows_d,
                                            bass.IndirectOffsetOnAxis(idx[:, k:k + 1].bitcast(U32), 0)
                                            ).then_inc(arrived[par], 16)

            pool.wait_ge(tab_out, 32 * N)
            for n in range(2):
                gather(k_rows, kraw, kg_in, idx_a, n, n)
                gather(v_rows, vraw, vg_in, idx_a, n, n)

            def stats(J, par):
                wait_alone(pool, sq_done, J + 1)
                pool.tensor_scalar(ms[:, par, HG:], ss[:, par, HG:], 1.0 / P, EPS_RMS, ALU.mult, ALU.add
                                   ).then_inc(st_pool, 1)
                wait_alone(pool, st_pool, J * 3 + 1)
                pool.tensor_tensor(rs[:, par, HG:], ms[:, par, HG:], halfs[:, HG:], ALU.pow).then_inc(rms_k, 1)
                wait_alone(pool, sqq_done, (J + 1) * HG + 1)
                pool.tensor_scalar(ms[:, par, 0:HG], ss[:, par, 0:HG], 1.0 / P, EPS_RMS, ALU.mult, ALU.add
                                   ).then_inc(st_pool, 1)
                wait_alone(pool, st_pool, J * 3 + 2)
                pool.tensor_tensor(rs[:, par, 0:HG], ms[:, par, 0:HG], halfs[:, 0:HG], ALU.pow).then_inc(st_pool, 1)
                wait_alone(pool, st_pool, J * 3 + 3)
                pool.tensor_scalar(qs[:, par, :], rs[:, par, 0:HG], -SCALE, None, ALU.mult).then_inc(st_done, 1)

            stats(0, 0)
            for i in range(2):
                pool.wait_ge(x2_out[i], 16 * (N // 2))

            def step(g, n, last):
                J = g * N + n
                par = n % 2
                more = not (last and n >= N - 2)
                if n == 0 and not last:
                    pool.tensor_scalar(idx_b[:], idx_a[:], 1.0, None, ALU.add).then_inc(ix_ok, 1)
                    wait_alone(pool, ix_ok, g * 2 + 1)
                idx = idx_a if n < N - 2 else idx_b
                if more:
                    wait_alone(pool, t_full, g * PER_G + PRO + sum(len(groups_of(m, last)) for m in range(n)))
                    gather(k_rows, kraw, kg_in, idx, (n + 2) % N, par)
                wait_alone(pool, vg_in[par], (g * 4 + n // 2 + 1) * 64)
                wait_alone(pool, pv_full, J + 1)
                pool.tensor_copy(v_hi[:, 0:KC, :], vraw[:, par, :, :]).then_inc(vc_hi, 1)
                wait_alone(pool, vc_hi, J + 1)
                pool.tensor_tensor(v_lo[:, 0:KC, :], vraw[:, par, :, :], v_hi[:, 0:KC, :].bitcast(F32),
                                   ALU.subtract).then_inc(vc_lo, 1)
                if more:
                    wait_alone(pool, vc_lo, J + 1)
                    gather(v_rows, vraw, vg_in, idx, (n + 2) % N, par)
                if not (last and n == N - 1):
                    stats(J + 1, 1 - par)
                if n == N - 1 and not last:
                    wait_alone(pool, kg_in[1], (g * 4 + 4) * 64)
                    wait_alone(pool, vg_in[1], (g * 4 + 4) * 64)
                    pool.tensor_copy(idx_a[:], idx_b[:]).then_inc(ix_ok, 1)
                    wait_alone(pool, ix_ok, g * 2 + 2)
                    wait_alone(pool, kg_in[1], (g * 4 + 5) * 64)
                    wait_alone(pool, vg_in[1], (g * 4 + 5) * 64)
                    wait_alone(pool, kg_in[0], (g * 4 + 5) * 64)
                    wait_alone(pool, vg_in[0], (g * 4 + 5) * 64)

            with pool.Fori(0, G - 1) as g:
                for n in range(N):
                    step(g, n, False)
            for n in range(N):
                step(G - 1, n, True)
            pool.wait_ge(f_full, N * G)
            pool.memset(before[:], 1.0).then_inc(bias_ok, 1)
            pool.wait_ge(bias_ok, 1)
            pool.affine_select(out=before[:], in_=before[:], compare_op=ALU.is_gt, fill=0.0, base=0,
                               pattern=[[1, E], [-1, E]], channel_multiplier=0).then_inc(bias_ok, 1)
            pool.wait_ge(lw_in, 16 * LATE_DMAS)
            pool.tensor_copy(ebj[:, :, :, :], ebraw[:, :, :, :].rearrange("p e j r -> p j e r")).then_inc(eb_ok, 1)
            for n in range(N):
                pool.wait_ge(x2r_in[n % 2], 16 * (n // 2 + 1))
                pool.tensor_tensor(x2r[:, n % 2, :], x2r[:, n % 2, :], bias_b[:], ALU.add).then_inc(x2b, 1)

        def mm3(pe, o, l_hi, l_lo, r_hi, r_lo, start, stop):
            pe.matmul(o, l_hi, r_lo, start=start, stop=False)
            pe.matmul(o, l_lo, r_hi, start=False, stop=False)
            return pe.matmul(o, l_hi, r_hi, start=False, stop=stop)

        @block.tensor
        def _(pe):
            pe.wait_ge(ident_ok, 2)
            for n in range(N):
                pe.wait_ge(x_in[n // 4], 16)
                if n >= 2:
                    pe.wait_ge(xt_act if n % 2 == 0 else xt_dve, n // 2)
                for c in range(NC_):
                    mm = pe.transpose(ps_t[n % 2][:, c * P:(c + 1) * P], xin[:, n, c * P:(c + 1) * P], ident[:])
                mm.then_inc(xt_full, 1)
            pe.wait_ge(lora_in, 32 * N)
            for c in range(NC_):
                mm = pe.transpose(ps_q[:, c * P:(c + 1) * P], bsel[:, c * P:(c + 1) * P], ident[:])
            mm.then_inc(bt_full, 1)
            pe.wait_ge(bt_done, 1)
            pe.wait_ge(xt_act, 4)
            pe.wait_ge(xt_dve, 4)
            for h in range(2):
                for c in range(NC_):
                    mm = pe.matmul(ps_a[:, h * HID:(h + 1) * HID], bselT[:, c, :],
                                   xT[:, c, 4 * h:4 * h + 4, :].rearrange("p n b -> p (n b)"),
                                   start=(c == 0), stop=(c == NC_ - 1))
                mm.then_inc(zT_full, 1)
            pe.wait_ge(zT_done, 2)
            for n in range(N):
                mm = pe.matmul(ps_o[:, n * R:(n + 1) * R], zlT[:, n, :], ident[:, n * R:(n + 1) * R],
                               start=True, stop=True)
            mm.then_inc(zl_full, 1)
            pe.wait_ge(zl_done, 1)

            def part_a(g, par, arrivals, new=True, old=True):
                t0 = g * 10
                go = g - 1

                def transposed(i, srcs):
                    pe.wait_ge(t2_done, t0 + i + 1)
                    for c, src in enumerate(srcs):
                        mm = pe.transpose(ps_t[i % 2][:, c * P:(c + 1) * P], src, ident[:])
                    return mm.then_inc(t2_full, 1)

                def w_group(t):
                    return transposed(t, [wraw[:, par, t, :].rearrange("p (o j) -> p o j", j=NC_)[:, :, j]
                                          for j in range(NC_)])

                def p_group(h):
                    return transposed(6 + h, [wpraw[:, par, ot, h * P:(h + 1) * P] for ot in range(NC_)])

                def fold(t):
                    pe.wait_ge(t2_done, t0 + t + 1 + 2)
                    for j in range(NC_):
                        mm = pe.matmul(ps_a[:, t * P:(t + 1) * P], wT[:, t, j, :], aall[:, :, j, :],
                                       start=(j == 0), stop=(j == NC_ - 1))
                    return mm

                def scores_s(s):
                    if s == 0:
                        pe.wait_ge(mix_done, go + 1)
                    pe.wait_ge(y_done, go * 8 + s + 1)
                    o = y_bank(s, not new)[:, 0:HG * R * (s + 1)]
                    pe.matmul(o.rearrange("p (h m) -> p h m", h=HG), zlT[:, s, :], mix[:, :, 0:R * (s + 1)],
                              start=True, stop=True).then_inc(y_full, 1)

                def fold_out(h):
                    if h == 0:
                        pe.wait_ge(t2_done, g * 10 + 2)
                    done = fv_even if h % 2 == 0 else fv_odd
                    pe.wait_ge(done, go * 2 + h // 2 + 1)
                    pe.matmul(ps_b[:, (h % 2) * HID:(h % 2 + 1) * HID], folded[:, 5, :], wpT[:, h, :],
                              start=True, stop=True).then_inc(fv_full, 1)

                if new:
                    pe.wait_ge(wq_in[par], arrivals)
                    w_group(0)
                    w_group(1)
                steps = [(scores_s, 0), (fold, 0), (fold_out, 0), (w_group, 2), (scores_s, 1), (fold, 1),
                         (fold_out, 1), (w_group, 3), (scores_s, 2), (fold, 2), (scores_s, 3), (w_group, 4),
                         (fold_out, 2), (fold, 3), (scores_s, 4), (w_group, 5), (fold_out, 3), (fold, 4),
                         (scores_s, 5), (p_group, 0), (scores_s, 6), (fold, 5), (p_group, 1), (scores_s, 7)]
                for what, i in steps:
                    if what in (scores_s, fold_out):
                        if old:
                            what(i)
                    elif new:
                        if what == p_group and i == 0:
                            pe.wait_ge(wp_in[par], arrivals)
                        mm = what(i)
                        if what == fold and i == 5:
                            mm.then_inc(fold_full, 1)
                if new:
                    p_group(2)
                    pe.wait_ge(fold_done, g + 1)
                    pe.wait_ge(y_done, g * 8 + 2)
                    for h in range(HG):
                        mm = pe.matmul(ps_q[:, h * P:(h + 1) * P], folded[:, h, :], folded[:, 4, :],
                                       start=True, stop=True)
                    mm.then_inc(mix_full, 1)
                    p_group(3)

            part_a(0, 0, 16, old=False)
            with pe.Fori(0, G // 2 - 1) as gp:
                for par in range(2):
                    part_a(gp * 2 + par + 1, 1 - par, (gp + 1 + par) * 16)
            part_a(G - 1, 1, G // 2 * 16)
            part_a(G, 0, 0, new=False)

            pe.wait_ge(t2_done, 10 * G + 2)
            pe.wait_ge(fv_even, 2 * G + 1)
            pe.wait_ge(fv_odd, 2 * G + 1)

            def z_transposes(k):
                pe.wait_ge(z_done, k + 1)
                for half in range(2):
                    if k >= 1:
                        pe.wait_ge(zt_done, 2 * (k - 1) + half + 1)
                    for i in range(4):
                        g = 4 * half + i
                        mm = pe.transpose(ps_t[half][:, i * P:(i + 1) * P],
                                          z_ring[:, k % 2, g * HG:(g + 1) * HG, :].rearrange("p h m -> p (h m)"),
                                          ident[:])
                    mm.then_inc(zt_full, 1)

            def z_products(k):
                s, tp = PAIRS[k]
                o = ps_o if s % 2 == 0 else ps_q
                if tp == 0 and s >= 2:
                    pe.wait_ge(out2_done, s - 1)
                for g in range(G):
                    if g % 4 == 0:
                        pe.wait_ge(zt_done, 2 * k + g // 4 + 1)
                    mm = pe.matmul(o[:, :], zT_ring[:, k % 2, g, :], fold_v[:, tp, g, :],
                                   start=(tp == 0 and g == 0), stop=(tp == s // 2 and g == G - 1))
                if tp == s // 2:
                    mm.then_inc(out2_full, 1)

            def x2_transposes(s):
                pe.wait_ge(out2_done, s + 1)
                if s >= 2:
                    pe.wait_ge(x2t_lo, s - 1)
                for c in range(NC_):
                    mm = pe.transpose(ps_b[:, (s % 2) * HID + c * P:(s % 2) * HID + (c + 1) * P],
                                      x2sb[:, s % 2, c * P:(c + 1) * P], ident[:])
                mm.then_inc(x2t_full, 1)

            z_transposes(0)
            for k in range(len(PAIRS)):
                if k + 1 < len(PAIRS):
                    z_transposes(k + 1)
                z_products(k)
                s, tp = PAIRS[k]
                if tp == 0 and s >= 1:
                    x2_transposes(s - 1)
            x2_transposes(N - 1)

            pe.sem_inc(pv_full, 1)

            def transposed(idx, bank, outs_ins):
                pe.wait_ge(t_lo, idx + 1)
                for o, i in outs_ins:
                    mm = pe.transpose(ps_t[bank][:, o * P:(o + 1) * P], i, ident[:])
                return mm.then_inc(t_full, 1)

            def w_tile(idx, bank, t, arrivals):
                pe.wait_ge(wt_in[t % 2], arrivals)
                transposed(idx, bank, [(c, wtile[:, t % 2, c * P:(c + 1) * P]) for c in range(NC_)])

            def k_group(idx, bank, g, n):
                pe.wait_ge(kg_in[n % 2], (g * 4 + n // 2 + 1) * 64)
                transposed(idx, bank, [(c, kraw[:, n % 2, c, :]) for c in range(KC)])

            def project_q(n, wpar, cs):
                for c in cs:
                    wh, wl = (w[:, bass.ds(wpar, 1), c, 0:QW].rearrange("p a m -> p (a m)") for w in (wa_hi, wa_lo))
                    mm = mm3(pe, ps_q[:, :], x2T_hi[:, c, n, :], x2T_lo[:, c, n, :], wh, wl, c == 0, c == NC_ - 1)
                if cs[-1] == NC_ - 1:
                    mm.then_inc(aq_full, 1)

            def project_kv(n, wpar):
                for c in range(NC_):
                    wh, wl = (w[:, bass.ds(wpar, 1), c, QW:PW].rearrange("p a m -> p (a m)") for w in (wa_hi, wa_lo))
                    mm = mm3(pe, ps_o[:, 0:2 * P], x2T_hi[:, c, n, :], x2T_lo[:, c, n, :], wh, wl,
                             c == 0, c == NC_ - 1)
                mm.then_inc(akv_full, 1)

            pe.wait_ge(zt_done, 2 * len(PAIRS))
            for t in range(TILES_W):
                w_tile(t, t % 2, t, 16 * (t // 2 + 1))
            pe.wait_ge(x2t_lo, N)
            pe.wait_ge(t_lo, 2 + TILES_W)
            project_q(0, 0, range(NC_))
            project_kv(0, 0)
            k_group(TILES_W, TILES_W % 2, 0, 0)
            pe.wait_ge(rq_done, 1)
            transposed(TILES_W + 1, (TILES_W + 1) % 2, [(h, rope_a[:, h, :]) for h in range(HG)])
            def own_k(J):
                pe.wait_ge(rk_done, J + 1)
                pe.transpose(ps_k, rope_a[:, HG, :], ident[:]).then_inc(kt_full, 1)

            def values(cs, own_group, last_head_group):
                for c in cs:
                    if c == 0:
                        pe.wait_ge(t_lo, last_head_group + 1 + 2)
                    if c == KC:
                        pe.wait_ge(t_lo, own_group + 1 + 2)
                    mm = mm3(pe, ps_o[:, :], v_hi[:, c, :], v_lo[:, c, :], pT_hi[:, c, :], pT_lo[:, c, :],
                             c == 0, c == KC)
                if cs[-1] == KC:
                    mm.then_inc(pv_full, 1)

            def out_proj(wpar, heads):
                for h in heads:
                    wh, wl = (w[:, bass.ds(wpar, 1), h, :].rearrange("p a m -> p (a m)") for w in (wo_hi, wo_lo))
                    mm = mm3(pe, ps_o[:, :], oT_hi[:, h, :], oT_lo[:, h, :], wh, wl, h == 0, h == HG - 1)
                if heads[-1] == HG - 1:
                    mm.then_inc(f_full, 1)

            own_k(0)

            def step(g, n, first, last):
                J = g * N + n
                base = g * PER_G + PRO
                par = n % 2
                names = groups_of(n, last)
                first = first and n == 0
                nxt = not (last and n == N - 1)
                n1 = (n + 1) % N
                wpar1 = (g + (n == N - 1)) % 2
                wpar0 = (g + (n == 0)) % 2
                start = base + t_index(n, names[0], last)[0]

                def idx(name):
                    i, bank = t_index(n, name, last)
                    return base + i, bank

                def scores(h):
                    pe.wait_ge(s_read, J * 4 + h + 1)
                    s, q = ps_s[h % 2], slice(h * P, (h + 1) * P)
                    mm3(pe, s[:, 0:CACHED], qT_hi[:, q], qT_lo[:, q], kT_hi[:, par, 0:CACHED],
                        kT_lo[:, par, 0:CACHED], True, True)
                    if h == 0:
                        pe.wait_ge(kt_lo, J + 1)
                    mm3(pe, s[:, CACHED:KEYS], qT_hi[:, q], qT_lo[:, q], kT_hi[:, par, CACHED:KEYS],
                        kT_lo[:, par, CACHED:KEYS], True, True).then_inc(s_full, 1)

                def probs_group(h):
                    pe.wait_ge(p_dve if h < 2 else p_act, J * 2 + h % 2 + 1)
                    transposed(*idx(f"D{h}"), [(c, sm[:, h, c * P:(c + 1) * P]) for c in range(KC)])

                pe.wait_ge(t_lo, start + (2 if first else 0))
                scores(0)
                scores(1)
                for name in names:
                    if name[0] == "W":
                        t = int(name[1:])
                        w_tile(*idx(name), t, (g + 1) * (16 * TILES_W // 2) + 16 * (t // 2 + 1))
                if not first:
                    pe.wait_ge(f_done, J)
                    pe.wait_ge(vc_lo, J)
                    values(range(KC + 1), start - 1, start - 2)
                if nxt:
                    k_group(*idx("K"), g + (n == N - 1), n1)
                    pe.wait_ge(rq_done, J + 1)
                    pe.wait_ge(sqq_done, (J + 1) * HG + 1)
                    if n == N - 1:
                        pe.wait_ge(t_lo, base + t_index(6, "W9", last)[0] + 1 + 2)
                    project_q(n1, wpar1, [0, 1])
                probs_group(0)
                scores(2)
                if nxt:
                    project_q(n1, wpar1, [2, 3])
                probs_group(1)
                scores(3)
                if not first:
                    pe.wait_ge(o_lo, J)
                if nxt:
                    pe.wait_ge(vs_lo, J + 1)
                    project_kv(n1, wpar1)
                probs_group(2)
                if not first:
                    if nxt:
                        pe.wait_ge(kv_copied, J + 2)
                    out_proj(wpar0, [0])
                if nxt:
                    pe.wait_ge(rq_done, J + 2)
                    transposed(*idx("q"), [(h, rope_a[:, h, :]) for h in range(HG)])
                if not first:
                    out_proj(wpar0, [1])
                    out_proj(wpar0, [2])
                probs_group(3)
                if not first:
                    out_proj(wpar0, [3])
                if nxt:
                    pe.wait_ge(s_read, J * 4 + 4 + 2)
                    own_k(J + 1)
                transposed(*idx("DS"), [(h, sm[:, h, CACHED:KEYS]) for h in range(HG)])

            for n in range(N):
                step(0, n, True, False)
            with pe.Fori(1, G - 1) as g:
                for n in range(N):
                    step(g, n, False, False)
            for n in range(N):
                step(G - 1, n, False, True)
            end = (G - 1) * PER_G + PRO + sum(len(groups_of(n, True)) for n in range(N))
            pe.wait_ge(f_done, G * N)
            pe.wait_ge(vc_lo, G * N)
            values(range(KC + 1), end - 1, end - 2)
            pe.wait_ge(o_lo, G * N)
            out_proj((G - 1) % 2, range(HG))

            pe.wait_ge(lw_in, 16 * (3 + E + 1))
            pe.wait_ge(t_lo, 2 + PRO + PER_G * (G - 1) + sum(len(groups_of(n, True)) for n in range(N)))

            def late(i, outs_ins, k=P, m=P):
                if i >= 2:
                    pe.wait_ge(lt_done, i - 1)
                for o, src in outs_ins:
                    mm = pe.transpose(ps_t[i % 2][0:m, o * P:o * P + k], src, ident[0:k, 0:k])
                mm.then_inc(lt_full, 1)

            for ot in range(NC_):
                late(ot, [(c, wbraw[:, ot, c * P:(c + 1) * P]) for c in range(NC_)])
            late(4, [(c, earaw[:, c * P:(c + 1) * P]) for c in range(NC_)])
            late(5, [(c, gateraw[:, c * P:(c + 1) * P]) for c in range(NC_)], k=E)
            pe.wait_ge(eb_ok, 1)
            late(6, [(j, ebj[:, j, :, :].rearrange("p e r -> p (e r)")) for j in range(NC_)])
            pe.wait_ge(lt_done, 7)
            pe.wait_ge(f_done, N * G + 1)

            def y_transposes(n):
                if n >= 2:
                    pe.wait_ge(yt_done, n - 1)
                for c in range(NC_):
                    mm = pe.transpose(ps_t[n % 2][:, c * P:(c + 1) * P], y[:, n, c * P:(c + 1) * P], ident[:])
                mm.then_inc(yt_full, 1)

            def base_and_gate(n):
                pe.wait_ge(yt_done, n + 1)
                if n >= 2:
                    pe.wait_ge(fin_done, n - 1)
                    pe.wait_ge(hw_done, n - 1)
                for c in range(NC_):
                    pe.matmul(ps_b[:, (n % 2) * HID:(n % 2) * HID + P + E], yT[:, n % 2, c, :], gaT[:, c, :],
                              start=(c == 0), stop=(c == NC_ - 1)).then_inc(g_full, 1)
                for c in range(NC_):
                    pe.matmul(ps_a[:, (n % 2) * HID:(n % 2 + 1) * HID], yT[:, n % 2, c, :], wbT[:, c, :],
                              start=(c == 0), stop=False)

            def experts(n):
                pe.wait_ge(hw_done, n + 1)
                if n >= 1:
                    pe.wait_ge(ht_done, n)
                pe.transpose(ps_q[:, 0:P], hw[:, n % 2, :, :].rearrange("p e r -> p (e r)"), ident[:]
                             ).then_inc(ht_full, 1)
                pe.wait_ge(ht_done, n + 1)
                pe.matmul(ps_a[:, (n % 2) * HID:(n % 2 + 1) * HID], hwT[:, n % 2, :], ebT[:, :],
                          start=False, stop=True).then_inc(d_full, 1)

            y_transposes(0)
            for n in range(N):
                if n + 1 < N:
                    y_transposes(n + 1)
                base_and_gate(n)
                if n >= 1:
                    experts(n - 1)
            experts(N - 1)

        @block.scalar
        def _(act):
            for n in range(0, N, 2):
                act.wait_ge(xt_full, n + 1)
                act.activation(xT[:, :, n, :], ps_t[0][:, :].rearrange("p (c b) -> p c b", c=NC_), ACT.Copy
                               ).then_inc(xt_act, 1)
            act.wait_ge(xt_dve, N // 2)
            act.sem_inc(t2_done, 2)
            act.sem_inc(fv_even, 1)

            def fold_v_copy(g, h, tps):
                for tp in tps:
                    ins = act.activation(
                        fold_v[2 * R * h:2 * R * h + 2 * R, tp, bass.ds(g, 1), :].rearrange("p a m -> p (a m)"),
                        ps_b[2 * R * tp:2 * R * tp + 2 * R, (h % 2) * HID:(h % 2 + 1) * HID], ACT.Copy)
                if tps[-1] == 3:
                    ins.then_inc(fv_even if h % 2 == 0 else fv_odd, 1)

            def part_a(g, old=True):
                def copy_group(i):
                    act.wait_ge(t2_full, g * 10 + i + 1)
                    if i < 6:
                        dst, src = wT[:, i, :, :], ps_t[i % 2][:, :].rearrange("p (c b) -> p c b", c=NC_)
                    else:
                        dst, src = wpT[:, i - 6, :], ps_t[i % 2][:, :]
                    act.activation(dst, src, ACT.Copy).then_inc(t2_done, 1)

                for i in range(10):
                    copy_group(i)
                    if old and 2 <= i < 6:
                        h = 0 if i < 4 else 2
                        act.wait_ge(fv_full, (g - 1) * 4 + h + 1)
                        fold_v_copy(g - 1, h, range(2) if i % 2 == 0 else range(2, 4))
                    if i == 7:
                        act.wait_ge(fold_full, g + 1)
                        act.activation(folded[:, :, :].rearrange("p a m -> p (a m)"), ps_a[:, 0:6 * P], ACT.Copy
                                       ).then_inc(fold_done, 1)

            part_a(0, old=False)
            with act.Fori(1, G) as g:
                part_a(g)

            def soft_exp(i):
                s0, count = SOFT[i]
                act.wait_ge(smx, 4 * i + 2)
                sc = score[:, s0:s0 + count, :, :].rearrange("p s h t -> p (s h t)")
                act.activation(sc, sc, ACT.Exp, scale=SCALE).then_inc(exp2, 1)

            def zt_copy(k):
                for half in range(2):
                    act.wait_ge(zt_full, 2 * k + half + 1)
                    act.activation(zT_ring[:, k % 2, 4 * half:4 * half + 4, :].rearrange("p g m -> p (g m)"),
                                   ps_t[half][:, :], ACT.Copy).then_inc(zt_done, 1)

            for h in range(HG):
                act.wait_ge(fv_full, (G - 1) * 4 + h + 1)
                fold_v_copy(G - 1, h, range(4))
                if h == 0:
                    soft_exp(0)

            def x2_hi(s):
                act.wait_ge(x2t_full, s + 1)
                act.activation(x2T_hi[:, :, s, :],
                               ps_b[:, (s % 2) * HID:(s % 2 + 1) * HID].rearrange("p (c b) -> p c b", c=NC_),
                               ACT.Copy).then_inc(x2t_hi, 1)

            for k in range(len(PAIRS)):
                zt_copy(k)
                if k == 1:
                    soft_exp(1)
                    soft_exp(2)
                s, tp = PAIRS[k]
                if tp == 0 and s >= 2:
                    x2_hi(s - 2)
                if k == 1:
                    act.wait_ge(tb, TB_ANGLES)
                    act.activation(sin_t[:], sin_t[:], ACT.Sin).then_inc(sin_ok, 1)
                    act.activation(cos_t[:], cos_t[:], ACT.Sin).then_inc(sin_ok, 1)
            x2_hi(N - 2)
            x2_hi(N - 1)

            def copy_hi(idx, bank, dst, width=HID):
                act.wait_ge(t_full, idx + 1)
                src = ps_t[bank][:, 0:width]
                if len(dst.shape) == 3:
                    src = src.rearrange("p (c m) -> p c m", c=dst.shape[1])
                act.activation(dst, src, ACT.Copy).then_inc(t_hi, 1)

            def copy_kv(J):
                act.wait_ge(akv_full, J + 1)
                act.activation(kvown[:, :, :].rearrange("p a d -> p (a d)"), ps_o[:, 0:2 * P], ACT.Copy
                               ).then_inc(kv_copied, 1)

            def square_k(J, par):
                act.wait_ge(kv_copied, J + 1)
                act.activation(rope_b[:, HG, :], kvown[:, 0, :], ACT.Square, accum_out=ss[:, par, HG:HG + 1]
                               ).then_inc(sq_done, 1)

            def own_k_hi(J, par):
                act.wait_ge(kt_full, J + 1)
                act.activation(kT_hi[:, par, CACHED:KEYS], ps_k, ACT.Copy).then_inc(kt_hi, 1)

            def squares_q(J, par, heads=range(HG)):
                for h in heads:
                    if h == 0:
                        act.wait_ge(ro_ab, (J + 1) * 3)
                    act.wait_ge(sqq_done, J * HG + h + 1)
                    act.activation(squares[:], ps_q[:, h * P:(h + 1) * P], ACT.Square, accum_out=ss[:, par, h:h + 1]
                                   ).then_inc(sqq_done, 1)

            act.sem_inc(sqq_done, 1)
            for t in range(TILES_W):
                copy_hi(t, t % 2, w_dst(wa_hi, wo_hi, 0, t))
            copy_kv(0)
            square_k(0, 0)
            squares_q(0, 0)
            copy_hi(TILES_W, TILES_W % 2, kT_hi[:, 0, 0:CACHED])
            copy_hi(TILES_W + 1, (TILES_W + 1) % 2, qT_hi[:, :])
            own_k_hi(0, 0)

            def output_hi(count):
                act.wait_ge(pv_full, count + 1)
                act.activation(oT_hi[:, :, :].rearrange("p h m -> p (h m)"), ps_o[:, :], ACT.Copy).then_inc(o_hi, 1)

            def step(g, n, first, last):
                first = first and n == 0
                J = g * N + n
                base = g * PER_G + PRO
                names = groups_of(n, last)
                nxt = not (last and n == N - 1)
                kpar1 = 1 - n % 2

                def group(name):
                    i, bank = t_index(n, name, last)
                    dst, width = hi_lo_target(name, g, kpar1, 0)
                    copy_hi(base + i, bank, dst, width)

                def exponentials(h):
                    act.wait_ge(s_read, J * 4 + h + 1 + 2)
                    act.activation(sm[:, h, :], sm[:, h, :], ACT.Exp, bias=mn[:, h:h + 1], scale=-1.0,
                                   accum_out=den[:, h:h + 1]).then_inc(e_done, 1)

                def own_v_hi():
                    act.wait_ge(kv_copied, J + 1)
                    act.wait_ge(pv_full, J + 1)
                    act.activation(v_hi[:, KC, :], kvown[:, 1, :], ACT.Copy).then_inc(vs_hi, 1)

                def normalise(h):
                    act.wait_ge(r_done, J * 4 + h + 1)
                    act.activation(sm[:, h, :], sm[:, h, :], ACT.Copy, scale=rd[:, h:h + 1]).then_inc(p_act, 1)

                w = [m for m in names if m[0] == "W"]
                exponentials(0)
                if w:
                    group(w[0])
                exponentials(1)
                if len(w) > 1:
                    group(w[1])
                if not first:
                    output_hi(J)
                own_v_hi()
                if nxt:
                    group("K")
                group("D0")
                exponentials(2)
                group("D1")
                normalise(2)
                if nxt:
                    squares_q(J + 1, kpar1, [0, 1])
                    copy_kv(J + 1)
                exponentials(3)
                if nxt:
                    square_k(J + 1, kpar1)
                group("D2")
                normalise(3)
                if nxt:
                    group("q")
                    squares_q(J + 1, kpar1, [2, 3])
                group("D3")
                if nxt:
                    own_k_hi(J + 1, kpar1)
                group("DS")

            for n in range(N):
                step(0, n, True, False)
            with act.Fori(1, G - 1) as g:
                for n in range(N):
                    step(g, n, False, False)
            for n in range(N):
                step(G - 1, n, False, True)
            output_hi(G * N)

            for i in range(7):
                act.wait_ge(lt_full, i + 1)
                b = ps_t[i % 2]
                if i < 4:
                    dst, src = wbT[:, :, i * P:(i + 1) * P], b[:, :].rearrange("p (c m) -> p c m", c=NC_)
                elif i == 4:
                    dst, src = gaT[:, :, 0:P], b[:, :].rearrange("p (c m) -> p c m", c=NC_)
                elif i == 5:
                    dst = gaT[:, :, P:P + E]
                    src = b[:, :].rearrange("p (c m) -> p c m", c=NC_)[:, :, 0:E]
                else:
                    dst = ebT[:, :].rearrange("p (o j) -> p j o", j=NC_)
                    src = b[:, :].rearrange("p (j o) -> p j o", j=NC_)
                act.activation(dst, src, ACT.Copy).then_inc(lt_done, 1)

            def y_copy(n):
                act.wait_ge(yt_full, n + 1)
                if n >= 2:
                    act.wait_ge(g_full, NC_ * (n - 1))
                    act.wait_ge(ht_full, n - 1)
                act.activation(yT[:, n % 2, :, :].rearrange("p c m -> p (c m)"), ps_t[n % 2][:, :], ACT.Copy
                               ).then_inc(yt_done, 1)

            def gate_exp(n):
                act.wait_ge(gm, n + 1)
                act.activation(routes[:, n % 2, 0, :], ps_b[:, (n % 2) * HID + P:(n % 2) * HID + P + E], ACT.Exp,
                               bias=route1[:, n % 2, 0:1], accum_out=route1[:, n % 2, 1:2]).then_inc(ge, 1)

            def hw_copy(n):
                act.wait_ge(ht_full, n + 1)
                act.activation(hwT[:, n % 2, :], ps_q[:, 0:P], ACT.Copy).then_inc(ht_done, 1)

            y_copy(0)
            for n in range(N):
                if n + 1 < N:
                    y_copy(n + 1)
                gate_exp(n)
                if n >= 1:
                    hw_copy(n - 1)
            hw_copy(N - 1)

        @block.vector
        def _(dve):
            for n in range(1, N, 2):
                dve.wait_ge(xt_full, n + 1)
                dve.tensor_copy(xT[:, :, n, :], ps_t[1][:, :].rearrange("p (c b) -> p c b", c=NC_)
                                ).then_inc(xt_dve, 1)
            dve.wait_ge(bt_full, 1)
            dve.tensor_copy(bselT[:, :, :].rearrange("p c m -> p (c m)"), ps_q[:, :]).then_inc(bt_done, 1)
            dve.memset(score[:], NEG).then_inc(smx0, 1)
            dve.wait_ge(bmask_ok, 3)
            for h in range(2):
                dve.wait_ge(zT_full, h + 1)
                dve.tensor_tensor(zlT[:, 4 * h:4 * h + 4, :],
                                  ps_a[:, h * HID:(h + 1) * HID].rearrange("p (n b) -> p n b", n=4),
                                  blockmask[:, 4 * h:4 * h + 4].unsqueeze(2).broadcast_to([P, 4, P]), ALU.mult
                                  ).then_inc(zT_done, 1)
            dve.wait_ge(zl_full, 1)
            dve.tensor_copy(zl[:, :, :].rearrange("p n r -> p (n r)"), ps_o[:, 0:P]).then_inc(zl_done, 1)
            dve.wait_ge(zl_done, 1)
            dve.wait_ge(smx0, 1)
            dve.sem_inc(y_done, 2)
            dve.sem_inc(fv_odd, 1)

            def scores_s(g, s, end=False):
                w = R * (s + 1)
                dve.wait_ge(y_full, g * 8 + s + 1)
                dve.wait_ge(y_red, g * 8 + s + 1)
                src = y_bank(s, end)[:, 0:HG * w].rearrange("p (h m) -> p h m", h=HG)
                zz = zl[:, 0:s + 1, :].rearrange("p n r -> p (n r)").unsqueeze(1).broadcast_to([P, HG, w])
                dve.tensor_tensor(prod[:, s % 2, :, 0:w], src, zz, ALU.mult).then_inc(y_done, 1)

            def sums_s(g, s):
                dve.wait_ge(y_done, g * 8 + s + 1 + 2)
                dve.tensor_reduce(score[:, s, bass.ds(g * HG, HG), 0:s + 1],
                                  prod[:, s % 2, :, 0:R * (s + 1)].rearrange("p h (t r) -> p h t r", r=R),
                                  AX.X, ALU.add).then_inc(y_red, 1)

            def fold_v_copy(g, h, tps):
                if tps[0] == 0:
                    dve.wait_ge(fv_full, g * 4 + h + 1)
                for tp in tps:
                    ins = dve.tensor_copy(
                        fold_v[2 * R * h:2 * R * h + 2 * R, tp, bass.ds(g, 1), :].rearrange("p a m -> p (a m)"),
                        ps_b[2 * R * tp:2 * R * tp + 2 * R, (h % 2) * HID:(h % 2 + 1) * HID])
                if tps[-1] == 3:
                    ins.then_inc(fv_odd, 1)

            def mix_copy(g):
                dve.wait_ge(mix_full, g + 1)
                dve.tensor_copy(mix[:, :, :].rearrange("p h m -> p (h m)"), ps_q[:, :]).then_inc(mix_done, 1)

            def part_a(g):
                o = g - 1
                scores_s(o, 0)
                scores_s(o, 1)
                sums_s(o, 0)
                fold_v_copy(o, 1, range(2))
                scores_s(o, 2)
                sums_s(o, 1)
                fold_v_copy(o, 1, range(2, 4))
                scores_s(o, 3)
                sums_s(o, 2)
                scores_s(o, 4)
                sums_s(o, 3)
                fold_v_copy(o, 3, range(2))
                scores_s(o, 5)
                sums_s(o, 4)
                fold_v_copy(o, 3, range(2, 4))
                scores_s(o, 6)
                sums_s(o, 5)
                scores_s(o, 7)
                sums_s(o, 6)
                sums_s(o, 7)
                mix_copy(g)

            dve.sem_inc(y_red, 2)
            mix_copy(0)
            with dve.Fori(1, G) as g:
                part_a(g)

            def soft_views(i):
                s0, count = SOFT[i]
                sc = score[:, s0:s0 + count, :, :].rearrange("p s h t -> p (s h) t")
                return sc, count * NH, rmax[:, s0 * NH:(s0 + count) * NH], rden[:, s0 * NH:(s0 + count) * NH]

            def soft_max(i):
                s0, count = SOFT[i]
                sc, rows, rm, _ = soft_views(i)
                dve.wait_ge(y_red, 8 * (G - 1) + s0 + count + 2)
                dve.tensor_reduce(rm, sc, AX.X, ALU.max).then_inc(smx, 1)
                dve.wait_ge(smx, 4 * i + 1)
                dve.tensor_tensor(sc, sc, rm.unsqueeze(2).broadcast_to([P, rows, N]), ALU.subtract).then_inc(smx, 1)

            def soft_sum(i):
                sc, rows, _, rr = soft_views(i)
                dve.wait_ge(exp2, i + 1)
                dve.tensor_reduce(rr, sc, AX.X, ALU.add).then_inc(smx, 1)
                dve.wait_ge(smx, 4 * i + 3)
                dve.reciprocal(rr, rr).then_inc(smx, 1)
                dve.wait_ge(smx, 4 * i + 4)
                dve.tensor_tensor(sc, sc, rr.unsqueeze(2).broadcast_to([P, rows, N]), ALU.mult).then_inc(prob, 1)

            def last_scores(s0):
                scores_s(G - 1, s0, True)
                scores_s(G - 1, s0 + 1, True)
                sums_s(G - 1, s0)
                sums_s(G - 1, s0 + 1)

            last_scores(0)
            soft_max(0)
            last_scores(2)
            soft_sum(0)

            def z_pair(k):
                s, tp = PAIRS[k]
                dve.wait_ge(prob, [i for i, (s0, _) in enumerate(SOFT) if s0 <= s][-1] + 1)
                if k >= 2:
                    dve.wait_ge(zt_full, 2 * (k - 1))
                pr = score[:, s, :, 2 * tp:2 * tp + 2].unsqueeze(3).broadcast_to([P, NH, 2, R])
                zz = zl[:, 2 * tp:2 * tp + 2, :].unsqueeze(1).broadcast_to([P, NH, 2, R])
                dve.tensor_tensor(z_ring[:, k % 2, :, :].rearrange("p h (t r) -> p h t r", r=R), pr, zz, ALU.mult
                                  ).then_inc(z_done, 1)

            def x2_sum(s):
                dve.wait_ge(out2_full, s + 1)
                dve.wait_ge(xres_in[s % 2], 16 * (s // 2 + 1))
                if s >= 2:
                    dve.wait_ge(x2_out[s % 2], 16 * (s // 2))
                    dve.wait_ge(x2t_full, s - 1)
                dve.tensor_tensor(x2sb[:, s % 2, :], ps_o[:, :] if s % 2 == 0 else ps_q[:, :],
                                  xres[:, s % 2, :], ALU.add).then_inc(out2_done, 1)

            def x2_low(s):
                dve.wait_ge(x2t_hi, s + 1)
                dve.tensor_tensor(x2T_lo[:, :, s, :],
                                  ps_b[:, (s % 2) * HID:(s % 2 + 1) * HID].rearrange("p (c b) -> p c b", c=NC_),
                                  x2T_hi[:, :, s, :].bitcast(F32), ALU.subtract).then_inc(x2t_lo, 1)

            def angles():
                dve.wait_ge(small_in, 64)
                dve.wait_ge(iota_ok, 5)
                dve.wait_ge(y_full, 8 * G)
                c1 = 6.28125
                c2 = float(2 * np.pi - c1)
                magic = 1.5 * 2.0 ** 23
                dve.tensor_copy(len_f[:], len_i[:]).then_inc(tb, 1)
                dve.wait_ge(tb, 1)
                dve.tensor_scalar(pos[:], len_f[:], tok[:, 0:1], None, ALU.add).then_inc(tb, 1)
                dve.wait_ge(tb, 2)
                dve.tensor_tensor(theta[:], pos[:].unsqueeze(2).broadcast_to([P, N, 64]),
                                  freqs[:].unsqueeze(1).broadcast_to([P, N, 64]), ALU.mult).then_inc(tb, 1)
                dve.wait_ge(tb, 3)
                i = 3
                for dst, quarter in ((sin_t, 0.0), (cos_t, 0.25)):
                    dve.tensor_scalar(turns[:], theta[:], float(1 / (2 * np.pi)), quarter, ALU.mult, ALU.add
                                      ).then_inc(tb, 1)
                    dve.wait_ge(tb, i + 1)
                    dve.tensor_scalar(turns2[:], turns[:], magic, None, ALU.add).then_inc(tb, 1)
                    dve.wait_ge(tb, i + 2)
                    dve.tensor_scalar(turns[:], turns2[:], -magic, None, ALU.add).then_inc(tb, 1)
                    dve.wait_ge(tb, i + 3)
                    dve.scalar_tensor_tensor(out=turns2[:], in0=turns[:], scalar=-c1, in1=theta[:],
                                             op0=ALU.mult, op1=ALU.add).then_inc(tb, 1)
                    dve.wait_ge(tb, i + 4)
                    dve.scalar_tensor_tensor(out=dst[:], in0=turns[:], scalar=-c2, in1=turns2[:],
                                             op0=ALU.mult, op1=ALU.add).then_inc(tb, 1)
                    dve.wait_ge(tb, i + 5)
                    i += 5
                dve.tensor_scalar(cos_t[:], cos_t[:], float(np.pi / 2), None, ALU.add).then_inc(tb, 1)
                dve.wait_ge(tb, i + 1)
                for dst in (sin_t, cos_t):
                    dve.tensor_scalar(dst[:], dst[:], 3.1415925, -3.1415925, ALU.min, ALU.max).then_inc(tb, 1)
                assert i + 3 == TB_ANGLES

            def tables():
                dve.wait_ge(sin_ok, 2)
                for which, w in ((0, qn_b), (2, kn_b)):
                    for half in range(2):
                        wh = w[:, 64 * half:64 * half + 64].unsqueeze(1).broadcast_to([P, N, 64])
                        dve.tensor_tensor(tabs[:, :, which, 64 * half:64 * half + 64], cos_t[:], wh, ALU.mult
                                          ).then_inc(tb, 1)
                    dve.scalar_tensor_tensor(out=tabs[:, :, which + 1, 0:64], in0=sin_t[:], scalar=-1.0,
                                             in1=w[:, 64:128].unsqueeze(1).broadcast_to([P, N, 64]),
                                             op0=ALU.mult, op1=ALU.mult).then_inc(tb, 1)
                    dve.tensor_tensor(tabs[:, :, which + 1, 64:128], sin_t[:],
                                      w[:, 0:64].unsqueeze(1).broadcast_to([P, N, 64]), ALU.mult).then_inc(tb, 1)
                for n in range(N):
                    dve.tensor_scalar(maskall[:, n, :], keyidx[:], len_f[:, n:n + 1], MASKED, ALU.is_ge, ALU.mult
                                      ).then_inc(tb, 1)
                assert TB_ANGLES + 8 + N == TB_ALL

            z_pair(0)
            z_pair(1)
            last_scores(4)
            last_scores(6)
            soft_max(1)
            soft_sum(1)
            z_pair(2)
            soft_max(2)
            z_pair(3)
            soft_sum(2)
            for k in range(len(PAIRS)):
                if 4 <= k + 2 < len(PAIRS):
                    z_pair(k + 2)
                if k == 0:
                    angles()
                if k == 1:
                    tables()
                s, tp = PAIRS[k]
                if tp == 0 and s >= 2:
                    x2_low(s - 2)
                if tp == s // 2:
                    x2_sum(s)
            x2_low(N - 2)
            x2_low(N - 1)

            for i in range(2):
                dve.wait_ge(x2_out[i], 16 * (N // 2))
            dve.wait_ge(x2t_full, N)
            dve.memset(y[:], 0.0).then_inc(init3, 1)
            dve.wait_ge(init3, 1)
            dve.wait_ge(zt_done, 2 * len(PAIRS))
            dve.sem_inc(t_lo, 2)
            dve.sem_inc(s_read, 2)
            dve.sem_inc(f_done, 1)

            def copy_lo(idx, bank, hi, lo, width=HID):
                dve.wait_ge(t_hi, idx + 1)
                src = ps_t[bank][:, 0:width]
                if len(hi.shape) == 3:
                    src = src.rearrange("p (c m) -> p c m", c=hi.shape[1])
                dve.tensor_tensor(lo, src, hi.bitcast(F32), ALU.subtract).then_inc(t_lo, 1)

            def rope_q_parts(J, par):
                q = ps_q[:, :].rearrange("p (h d) -> p h d", h=HG)
                dve.wait_ge(aq_full, J + 1)
                dve.wait_ge(tab_in[par], tab_count(J, par))
                ta = tab[:, par, 0, :].unsqueeze(1).broadcast_to([P, HG, P])
                dve.tensor_tensor(rope_a[:, 0:HG, :], q, ta, ALU.mult).then_inc(ro_ab, 1)
                for half in range(2):
                    a, b = 64 * half, 64 * (1 - half)
                    ins = dve.tensor_tensor(rope_b[:, 0:HG, a:a + 64], q[:, :, b:b + 64],
                                            tab[:, par, 1, a:a + 64].unsqueeze(1).broadcast_to([P, HG, 64]), ALU.mult)
                    ins.then_inc(ro_ab, 1)

            def rope_q(J):
                dve.wait_ge(ro_ab, (J + 1) * 3)
                dve.tensor_tensor(rope_a[:, 0:HG, :], rope_a[:, 0:HG, :], rope_b[:, 0:HG, :], ALU.add
                                  ).then_inc(rq_done, 1)

            def own_k_lo(J, par):
                dve.wait_ge(kt_hi, J + 1)
                dve.tensor_tensor(kT_lo[:, par, CACHED:KEYS], ps_k, kT_hi[:, par, CACHED:KEYS].bitcast(F32),
                                  ALU.subtract).then_inc(kt_lo, 1)

            def rope_k(J, par):
                k = kvown[:, 0, :]
                dve.wait_ge(rms_k, J + 1)
                r = rs[:, par, HG:HG + 1]
                dve.scalar_tensor_tensor(out=rope_a[:, HG, :], in0=k, scalar=r, in1=tab[:, par, 2, :],
                                         op0=ALU.mult, op1=ALU.mult).then_inc(rk_ab, 1)
                for half in range(2):
                    a, b = 64 * half, 64 * (1 - half)
                    dve.scalar_tensor_tensor(out=rope_b[:, HG, a:a + 64], in0=k[:, b:b + 64], scalar=r,
                                             in1=tab[:, par, 3, a:a + 64], op0=ALU.mult, op1=ALU.mult
                                             ).then_inc(rk_ab, 1)
                dve.wait_ge(rk_ab, (J + 1) * 3)
                dve.tensor_tensor(rope_a[:, HG, :], rope_a[:, HG, :], rope_b[:, HG, :], ALU.add).then_inc(rk_done, 1)

            tab_g = [0, 0]

            def tab_count(J, par):
                g, n = tab_g
                return (g * 4 + n // 2 + 1) * 32

            for t in range(TILES_W):
                copy_lo(t, t % 2, w_dst(wa_hi, wo_hi, 0, t), w_dst(wa_lo, wo_lo, 0, t))
            rope_q_parts(0, 0)
            rope_q(0)
            rope_k(0, 0)
            copy_lo(TILES_W, TILES_W % 2, kT_hi[:, 0, 0:CACHED], kT_lo[:, 0, 0:CACHED])
            copy_lo(TILES_W + 1, (TILES_W + 1) % 2, qT_hi[:, :], qT_lo[:, :])
            own_k_lo(0, 0)

            def output_lo(count):
                dve.wait_ge(o_hi, count)
                dve.tensor_tensor(oT_lo[:, :, :].rearrange("p h m -> p (h m)"), ps_o[:, :],
                                  oT_hi[:, :, :].rearrange("p h m -> p (h m)").bitcast(F32), ALU.subtract
                                  ).then_inc(o_lo, 1)

            def add_output(count, m):
                dve.wait_ge(f_full, count)
                dve.tensor_tensor(y[:, m, :], ps_o[:, :], y[:, m, :], ALU.add).then_inc(f_done, 1)

            def step(g, n, first, last):
                J = g * N + n
                base = g * PER_G + PRO
                par = n % 2
                names = groups_of(n, last)
                nxt = not (last and n == N - 1)
                w = [m for m in names if m[0] == "W"]

                def group(name):
                    i, bank = t_index(n, name, last)
                    hi, width = hi_lo_target(name, g, 1 - par, 0)
                    lo, _ = hi_lo_target(name, g, 1 - par, 1)
                    copy_lo(base + i, bank, hi, lo, width)

                def least(h):
                    wait_alone(dve, s_full, J * 4 + h + 1)
                    if h == 0:
                        wait_alone(dve, st_done, J + 1)
                        wait_alone(dve, tab_in[par], (g * 4 + n // 2 + 1) * 32)
                    dve.tensor_tensor_reduce(out=sm[:, h, :], in0=ps_s[h % 2][:, 0:KEYS], in1=mask[:, par, :],
                                             scale=qs[:, par, h:h + 1], scalar=3.0e38, op0=ALU.add, op1=ALU.min,
                                             accum_out=mn[:, h:h + 1]).then_inc(s_read, 1)

                def reciprocal(h):
                    dve.wait_ge(e_done, J * 4 + h + 1)
                    dve.reciprocal(rd[:, h:h + 1], den[:, h:h + 1]).then_inc(r_done, 1)

                def normalise(h):
                    reciprocal(h)
                    dve.wait_ge(r_done, J * 4 + h + 1)
                    dve.tensor_scalar(sm[:, h, :], sm[:, h, :], rd[:, h:h + 1], None, ALU.mult).then_inc(p_dve, 1)

                if not (first and n < 2):
                    add_output(J - 1, (n - 2) % N)
                least(0)
                least(1)
                if w:
                    group(w[0])
                normalise(0)
                normalise(1)
                if len(w) > 1:
                    group(w[1])
                if not (first and n < 1):
                    output_lo(J)
                dve.wait_ge(vs_hi, J + 1)
                dve.tensor_tensor(v_lo[:, KC, :], kvown[:, 1, :], v_hi[:, KC, :].bitcast(F32), ALU.subtract
                                  ).then_inc(vs_lo, 1)
                if nxt:
                    group("K")
                group("D0")
                least(2)
                tab_g[:] = [g + (n == N - 1), (n + 1) % N]
                if nxt:
                    rope_q_parts(J + 1, 1 - par)
                reciprocal(2)
                least(3)
                group("D1")
                if nxt:
                    rope_q(J + 1)
                reciprocal(3)
                group("D2")
                if nxt:
                    rope_k(J + 1, 1 - par)
                    group("q")
                group("D3")
                if nxt:
                    own_k_lo(J + 1, 1 - par)
                group("DS")

            for n in range(N):
                step(0, n, True, False)
            with dve.Fori(1, G - 1) as g:
                for n in range(N):
                    step(g, n, False, False)
            for n in range(N):
                step(G - 1, n, False, True)
            add_output(G * N - 1, N - 2)
            output_lo(G * N)
            add_output(G * N, N - 1)

            dve.wait_ge(bias_ok, 2)
            RT = 11

            def route(n):
                i = n % 2
                g_ps = ps_b[:, i * HID:i * HID + P + E]
                e, p, sel, keep, wgt = (routes[:, i, m, :] for m in range(5))
                neg_max, total, inv, s2 = (route1[:, i, m:m + 1] for m in range(4))
                gt, eq = pairs[:, i, 0, :, :], pairs[:, i, 1, :, :]
                c = [n * RT]

                def after_last():
                    dve.wait_ge(rt, c[0])

                def chained(ins):
                    c[0] += 1
                    ins.then_inc(rt, 1)

                dve.wait_ge(g_full, NC_ * (n + 1))
                dve.tensor_reduce(neg_max, g_ps[:, P:P + E], AX.X, ALU.max, negate=True).then_inc(gm, 1)
                dve.wait_ge(ge, n + 1)
                chained(dve.reciprocal(inv, total))
                after_last()
                chained(dve.tensor_scalar(p, e, inv, None, ALU.mult))
                after_last()
                later = p.unsqueeze(1).broadcast_to([P, E, E])
                mine = p.unsqueeze(2).broadcast_to([P, E, E])
                chained(dve.tensor_tensor(gt, later, mine, ALU.is_gt))
                chained(dve.tensor_tensor(eq, later, mine, ALU.is_equal))
                after_last()
                chained(dve.tensor_tensor(eq, eq, before[:], ALU.mult))
                after_last()
                chained(dve.tensor_tensor(gt, gt, eq, ALU.add))
                after_last()
                chained(dve.tensor_reduce(sel, gt, AX.X, ALU.add))
                after_last()
                chained(dve.tensor_scalar(keep, sel, 1.5, None, ALU.is_lt))
                after_last()
                chained(dve.tensor_tensor(wgt, keep, p, ALU.mult))
                after_last()
                chained(dve.tensor_reduce(s2, wgt, AX.X, ALU.add))
                after_last()
                chained(dve.reciprocal(inv, s2))
                after_last()
                assert c[0] == (n + 1) * RT
                if n >= 2:
                    dve.wait_ge(ht_full, n - 1)
                dve.scalar_tensor_tensor(out=hw[:, i, :, :], in0=g_ps[:, 0:P].rearrange("p (e r) -> p e r", r=R),
                                         scalar=inv, in1=wgt.unsqueeze(2).broadcast_to([P, E, R]),
                                         op0=ALU.mult, op1=ALU.mult).then_inc(hw_done, 1)

            def finish(n):
                dve.wait_ge(d_full, n + 1)
                dve.wait_ge(x2b, n + 1)
                if n >= 2:
                    dve.wait_ge(fin_out[n % 2], 16 * (n // 2))
                dve.tensor_tensor(fin[:, n % 2, :], ps_a[:, (n % 2) * HID:(n % 2 + 1) * HID], x2r[:, n % 2, :],
                                  ALU.add).then_inc(fin_done, 1)

            for n in range(N):
                route(n)
                if n >= 1:
                    finish(n - 1)
            finish(N - 1)


_INS = ['x', 'itok_B_3_7', 'itok_Bx16_0_63', 'itok_B_207_1644', 'L0_cond_A', 'L0_cond_B', 'L0_attn_weight_qkv',
        'L0_attn_weight_proj', 'L0_cond2_Wq', 'L0_cond2_Wk', 'L0_cond2_Wv', 'L0_cond2_Wo', 'L0_cond2_q_norm_w',
        'L0_cond2_k_norm_w', 'L0_cond2_k_cache', 'L0_cond2_v_cache', 'L0_ffn_W_base', 'L0_ffn_b_base',
        'L0_ffn_W_gate', 'L0_ffn_A', 'L0_ffn_B']
_OUTS = [((8, 128, 512), 'float32')]


def kernel(**inputs):
    import numpy as _np
    import concourse.bacc as _bacc
    from concourse import mybir as _mybir
    from concourse.bass_utils import run_bass_kernel_spmd as _run

    nc = _bacc.Bacc("TRN2", target_bir_lowering=False, num_devices=1)
    arrays, args = {}, []
    for name in _INS:
        a = _np.ascontiguousarray(inputs[name])
        arrays[f"in_{name}_dram"] = a
        args.append(nc.dram_tensor(f"in_{name}_dram", a.shape, _mybir.dt.from_np(a.dtype), kind="ExternalInput").ap())
    for i, (shape, dtype) in enumerate(_OUTS):
        dt = _mybir.dt.from_np(_np.dtype(dtype))
        args.append(nc.dram_tensor(f"out_{i}_dram", shape, dt, kind="ExternalOutput").ap())
    block_program(nc, *args)
    r = _run(nc, [arrays], core_ids=[0])
    got = tuple(r.results[0][f"out_{i}_dram"] for i in range(len(_OUTS)))
    return got[0]
```

```python
from contextlib import ExitStack

import numpy as np

import concourse.bass as bass
from concourse import mybir

F32 = mybir.dt.float32
F32R = mybir.dt.float32r
BF16 = mybir.dt.bfloat16
I32 = mybir.dt.int32
U32 = mybir.dt.uint32
ALU = mybir.AluOpType
ACT = mybir.ActivationFunctionType
AX = mybir.AxisListType

P = 128
N = 8
HID = 512
NC_ = HID // P
R = 16
G = 8
HG = 4
NH = G * HG
PAGE = 32
CACHED = 512
KC = CACHED // P
KEYS = CACHED + P
E = 8
SCALE = float(1.0 / np.sqrt(128.0))
EPS_RMS = 1e-6
NEG = -3.0e38
MASKED = -1.0e30
QW = HG * P
PW = QW + 2 * P
TILES_W = 10


def inverse_frequencies():
    return (np.float32(1.0) / np.power(np.float32(10000.0), np.arange(0, P, 2, dtype=np.float32) / np.float32(P))
            ).astype(np.float32)


def block_program(nc, x, ids_adapter, table_pages, cache_len, lora_a, lora_b, w_qkv, w_proj, wq, wk, wv, wo,
                  q_norm, k_norm, k_cache, v_cache, w_base, b_base, w_gate, ex_a, ex_b, out):
    KB = 1024
    base0 = (nc.sbuf_base + 63) // 64 * 64
    ctx = ExitStack()
    with ctx:
        def at(name, shape, dt, kb):
            return nc.alloc_sbuf_tensor_at(name, shape, dt, offset=base0 + int(kb * KB))

        def sem(name):
            return ctx.enter_context(nc.semaphore(name))

        wraw = at("wraw", [P, 2, 6, HID], F32, 0)
        wpraw = at("wpraw", [P, 2, 4, HID], F32, 24)
        fold_v = at("fold_v", [P, 4, G, HID], F32, 40)
        xin = at("xin", [P, N, HID], F32, 40)
        xT = at("xT", [P, NC_, N, P], F32, 56)
        bsel = at("bsel", [P, HID], F32, 72)
        bselT = at("bselT", [P, NC_, P], F32, 74)
        tabs = at("tabs", [P, N, 4, P], F32, 184)
        maskall = at("maskall", [P, N, CACHED], BF16, 174)
        score = at("score", [P, N, NH, N], F32, 104)
        theta = at("theta", [P, N, 64], F32, 136)
        turns = at("turns", [P, N, 64], F32, 138)
        turns2 = at("turns2", [P, N, 64], F32, 140)
        sin_t = at("sin_t", [P, N, 64], F32, 142)
        cos_t = at("cos_t", [P, N, 64], F32, 144)
        keyidx = at("keyidx", [P, CACHED], F32, 202.5)
        freqs = at("freqs", [P, 64], F32, 172.5)
        qn_b = at("qn_b", [P, P], F32, 172.75)
        kn_b = at("kn_b", [P, P], F32, 173.25)
        z_ring = at("z_ring", [P, 2, NH, 2 * R], F32, 112)
        zT_ring = at("zT_ring", [P, 2, G, P], F32, 120)
        xres = at("xres", [P, 2, HID], F32, 128)
        x2sb = at("x2sb", [P, 2, HID], F32, 132)
        wT = at("wT", [P, 6, NC_, P], F32, 136)
        folded = at("folded", [P, 6, P], F32, 148)
        mix = at("mix", [P, HG, P], F32, 151)
        wpT = at("wpT", [P, HG, HID], F32, 153)
        prod = at("prod", [P, 2, HG, P], F32, 161)
        zlT = at("zlT", [P, N, P], F32, 165)
        aall = at("aall", [P, N, NC_, R], F32, 169)
        x2T_hi = at("x2T_hi", [P, NC_, N, P], F32R, 0)
        x2T_lo = at("x2T_lo", [P, NC_, N, P], F32R, 16)
        y = at("y", [P, N, HID], F32, 32)
        wo_hi = at("wo_hi", [P, 2, HG, HID], F32R, 48)
        wo_lo = at("wo_lo", [P, 2, HG, HID], F32R, 64)
        pT_hi = at("pT_hi", [P, KC + 1, QW], F32R, 80)
        pT_lo = at("pT_lo", [P, KC + 1, QW], F32R, 90)
        sm = at("sm", [P, HG, KEYS], F32, 100)
        oT_hi = at("oT_hi", [P, HG, P], F32R, 110)
        oT_lo = at("oT_lo", [P, HG, P], F32R, 112)
        qT_hi = at("qT_hi", [P, QW], F32R, 114)
        qT_lo = at("qT_lo", [P, QW], F32R, 116)
        rope_a = at("rope_a", [P, HG + 1, P], F32, 118)
        rope_b = at("rope_b", [P, HG + 1, P], F32, 120.5)
        kT_hi = at("kT_hi", [P, 2, KEYS], F32R, 123)
        kT_lo = at("kT_lo", [P, 2, KEYS], F32R, 128)
        wa_hi = at("wa_hi", [P, 2, NC_, PW], F32R, 136)
        wa_lo = at("wa_lo", [P, 2, NC_, PW], F32R, 160)
        wtile = at("wtile", [P, 2, HID], F32, 184)
        kraw = at("kraw", [P, 2, KC, P], F32, 188)
        vraw = at("vraw", [P, 2, KC, P], F32, 192)
        tab = at("tab", [P, 2, 4, P], F32, 196)
        mask = at("mask", [P, 2, KEYS], BF16, 200)
        v_hi = at("v_hi", [P, KC + 1, P], F32R, 202.5)
        v_lo = at("v_lo", [P, KC + 1, P], F32R, 133)
        squares = at("squares", [P, P], F32, 135.5)
        w0raw_a = at("w0raw_a", [P, 6, HID], F32, 148)
        w0raw_b = at("w0raw_b", [P, HG, HID], F32, 172)
        wbraw = at("wbraw", [P, NC_, HID], F32, 136)
        earaw = at("earaw", [P, HID], F32, 144)
        gateraw = at("gateraw", [E, HID], F32, 146)
        ebraw = at("ebraw", [P, E, NC_, R], F32, 160)
        ebj = at("ebj", [P, NC_, E, R], F32, 162)
        wbT_hi = at("wbT_hi", [P, NC_, HID], F32R, 164)
        wbT_lo = at("wbT_lo", [P, NC_, HID], F32R, 64)
        gaT_hi = at("gaT_hi", [P, NC_, P + E], F32R, 48)
        gaT_lo = at("gaT_lo", [P, NC_, P + E], F32R, 50.5)
        bias_b = at("bias_b", [P, HID], F32, 184)
        ebT = at("ebT", [P, HID], F32, 186)
        yT_hi = at("yT_hi", [P, 2, NC_, P], F32R, 148)
        yT_lo = at("yT_lo", [P, 2, NC_, P], F32R, 152)
        x2r = at("x2r", [P, 2, HID], F32, 156)
        fin = at("fin", [P, 2, HID], F32, 172)
        hw = at("hw", [P, 2, E, R], F32, 176)
        hwT = at("hwT", [P, 2, P], F32, 177)
        routes = at("routes", [P, 2, 8, E], F32, 179)
        pairs = at("pairs", [P, 2, 4, E, E], F32, 179.5)
        route1 = at("route1", [P, 2, 4], F32, 181.5)
        before = at("before", [P, E, E], F32, 182)
        ident = at("ident", [P, P], F32, 205)
        zl = at("zl", [P, N, R], F32, 205.5)
        SM = 206.0
        blockmask = at("blockmask", [P, N], F32, SM)
        pos = at("pos", [P, N], F32, SM + 0.03125)
        len_i = at("len_i", [P, N], I32, SM + 0.0625)
        len_f = at("len_f", [P, N], F32, SM + 0.09375)
        tok = at("tok", [P, 1], F32, SM + 0.125)
        id_sb = at("id_sb", [1, N], I32, SM + 0.15625)
        ss = at("ss", [P, 2, HG + 1], F32, SM + 0.1875)
        ms = at("ms", [P, 2, HG + 1], F32, SM + 0.25)
        rs = at("rs", [P, 2, HG + 1], F32, SM + 0.3125)
        qs = at("qs", [P, 2, HG], F32, SM + 0.375)
        mn = at("mn", [P, HG], F32, SM + 0.40625)
        den = at("den", [P, HG], F32, SM + 0.4375)
        rd = at("rd", [P, HG], F32, SM + 0.46875)
        halfs = at("halfs", [P, HG + 1], F32, SM + 0.5)
        idx_a = at("idx_a", [P, N * KC], I32, SM + 0.53125)
        idx_b = at("idx_b", [P, N * KC], I32, SM + 0.65625)
        slot8 = at("slot8", [P, 1], I32, SM + 0.78125)
        kvown = at("kvown", [P, 2, P], F32, SM + 0.8125)
        rmax = at("rmax", [P, N * NH], F32, 182)
        rden = at("rden", [P, N * NH], F32, 183)
        pages = at("pages", [P, N * 16], I32, 172)

        ps_a = ctx.enter_context(nc.psum_tensor("ps_a", [P, 2 * HID], F32))
        ps_b = ctx.enter_context(nc.psum_tensor("ps_b", [P, 2 * HID], F32))
        ps_t = [ctx.enter_context(nc.psum_tensor(f"ps_t{i}", [P, HID], F32)) for i in range(2)]
        ps_q = ctx.enter_context(nc.psum_tensor("ps_q", [P, HID], F32))
        ps_o = ctx.enter_context(nc.psum_tensor("ps_o", [P, HID], F32))
        ps_s = [ps_a, ps_b]
        HALF = KEYS // 2
        ps_k = ps_b[:, HID + HALF:HID + HALF + P]

        x2_d = nc.dram_tensor("x2_scratch", [N, P, HID], F32, kind="Internal").ap()
        tab_d = nc.dram_tensor("tab_scratch", [N, P, 4 * P], F32, kind="Internal").ap()
        mask_d = nc.dram_tensor("mask_scratch", [N, P, CACHED], BF16, kind="Internal").ap()
        freq_d = nc.inline_tensor(inverse_frequencies().reshape(1, 64), "rotary_freqs").ap()

        k_rows = k_cache.rearrange("a s g d -> (a s g) d")
        v_rows = v_cache.rearrange("a s g d -> (a s g) d")

        x_in = [sem(f"x_in{i}") for i in range(N // 2)]
        id_in = sem("id_in")
        lora_in = sem("lora_in")
        small_in = sem("small_in")
        pages_in = sem("pages_in")
        ident_ok = sem("ident_ok")
        bmask_ok = sem("bmask_ok")
        iota_ok = sem("iota_ok")
        xt_full = sem("xt_full")
        xt_act = sem("xt_act")
        xt_dve = sem("xt_dve")
        bt_full = sem("bt_full")
        bt_done = sem("bt_done")
        zT_full = sem("zT_full")
        zT_done = sem("zT_done")
        zl_full = sem("zl_full")
        zl_done = sem("zl_done")
        tb = sem("tb")
        sin_ok = sem("sin_ok")
        tab_out = sem("tab_out")
        idx_ok = sem("idx_ok")
        wq_in = [sem(f"wq_in{i}") for i in range(2)]
        wp_in = [sem(f"wp_in{i}") for i in range(2)]
        t2_full = sem("t2_full")
        t2_done = sem("t2_done")
        fold_full = sem("fold_full")
        fold_done = sem("fold_done")
        mix_full = sem("mix_full")
        mix_done = sem("mix_done")
        y_full = sem("y_full")
        y_done = sem("y_done")
        y_red = sem("y_red")
        fv_full = sem("fv_full")
        fv_even = sem("fv_even")
        fv_odd = sem("fv_odd")
        smx = sem("smx")
        exp2 = sem("exp2")
        prob = sem("prob")
        z_done = sem("z_done")
        zt_full = sem("zt_full")
        zt_done = sem("zt_done")
        out2_full = sem("out2_full")
        out2_done = sem("out2_done")
        xres_in = [sem(f"xres_in{i}") for i in range(2)]
        x2_out = [sem(f"x2_out{i}") for i in range(2)]
        x2t_full = sem("x2t_full")
        x2t_hi = sem("x2t_hi")
        x2t_lo = sem("x2t_lo")
        wt_in = [sem(f"wt_in{i}") for i in range(2)]
        tab_in = [sem(f"tab_in{i}") for i in range(2)]
        kg_in = [sem(f"kg_in{i}") for i in range(2)]
        vg_in = [sem(f"vg_in{i}") for i in range(2)]
        init3 = sem("init3")
        t_full = sem("t_full")
        t_hi = sem("t_hi")
        t_lo = sem("t_lo")
        s_full = sem("s_full")
        s_read = sem("s_read")
        e_done = sem("e_done")
        r_done = sem("r_done")
        p_dve = sem("p_dve")
        p_act = sem("p_act")
        aq_full = sem("aq_full")
        akv_full = sem("akv_full")
        sq_done = sem("sq_done")
        st_pool = sem("st_pool")
        st_done = sem("st_done")
        kt_full = sem("kt_full")
        kt_hi = sem("kt_hi")
        kt_lo = sem("kt_lo")
        rms_k = sem("rms_k")
        ro_ab = sem("ro_ab")
        rq_done = sem("rq_done")
        kv_copied = sem("kv_copied")
        sqq_done = sem("sqq_done")
        smx0 = sem("smx0")
        rk_ab = sem("rk_ab")
        rk_done = sem("rk_done")
        vs_hi = sem("vs_hi")
        vs_lo = sem("vs_lo")
        vc_hi = sem("vc_hi")
        vc_lo = sem("vc_lo")
        pv_full = sem("pv_full")
        o_hi = sem("o_hi")
        o_lo = sem("o_lo")
        f_full = sem("f_full")
        f_done = sem("f_done")
        ix_ok = sem("ix_ok")
        lw_in = sem("lw_in")
        bias_in = sem("bias_in")
        base_full = sem("base_full")
        yt_hi = sem("yt_hi")
        w0_in = sem("w0_in")
        w0_full = sem("w0_full")
        w0_hi = sem("w0_hi")
        w0_lo = sem("w0_lo")
        x2r_in = [sem(f"x2r_in{i}") for i in range(2)]
        yt_full = sem("yt_full")
        yt_done = sem("yt_done")
        g_full = sem("g_full")
        gm = sem("gm")
        ge = sem("ge")
        rt = sem("rt")
        hw_done = sem("hw_done")
        ht_full = sem("ht_full")
        ht_done = sem("ht_done")
        d_full = sem("d_full")
        fin_done = sem("fin_done")
        fin_out = [sem(f"fin_out{i}") for i in range(2)]
        bias_ok = sem("bias_ok")
        x2b = sem("x2b")
        eb_ok = sem("eb_ok")
        waits_alone = sem("waits_alone")

        W_FIRST = {0: 0, 1: 1, 2: 3, 3: 4, 4: 6, 5: 7, 6: 9}
        W_COUNT = {0: 1, 1: 2, 2: 1, 3: 2, 4: 1, 5: 2, 6: 1, 7: 0}
        PRO = HG + 2

        def groups_of(n, last):
            if last:
                w = [f"L{i}" for i in range(7) if i // 2 + 1 == n]
            else:
                w = [f"W{W_FIRST[n] + i}" for i in range(W_COUNT[n])] if W_COUNT[n] else []
            nxt = not (last and n == N - 1)
            return w + ["K"] * nxt + ["D0", "D1", "D2"] + ["q"] * nxt + ["D3", "DS"]

        PER_G = sum(len(groups_of(n, False)) for n in range(N))
        assert PER_G % 2 == 0

        def t_index(n, name, last):
            i = sum(len(groups_of(m, last)) for m in range(n)) + groups_of(n, last).index(name)
            return i, (PRO + i) % 2

        END = (G - 1) * PER_G + PRO + sum(len(groups_of(n, True)) for n in range(N))

        def yt_bank(n):
            return ps_t[(END + n) % 2]

        LATE_DMAS = 3 + E
        K_W0 = 9
        TB_ALL = 32
        TB_ANGLES = 16
        SOFT = [(0, 2), (2, 2), (4, 4)]
        PAIRS = [(s, tp) for s in range(N) for tp in range(s // 2 + 1)]

        def y_bank(s, end):
            if end:
                return ps_a[:, (s % 2) * HID:(s % 2 + 1) * HID]
            return ps_o if s % 2 == 0 else ps_q

        def w_dst(wa, wo_t, wpar, t):
            one = bass.ds(wpar, 1)
            if t < 6:
                return wa[:, one, :, t * P:(t + 1) * P].rearrange("p a c m -> p (a c) m")
            return wo_t[:, one, :, (t - 6) * P:(t - 5) * P].rearrange("p a h m -> p (a h) m")

        def hi_lo_target(name, g, kpar1, lo):
            if name == "K":
                return (kT_hi, kT_lo)[lo][:, kpar1, 0:CACHED], HID
            if name == "q":
                return (qT_hi, qT_lo)[lo][:, :], HID
            pT = (pT_hi, pT_lo)[lo]
            if name == "DS":
                return pT[:, KC, :], HID
            if name[0] == "D":
                h = int(name[1])
                return pT[:, 0:KC, h * P:(h + 1) * P], HID
            return w_dst((wa_hi, wa_lo)[lo], (wo_hi, wo_lo)[lo], (g + 1) % 2, int(name[1:])), HID

        def late_parts(bank, i, lo):
            b = ps_t[bank][:, :].rearrange("p (c m) -> p c m", c=NC_)
            if i < 4:
                return (wbT_hi, wbT_lo)[lo][:, :, i * P:(i + 1) * P], b
            if i == 4:
                return (gaT_hi, gaT_lo)[lo][:, :, 0:P], b
            return (gaT_hi, gaT_lo)[lo][:, :, P:P + E], b[:, :, 0:E]

        def wait_alone(eng, s, value):
            eng.wait_ge(s, value)
            eng.sem_inc(waits_alone, 1)

        block = ctx.enter_context(nc.Block())

        @block.sync
        def _(sp):
            sp.dma_start(id_sb[:], ids_adapter.rearrange("(o n) -> o n", o=1)).then_inc(id_in, 16)
            for n in range(0, N, 2):
                sp.dma_start(xin[:, n:n + 2, :], x[n:n + 2].rearrange("n b i -> b n i")).then_inc(x_in[n // 2], 16)
            def load_weights(g, par):
                sp.dma_start(wraw[:, par, :, :],
                             w_qkv[bass.ds(g * 6 * P, 6 * P), :].rearrange("(t p) o -> p t o", p=P)
                             ).then_inc(wq_in[par], 16)
                sp.dma_start(wpraw[:, par, :, :],
                             w_proj[:, bass.ds(g * QW, QW)].rearrange("(t p) e -> p t e", p=P)
                             ).then_inc(wp_in[par], 16)

            load_weights(0, 0)
            sp.dma_start(len_i[:], cache_len.rearrange("(o n) -> o n", o=1).broadcast_to([P, N])).then_inc(small_in, 16)
            sp.dma_start(freqs[:], freq_d.broadcast_to([P, 64])).then_inc(small_in, 16)
            sp.dma_start(qn_b[:], q_norm.rearrange("(o d) -> o d", o=1).broadcast_to([P, P])).then_inc(small_in, 16)
            sp.dma_start(kn_b[:], k_norm.rearrange("(o d) -> o d", o=1).broadcast_to([P, P])).then_inc(small_in, 16)
            sp.dma_start(pages[:], table_pages.rearrange("(o n) k -> o (n k)", o=1).broadcast_to([P, N * 16])
                         ).then_inc(pages_in, 16)
            sp.wait_ge(id_in, 16)
            for n in range(N):
                a_id = sp.value_load(id_sb[0:1, n:n + 1], min_val=0, max_val=7)
                sp.dma_start(bsel[R * n:R * n + R, :],
                             lora_b[bass.ds(a_id, 1), :, :].rearrange("a r i -> (a r) i")).then_inc(lora_in, 16)
                sp.dma_start(aall[:, n, :, :].rearrange("p j r -> p (j r)"),
                             lora_a[bass.ds(a_id, 1), :, :].rearrange("a (p j) r -> (a p) (j r)", j=NC_)
                             ).then_inc(lora_in, 16)

            load_weights(1, 1)
            with sp.Fori(0, G // 2 - 1) as gp:
                for par in range(2):
                    wait_alone(sp, t2_full, (gp * 2 + par + 1) * 10)
                    load_weights(gp * 2 + par + 2, par)

            for s in range(2):
                sp.dma_start(xres[:, s, :], x[s]).then_inc(xres_in[s], 16)
            def load_tables(n, par):
                sp.dma_start(tab[:, par, :, :].rearrange("p a d -> p (a d)"), tab_d[n]).then_inc(tab_in[par], 16)
                sp.dma_start(mask[:, par, 0:CACHED], mask_d[n]).then_inc(tab_in[par], 16)

            def load_wtile(g, t, slot):
                if t < HG:
                    src = wq[bass.ds(g * QW + t * P, P), :]
                elif t == HG:
                    src = wk[bass.ds(g * P, P), :]
                elif t == HG + 1:
                    src = wv[bass.ds(g * P, P), :]
                else:
                    src = wo[(t - 6) * P:(t - 5) * P, bass.ds(g * QW, QW)]
                sp.dma_start(wtile[:, slot, :], src).then_inc(wt_in[slot], 16)

            sp.wait_ge(y_full, 8 * G)
            sp.wait_ge(fv_full, HG * G)
            sp.dma_start(w0raw_a[:, 0:HG, :], wq[0:QW, :].rearrange("(t p) i -> p t i", p=P)).then_inc(w0_in, 16)
            sp.dma_start(w0raw_a[:, HG, :], wk[0:P, :]).then_inc(w0_in, 16)
            sp.dma_start(w0raw_a[:, HG + 1, :], wv[0:P, :]).then_inc(w0_in, 16)
            for s in range(N):
                if s == 3:
                    sp.wait_ge(tb, TB_ALL)
                    for n in range(N):
                        sp.dma_start(tab_d[n], tabs[:, n, :, :].rearrange("p a d -> p (a d)")).then_inc(tab_out, 16)
                        sp.dma_start(mask_d[n], maskall[:, n, :]).then_inc(tab_out, 16)
                sp.wait_ge(out2_done, s + 1)
                sp.dma_start(x2_d[s], x2sb[:, s % 2, :]).then_inc(x2_out[s % 2], 16)
                if s + 2 < N:
                    sp.dma_start(xres[:, s % 2, :], x[s + 2]).then_inc(xres_in[s % 2], 16)
                if s == 5:
                    sp.wait_ge(tab_out, 32 * N)
                    load_tables(0, 0)
                    load_tables(1, 1)
                    sp.wait_ge(idx_ok, 5)
                    sp.dma_start(w0raw_b[:], wo[:, 0:QW].rearrange("(t p) e -> p t e", p=P)).then_inc(w0_in, 16)

            def step(g, n, last):
                J = g * N + n
                base = g * PER_G + PRO
                if not last and n == 0:
                    wait_alone(sp, t_full, base)
                    load_wtile(g + 1, 0, 0)
                    load_wtile(g + 1, 1, 1)
                for name in groups_of(n, last):
                    if name[0] == "W" and int(name[1:]) + 2 < TILES_W:
                        t = int(name[1:])
                        wait_alone(sp, t_full, base + t_index(n, name, last)[0] + 1)
                        load_wtile(g + 1, t + 2, t % 2)
                if not (last and n >= N - 2):
                    wait_alone(sp, s_read, J * 4 + 4 + 2)
                    load_tables((n + 2) % N, n % 2)

            with sp.Fori(0, G - 1) as g:
                for n in range(N):
                    step(g, n, False)
            for n in range(N):
                step(G - 1, n, True)
                if n == 0:
                    sp.wait_ge(akv_full, N * (G - 1))
                    sp.dma_start(wbraw[:], w_base.rearrange("(t p) i -> p t i", p=P)).then_inc(lw_in, 16)
                    sp.dma_start(earaw[:], ex_a.rearrange("e r i -> (e r) i")).then_inc(lw_in, 16)
                    sp.dma_start(gateraw[:], w_gate).then_inc(lw_in, 16)
                    for e in range(E):
                        sp.dma_start(ebraw[:, e, :, :].rearrange("p j r -> p (j r)"),
                                     ex_b[e].rearrange("(p j) r -> p (j r)", j=NC_)).then_inc(lw_in, 16)
                    sp.wait_ge(f_full, N * (G - 1))
                    sp.dma_start(bias_b[:], b_base.rearrange("(o i) -> o i", o=1).broadcast_to([P, HID])
                                 ).then_inc(bias_in, 16)

            for i in range(2):
                sp.wait_ge(x2_out[i], 16 * (N // 2))
            sp.wait_ge(akv_full, N * G)
            for n in range(2):
                sp.dma_start(x2r[:, n, :], x2_d[n]).then_inc(x2r_in[n], 16)
            for n in range(N):
                sp.wait_ge(fin_done, n + 1)
                sp.dma_start(out[n], fin[:, n % 2, :]).then_inc(fin_out[n % 2], 16)
                if n + 2 < N:
                    sp.dma_start(x2r[:, n % 2, :], x2_d[n + 2]).then_inc(x2r_in[n % 2], 16)
            for i in range(2):
                sp.wait_ge(fin_out[i], 16 * (N // 2))

        @block.gpsimd
        def _(pool):
            pool.memset(ident[:], 0.0).then_inc(ident_ok, 1)
            pool.wait_ge(ident_ok, 1)
            pool.affine_select(out=ident[:], in_=ident[:], compare_op=ALU.not_equal, fill=1.0, base=0,
                               pattern=[[-1, P]], channel_multiplier=1).then_inc(ident_ok, 1)
            pool.memset(blockmask[:], 1.0).then_inc(bmask_ok, 1)
            pool.iota(tok[:], pattern=[[0, 1]], base=0, channel_multiplier=1,
                      allow_small_or_imprecise_dtypes=True).then_inc(iota_ok, 1)
            pool.iota(keyidx[:], pattern=[[1, CACHED]], base=0, channel_multiplier=0,
                      allow_small_or_imprecise_dtypes=True).then_inc(iota_ok, 1)
            pool.iota(slot8[:], pattern=[[0, 1]], base=0, channel_multiplier=8).then_inc(iota_ok, 1)
            pool.wait_ge(bmask_ok, 1)
            pool.affine_select(out=blockmask[:], in_=blockmask[:], compare_op=ALU.is_ge, fill=0.0, base=0,
                               pattern=[[-R, N]], channel_multiplier=1).then_inc(bmask_ok, 1)
            pool.wait_ge(bmask_ok, 2)
            pool.affine_select(out=blockmask[:], in_=blockmask[:], compare_op=ALU.is_ge, fill=0.0, base=R - 1,
                               pattern=[[R, N]], channel_multiplier=-1).then_inc(bmask_ok, 1)
            pool.memset(halfs[:], -0.5).then_inc(iota_ok, 1)
            pool.memset(mask[:, :, CACHED:KEYS], 0.0).then_inc(iota_ok, 1)
            pool.wait_ge(pages_in, 16)
            pool.wait_ge(iota_ok, 5)
            for q in range(4):
                rows = slice(PAGE * q, PAGE * q + PAGE)
                pool.tensor_scalar(idx_a[rows, :], pages[rows, :].rearrange("p (m q) -> p m q", q=4)[:, :, q],
                                   float(PAGE * G), float(-PAGE * G * q), ALU.mult, ALU.add).then_inc(idx_ok, 1)
            pool.wait_ge(idx_ok, 4)
            pool.tensor_tensor(idx_a[:], idx_a[:], slot8[:].broadcast_to([P, N * KC]), ALU.add).then_inc(idx_ok, 1)
            pool.wait_ge(idx_ok, 5)

            def gather(rows_d, raw, arrived, idx, n, par):
                for c in range(KC):
                    k = n * KC + c
                    pool.indirect_dma_start(raw[:, par, c, :], None, rows_d,
                                            bass.IndirectOffsetOnAxis(idx[:, k:k + 1].bitcast(U32), 0)
                                            ).then_inc(arrived[par], 16)

            pool.wait_ge(tab_out, 32 * N)
            for n in range(2):
                gather(k_rows, kraw, kg_in, idx_a, n, n)
                gather(v_rows, vraw, vg_in, idx_a, n, n)

            def stats(J, par):
                wait_alone(pool, sq_done, J + 1)
                pool.tensor_scalar(ms[:, par, HG:], ss[:, par, HG:], 1.0 / P, EPS_RMS, ALU.mult, ALU.add
                                   ).then_inc(st_pool, 1)
                wait_alone(pool, st_pool, J * 3 + 1)
                pool.tensor_tensor(rs[:, par, HG:], ms[:, par, HG:], halfs[:, HG:], ALU.pow).then_inc(rms_k, 1)
                wait_alone(pool, sqq_done, (J + 1) * HG + 1)
                pool.tensor_scalar(ms[:, par, 0:HG], ss[:, par, 0:HG], 1.0 / P, EPS_RMS, ALU.mult, ALU.add
                                   ).then_inc(st_pool, 1)
                wait_alone(pool, st_pool, J * 3 + 2)
                pool.tensor_tensor(rs[:, par, 0:HG], ms[:, par, 0:HG], halfs[:, 0:HG], ALU.pow).then_inc(st_pool, 1)
                wait_alone(pool, st_pool, J * 3 + 3)
                pool.tensor_scalar(qs[:, par, :], rs[:, par, 0:HG], -SCALE, None, ALU.mult).then_inc(st_done, 1)

            stats(0, 0)
            for i in range(2):
                pool.wait_ge(x2_out[i], 16 * (N // 2))

            def step(g, n, last):
                J = g * N + n
                par = n % 2
                more = not (last and n >= N - 2)
                if n == 0 and not last:
                    pool.tensor_scalar(idx_b[:], idx_a[:], 1.0, None, ALU.add).then_inc(ix_ok, 1)
                    wait_alone(pool, ix_ok, g * 2 + 1)
                idx = idx_a if n < N - 2 else idx_b
                if more:
                    wait_alone(pool, t_full, g * PER_G + PRO + sum(len(groups_of(m, last)) for m in range(n)))
                    gather(k_rows, kraw, kg_in, idx, (n + 2) % N, par)
                wait_alone(pool, vg_in[par], (g * 4 + n // 2 + 1) * 64)
                wait_alone(pool, pv_full, J + 1)
                pool.tensor_copy(v_hi[:, 0:KC, :], vraw[:, par, :, :]).then_inc(vc_hi, 1)
                wait_alone(pool, vc_hi, J + 1)
                pool.tensor_tensor(v_lo[:, 0:KC, :], vraw[:, par, :, :], v_hi[:, 0:KC, :].bitcast(F32),
                                   ALU.subtract).then_inc(vc_lo, 1)
                if more:
                    wait_alone(pool, vc_lo, J + 1)
                    gather(v_rows, vraw, vg_in, idx, (n + 2) % N, par)
                if not (last and n == N - 1):
                    stats(J + 1, 1 - par)
                if n == N - 1 and not last:
                    wait_alone(pool, kg_in[1], (g * 4 + 4) * 64)
                    wait_alone(pool, vg_in[1], (g * 4 + 4) * 64)
                    pool.tensor_copy(idx_a[:], idx_b[:]).then_inc(ix_ok, 1)
                    wait_alone(pool, ix_ok, g * 2 + 2)
                    wait_alone(pool, kg_in[1], (g * 4 + 5) * 64)
                    wait_alone(pool, vg_in[1], (g * 4 + 5) * 64)
                    wait_alone(pool, kg_in[0], (g * 4 + 5) * 64)
                    wait_alone(pool, vg_in[0], (g * 4 + 5) * 64)

            with pool.Fori(0, G - 1) as g:
                for n in range(N):
                    step(g, n, False)
            for n in range(N):
                step(G - 1, n, True)
                if n == 0:
                    pool.wait_ge(lw_in, 16 * LATE_DMAS)
                    pool.tensor_copy(ebj[:, :, :, :], ebraw[:, :, :, :].rearrange("p e j r -> p j e r")
                                     ).then_inc(eb_ok, 1)
            pool.wait_ge(akv_full, N * G)
            pool.memset(before[:], 1.0).then_inc(bias_ok, 1)
            pool.wait_ge(bias_ok, 1)
            pool.affine_select(out=before[:], in_=before[:], compare_op=ALU.is_gt, fill=0.0, base=0,
                               pattern=[[1, E], [-1, E]], channel_multiplier=0).then_inc(bias_ok, 1)
            pool.wait_ge(bias_in, 16)
            for n in range(N):
                pool.wait_ge(x2r_in[n % 2], 16 * (n // 2 + 1))
                pool.tensor_tensor(x2r[:, n % 2, :], x2r[:, n % 2, :], bias_b[:], ALU.add).then_inc(x2b, 1)

        def mm3(pe, o, l_hi, l_lo, r_hi, r_lo, start, stop):
            pe.matmul(o, l_hi, r_lo, start=start, stop=False)
            pe.matmul(o, l_lo, r_hi, start=False, stop=False)
            return pe.matmul(o, l_hi, r_hi, start=False, stop=stop)

        @block.tensor
        def _(pe):
            pe.wait_ge(ident_ok, 2)
            for n in range(N):
                pe.wait_ge(x_in[n // 2], 16)
                if n >= 2:
                    pe.wait_ge(xt_act if n % 2 == 0 else xt_dve, n // 2)
                for c in range(NC_):
                    mm = pe.transpose(ps_t[n % 2][:, c * P:(c + 1) * P], xin[:, n, c * P:(c + 1) * P], ident[:])
                mm.then_inc(xt_full, 1)
            def part_a(g, par, arrivals, new=True, old=True, stage=None):
                t0 = g * 10
                go = g - 1

                def transposed(i, srcs):
                    pe.wait_ge(t2_done, t0 + i + 1)
                    for c, src in enumerate(srcs):
                        mm = pe.transpose(ps_t[i % 2][:, c * P:(c + 1) * P], src, ident[:])
                    return mm.then_inc(t2_full, 1)

                def w_group(t):
                    return transposed(t, [wraw[:, par, t, :].rearrange("p (o j) -> p o j", j=NC_)[:, :, j]
                                          for j in range(NC_)])

                def p_group(h):
                    return transposed(6 + h, [wpraw[:, par, ot, h * P:(h + 1) * P] for ot in range(NC_)])

                def fold(t):
                    pe.wait_ge(t2_done, t0 + t + 1 + 2)
                    for j in range(NC_):
                        mm = pe.matmul(ps_a[:, t * P:(t + 1) * P], wT[:, t, j, :], aall[:, :, j, :],
                                       start=(j == 0), stop=(j == NC_ - 1))
                    return mm

                def scores_s(s):
                    if s == 0:
                        pe.wait_ge(mix_done, go + 1)
                    pe.wait_ge(y_done, go * 8 + s + 1)
                    o = y_bank(s, not new)[:, 0:HG * R * (s + 1)]
                    pe.matmul(o.rearrange("p (h m) -> p h m", h=HG), zlT[:, s, :], mix[:, :, 0:R * (s + 1)],
                              start=True, stop=True).then_inc(y_full, 1)

                def fold_out(h):
                    if h == 0:
                        pe.wait_ge(t2_done, g * 10 + 2)
                    done = fv_even if h % 2 == 0 else fv_odd
                    pe.wait_ge(done, go * 2 + h // 2 + 1)
                    pe.matmul(ps_b[:, (h % 2) * HID:(h % 2 + 1) * HID], folded[:, 5, :], wpT[:, h, :],
                              start=True, stop=True).then_inc(fv_full, 1)

                def mix_product():
                    pe.wait_ge(fold_done, g + 1)
                    pe.wait_ge(y_done, g * 8 + 2)
                    for h in range(HG):
                        mm = pe.matmul(ps_q[:, h * P:(h + 1) * P], folded[:, h, :], folded[:, 4, :],
                                       start=True, stop=True)
                    mm.then_inc(mix_full, 1)

                if stage == "transposes":
                    pe.wait_ge(wq_in[par], arrivals)
                    for t in range(6):
                        w_group(t)
                    pe.wait_ge(wp_in[par], arrivals)
                    for h in range(HG):
                        p_group(h)
                    return
                if stage == "folds":
                    for t in range(6):
                        mm = fold(t)
                    mm.then_inc(fold_full, 1)
                    mix_product()
                    return
                if new:
                    pe.wait_ge(wq_in[par], arrivals)
                    w_group(0)
                    w_group(1)
                steps = [(scores_s, 0), (fold, 0), (fold_out, 0), (w_group, 2), (scores_s, 1), (fold, 1),
                         (fold_out, 1), (w_group, 3), (scores_s, 2), (fold, 2), (scores_s, 3), (w_group, 4),
                         (fold_out, 2), (fold, 3), (scores_s, 4), (w_group, 5), (fold_out, 3), (fold, 4),
                         (scores_s, 5), (p_group, 0), (scores_s, 6), (fold, 5), (p_group, 1), (scores_s, 7)]
                for what, i in steps:
                    if what in (scores_s, fold_out):
                        if old:
                            what(i)
                    elif new:
                        if what == p_group and i == 0:
                            pe.wait_ge(wp_in[par], arrivals)
                        mm = what(i)
                        if what == fold and i == 5:
                            mm.then_inc(fold_full, 1)
                if new:
                    p_group(2)
                    mix_product()
                    p_group(3)

            pe.wait_ge(xt_act, 4)
            pe.wait_ge(xt_dve, 4)
            part_a(0, 0, 16, stage="transposes")
            pe.wait_ge(lora_in, 32 * N)
            for c in range(NC_):
                mm = pe.transpose(ps_q[:, c * P:(c + 1) * P], bsel[:, c * P:(c + 1) * P], ident[:])
            mm.then_inc(bt_full, 1)
            pe.wait_ge(bt_done, 1)
            for h in range(2):
                for c in range(NC_):
                    mm = pe.matmul(ps_a[:, h * HID:(h + 1) * HID], bselT[:, c, :],
                                   xT[:, c, 4 * h:4 * h + 4, :].rearrange("p n b -> p (n b)"),
                                   start=(c == 0), stop=(c == NC_ - 1))
                mm.then_inc(zT_full, 1)
            pe.wait_ge(zT_done, 2)
            for n in range(N):
                mm = pe.matmul(ps_o[:, n * R:(n + 1) * R], zlT[:, n, :], ident[:, n * R:(n + 1) * R],
                               start=True, stop=True)
            mm.then_inc(zl_full, 1)
            pe.wait_ge(zl_done, 1)

            part_a(0, 0, 16, stage="folds")
            with pe.Fori(0, G // 2 - 1) as gp:
                for par in range(2):
                    part_a(gp * 2 + par + 1, 1 - par, (gp + 1 + par) * 16)
            part_a(G - 1, 1, G // 2 * 16)
            part_a(G, 0, 0, new=False)

            pe.wait_ge(t2_done, 10 * G + 2)
            pe.wait_ge(fv_even, 2 * G + 1)
            pe.wait_ge(fv_odd, 2 * G + 1)

            def z_transposes(k):
                pe.wait_ge(z_done, k + 1)
                for half in range(2):
                    if k >= 1:
                        pe.wait_ge(zt_done, 2 * (k - 1) + half + 1)
                    for i in range(4):
                        g = 4 * half + i
                        mm = pe.transpose(ps_t[half][:, i * P:(i + 1) * P],
                                          z_ring[:, k % 2, g * HG:(g + 1) * HG, :].rearrange("p h m -> p (h m)"),
                                          ident[:])
                    mm.then_inc(zt_full, 1)

            def z_products(k):
                s, tp = PAIRS[k]
                o = ps_o if s % 2 == 0 else ps_q
                if tp == 0 and s >= 2:
                    pe.wait_ge(out2_done, s - 1)
                for g in range(G):
                    if g % 4 == 0:
                        pe.wait_ge(zt_done, 2 * k + g // 4 + 1)
                    mm = pe.matmul(o[:, :], zT_ring[:, k % 2, g, :], fold_v[:, tp, g, :],
                                   start=(tp == 0 and g == 0), stop=(tp == s // 2 and g == G - 1))
                if tp == s // 2:
                    mm.then_inc(out2_full, 1)

            def x2_transposes(s):
                pe.wait_ge(out2_done, s + 1)
                if s >= 2:
                    pe.wait_ge(x2t_lo, s - 1)
                for c in range(NC_):
                    mm = pe.transpose(ps_b[:, (s % 2) * HID + c * P:(s % 2) * HID + (c + 1) * P],
                                      x2sb[:, s % 2, c * P:(c + 1) * P], ident[:])
                mm.then_inc(x2t_full, 1)

            def w0_transposes(t):
                if t == 0:
                    pe.wait_ge(w0_in, 48)
                    pe.wait_ge(y_done, 8 * G + 2)
                if t >= 2:
                    pe.wait_ge(w0_lo, t - 1)
                for c in range(NC_):
                    mm = pe.transpose(ps_a[:, (t % 2) * HID + c * P:(t % 2) * HID + (c + 1) * P],
                                      w0raw_a[:, t, c * P:(c + 1) * P], ident[:])
                mm.then_inc(w0_full, 1)

            z_transposes(0)
            for k in range(len(PAIRS)):
                if k + 1 < len(PAIRS):
                    z_transposes(k + 1)
                z_products(k)
                s, tp = PAIRS[k]
                if tp == 0 and s >= 1:
                    x2_transposes(s - 1)
                if 0 <= k - K_W0 < 6:
                    w0_transposes(k - K_W0)

            pe.sem_inc(pv_full, 1)

            def transposed(idx, bank, outs_ins):
                pe.wait_ge(t_lo, idx + 1)
                for o, i in outs_ins:
                    mm = pe.transpose(ps_t[bank][:, o * P:(o + 1) * P], i, ident[:])
                return mm.then_inc(t_full, 1)

            def w_tile(idx, bank, t, arrivals):
                pe.wait_ge(wt_in[t % 2], arrivals)
                transposed(idx, bank, [(c, wtile[:, t % 2, c * P:(c + 1) * P]) for c in range(NC_)])

            def k_group(idx, bank, g, n):
                pe.wait_ge(kg_in[n % 2], (g * 4 + n // 2 + 1) * 64)
                transposed(idx, bank, [(c, kraw[:, n % 2, c, :]) for c in range(KC)])

            def project_q(n, wpar, cs):
                for c in cs:
                    wh, wl = (w[:, bass.ds(wpar, 1), c, 0:QW].rearrange("p a m -> p (a m)") for w in (wa_hi, wa_lo))
                    mm = mm3(pe, ps_q[:, :], x2T_hi[:, c, n, :], x2T_lo[:, c, n, :], wh, wl, c == 0, c == NC_ - 1)
                if cs[-1] == NC_ - 1:
                    mm.then_inc(aq_full, 1)

            def project_kv(n, wpar):
                for c in range(NC_):
                    wh, wl = (w[:, bass.ds(wpar, 1), c, QW:PW].rearrange("p a m -> p (a m)") for w in (wa_hi, wa_lo))
                    mm = mm3(pe, ps_o[:, 0:2 * P], x2T_hi[:, c, n, :], x2T_lo[:, c, n, :], wh, wl,
                             c == 0, c == NC_ - 1)
                mm.then_inc(akv_full, 1)

            pe.wait_ge(w0_lo, 6)
            pe.wait_ge(x2t_lo, 1)
            pe.wait_ge(out2_done, N - 1)
            project_kv(0, 0)
            x2_transposes(N - 1)
            project_q(0, 0, range(NC_))
            pe.wait_ge(w0_in, 64)
            for t in range(HG):
                transposed(t, t % 2, [(c, w0raw_b[:, t, c * P:(c + 1) * P]) for c in range(NC_)])
            k_group(HG, HG % 2, 0, 0)
            pe.wait_ge(rq_done, 1)
            transposed(HG + 1, (HG + 1) % 2, [(h, rope_a[:, h, :]) for h in range(HG)])

            def own_k(J):
                pe.wait_ge(rk_done, J + 1)
                pe.transpose(ps_k, rope_a[:, HG, :], ident[:]).then_inc(kt_full, 1)

            def values(cs, own_group, last_head_group):
                for c in cs:
                    if c == 0:
                        pe.wait_ge(t_lo, last_head_group + 1 + 2)
                    if c == KC:
                        pe.wait_ge(t_lo, own_group + 1 + 2)
                    mm = mm3(pe, ps_o[:, :], v_hi[:, c, :], v_lo[:, c, :], pT_hi[:, c, :], pT_lo[:, c, :],
                             c == 0, c == KC)
                if cs[-1] == KC:
                    mm.then_inc(pv_full, 1)

            def out_proj(wpar, heads):
                for h in heads:
                    wh, wl = (w[:, bass.ds(wpar, 1), h, :].rearrange("p a m -> p (a m)") for w in (wo_hi, wo_lo))
                    mm = mm3(pe, ps_o[:, :], oT_hi[:, h, :], oT_lo[:, h, :], wh, wl, h == 0, h == HG - 1)
                if heads[-1] == HG - 1:
                    mm.then_inc(f_full, 1)

            own_k(0)

            def late_group(i, bank, t):
                if t == 0:
                    pe.wait_ge(lw_in, 16 * LATE_DMAS)
                if t < NC_:
                    transposed(i, bank, [(c, wbraw[:, t, c * P:(c + 1) * P]) for c in range(NC_)])
                elif t == 4:
                    transposed(i, bank, [(c, earaw[:, c * P:(c + 1) * P]) for c in range(NC_)])
                elif t == 5:
                    pe.wait_ge(t_lo, i + 1)
                    for c in range(NC_):
                        mm = pe.transpose(ps_t[bank][:, c * P:c * P + E], gateraw[:, c * P:(c + 1) * P],
                                          ident[0:E, 0:E])
                    mm.then_inc(t_full, 1)
                else:
                    pe.wait_ge(eb_ok, 1)
                    transposed(i, bank, [(j, ebj[:, j, :, :].rearrange("p e r -> p (e r)")) for j in range(NC_)])

            def step(g, n, first, last):
                J = g * N + n
                base = g * PER_G + PRO
                par = n % 2
                names = groups_of(n, last)
                first = first and n == 0
                nxt = not (last and n == N - 1)
                n1 = (n + 1) % N
                wpar1 = (g + (n == N - 1)) % 2
                wpar0 = (g + (n == 0)) % 2
                start = base + t_index(n, names[0], last)[0]

                def idx(name):
                    i, bank = t_index(n, name, last)
                    return base + i, bank

                def scores(h, halves=(0, 1)):
                    s, q = ps_s[h % 2], slice(h * P, (h + 1) * P)
                    if 0 in halves:
                        pe.wait_ge(s_read, J * 4 + h + 1)
                        mm3(pe, s[:, 0:HALF], qT_hi[:, q], qT_lo[:, q], kT_hi[:, par, 0:HALF],
                            kT_lo[:, par, 0:HALF], True, True)
                    if 1 in halves:
                        if h == 0:
                            pe.wait_ge(kt_lo, J + 1)
                        mm3(pe, s[:, HID:HID + HALF], qT_hi[:, q], qT_lo[:, q], kT_hi[:, par, HALF:KEYS],
                            kT_lo[:, par, HALF:KEYS], True, True).then_inc(s_full, 1)

                def probs_group(h):
                    pe.wait_ge(p_dve if h < 2 else p_act, J * 2 + h % 2 + 1)
                    transposed(*idx(f"D{h}"), [(c, sm[:, h, c * P:(c + 1) * P]) for c in range(KC)])

                pe.wait_ge(t_lo, start + (2 if first else 0))
                scores(0, [0])
                scores(1, [0])
                scores(0, [1])
                scores(1, [1])
                for name in names:
                    if name[0] == "L":
                        late_group(*idx(name), int(name[1:]))
                    if name[0] == "W":
                        t = int(name[1:])
                        w_tile(*idx(name), t, g * (16 * TILES_W // 2) + 16 * (t // 2 + 1))
                if not first:
                    pe.wait_ge(f_done, J)
                    pe.wait_ge(vc_lo, J)
                    values(range(KC + 1), start - 1, start - 2)
                if nxt:
                    k_group(*idx("K"), g + (n == N - 1), n1)
                    pe.wait_ge(rq_done, J + 1)
                    pe.wait_ge(sqq_done, (J + 1) * HG + 1)
                    if n == N - 1:
                        pe.wait_ge(t_lo, base + t_index(6, "W9", last)[0] + 1 + 2)
                    project_q(n1, wpar1, [0, 1])
                probs_group(0)
                scores(2)
                if nxt:
                    project_q(n1, wpar1, [2, 3])
                probs_group(1)
                scores(3)
                if not first:
                    pe.wait_ge(o_lo, J)
                if nxt:
                    pe.wait_ge(vs_lo, J + 1)
                    project_kv(n1, wpar1)
                probs_group(2)
                if not first:
                    if nxt:
                        pe.wait_ge(kv_copied, J + 2)
                    out_proj(wpar0, [0])
                if nxt:
                    pe.wait_ge(rq_done, J + 2)
                    transposed(*idx("q"), [(h, rope_a[:, h, :]) for h in range(HG)])
                if not first:
                    out_proj(wpar0, [1])
                    out_proj(wpar0, [2])
                probs_group(3)
                if not first:
                    out_proj(wpar0, [3])
                if nxt:
                    pe.wait_ge(s_read, J * 4 + 4 + 2)
                    own_k(J + 1)
                transposed(*idx("DS"), [(h, sm[:, h, CACHED:KEYS]) for h in range(HG)])

            for n in range(N):
                step(0, n, True, False)
            with pe.Fori(1, G - 1) as g:
                for n in range(N):
                    step(g, n, False, False)
            for n in range(N):
                step(G - 1, n, False, True)
            def y_transposes(n):
                pe.wait_ge(f_done, N * (G - 1) + n + 2)
                if n < 2:
                    pe.wait_ge(t_lo, END + n + 1)
                if n >= 2:
                    pe.wait_ge(yt_done, n - 1)
                for c in range(NC_):
                    mm = pe.transpose(yt_bank(n)[:, c * P:(c + 1) * P], y[:, n, c * P:(c + 1) * P], ident[:])
                mm.then_inc(yt_full, 1)

            def gate(n):
                pe.wait_ge(yt_done, n + 1)
                if n >= 2:
                    pe.wait_ge(hw_done, n - 1)
                for c in range(NC_):
                    mm = mm3(pe, ps_b[:, (n % 2) * HID:(n % 2) * HID + P + E], yT_hi[:, n % 2, c, :],
                             yT_lo[:, n % 2, c, :], gaT_hi[:, c, :], gaT_lo[:, c, :], c == 0, c == NC_ - 1)
                mm.then_inc(g_full, 1)

            def base(n):
                if n >= 2:
                    pe.wait_ge(fin_done, n - 1)
                for c in range(NC_):
                    mm = mm3(pe, ps_a[:, (n % 2) * HID:(n % 2 + 1) * HID], yT_hi[:, n % 2, c, :],
                             yT_lo[:, n % 2, c, :], wbT_hi[:, c, :], wbT_lo[:, c, :], c == 0, False)
                mm.then_inc(base_full, 1)

            def hw_transpose(n):
                pe.wait_ge(hw_done, n + 1)
                if n >= 1:
                    pe.wait_ge(ht_done, n)
                pe.transpose(ps_q[:, 0:P], hw[:, n % 2, :, :].rearrange("p e r -> p (e r)"), ident[:]
                             ).then_inc(ht_full, 1)

            def experts(n):
                pe.wait_ge(ht_done, n + 1)
                pe.matmul(ps_a[:, (n % 2) * HID:(n % 2 + 1) * HID], hwT[:, n % 2, :], ebT[:, :],
                          start=False, stop=True).then_inc(d_full, 1)

            y_transposes(0)
            pe.wait_ge(f_done, G * N)
            pe.wait_ge(vc_lo, G * N)
            values(range(KC + 1), END - 1, END - 2)
            y_transposes(1)
            pe.wait_ge(s_read, G * N * HG + 2)
            gate(0)
            base(0)
            pe.wait_ge(o_lo, G * N)
            out_proj((G - 1) % 2, range(HG))
            for n in range(1, N):
                gate(n)
                if n + 1 < N:
                    y_transposes(n + 1)
                hw_transpose(n - 1)
                base(n)
                experts(n - 1)
            hw_transpose(N - 1)
            experts(N - 1)

        @block.scalar
        def _(act):
            for n in range(0, N, 2):
                act.wait_ge(xt_full, n + 1)
                act.activation(xT[:, :, n, :], ps_t[0][:, :].rearrange("p (c b) -> p c b", c=NC_), ACT.Copy
                               ).then_inc(xt_act, 1)
            act.wait_ge(xt_dve, N // 2)
            act.sem_inc(t2_done, 2)
            act.sem_inc(fv_even, 1)

            def fold_v_copy(g, h, tps):
                for tp in tps:
                    ins = act.activation(
                        fold_v[2 * R * h:2 * R * h + 2 * R, tp, bass.ds(g, 1), :].rearrange("p a m -> p (a m)"),
                        ps_b[2 * R * tp:2 * R * tp + 2 * R, (h % 2) * HID:(h % 2 + 1) * HID], ACT.Copy)
                if tps[-1] == 3:
                    ins.then_inc(fv_even if h % 2 == 0 else fv_odd, 1)

            def part_a(g, old=True):
                def copy_group(i):
                    act.wait_ge(t2_full, g * 10 + i + 1)
                    if i < 6:
                        dst, src = wT[:, i, :, :], ps_t[i % 2][:, :].rearrange("p (c b) -> p c b", c=NC_)
                    else:
                        dst, src = wpT[:, i - 6, :], ps_t[i % 2][:, :]
                    act.activation(dst, src, ACT.Copy).then_inc(t2_done, 1)

                for i in range(10):
                    copy_group(i)
                    if old and 2 <= i < 6:
                        h = 0 if i < 4 else 2
                        act.wait_ge(fv_full, (g - 1) * 4 + h + 1)
                        fold_v_copy(g - 1, h, range(2) if i % 2 == 0 else range(2, 4))
                    if i == (7 if old else 9):
                        act.wait_ge(fold_full, g + 1)
                        act.activation(folded[:, :, :].rearrange("p a m -> p (a m)"), ps_a[:, 0:6 * P], ACT.Copy
                                       ).then_inc(fold_done, 1)

            part_a(0, old=False)
            with act.Fori(1, G) as g:
                part_a(g)

            def soft_exp(i):
                s0, count = SOFT[i]
                act.wait_ge(smx, 4 * i + 2)
                sc = score[:, s0:s0 + count, :, :].rearrange("p s h t -> p (s h t)")
                act.activation(sc, sc, ACT.Exp, scale=SCALE).then_inc(exp2, 1)

            def zt_copy(k):
                for half in range(2):
                    act.wait_ge(zt_full, 2 * k + half + 1)
                    act.activation(zT_ring[:, k % 2, 4 * half:4 * half + 4, :].rearrange("p g m -> p (g m)"),
                                   ps_t[half][:, :], ACT.Copy).then_inc(zt_done, 1)

            for h in range(HG):
                act.wait_ge(fv_full, (G - 1) * 4 + h + 1)
                fold_v_copy(G - 1, h, range(4))
                if h == 0:
                    soft_exp(0)

            def x2_hi(s):
                act.wait_ge(x2t_full, s + 1)
                act.activation(x2T_hi[:, :, s, :],
                               ps_b[:, (s % 2) * HID:(s % 2 + 1) * HID].rearrange("p (c b) -> p c b", c=NC_),
                               ACT.Copy).then_inc(x2t_hi, 1)

            for k in range(len(PAIRS)):
                zt_copy(k)
                if k == 1:
                    soft_exp(1)
                    soft_exp(2)
                s, tp = PAIRS[k]
                if tp == 0 and s >= 2:
                    x2_hi(s - 2)
                if 0 <= k - K_W0 < 6:
                    t = k - K_W0
                    if t == 0:
                        act.wait_ge(tb, TB_ALL)
                    act.wait_ge(w0_full, t + 1)
                    act.activation(w_dst(wa_hi, wo_hi, 0, t),
                                   ps_a[:, (t % 2) * HID:(t % 2 + 1) * HID].rearrange("p (c m) -> p c m", c=NC_),
                                   ACT.Copy).then_inc(w0_hi, 1)
                if k == 2:
                    act.wait_ge(tb, TB_ANGLES)
                    act.activation(sin_t[:], sin_t[:], ACT.Sin).then_inc(sin_ok, 1)
                    act.activation(cos_t[:], cos_t[:], ACT.Sin).then_inc(sin_ok, 1)
            x2_hi(N - 2)

            def copy_hi(idx, bank, dst, width=HID):
                act.wait_ge(t_full, idx + 1)
                src = ps_t[bank][:, 0:width]
                if len(dst.shape) == 3:
                    src = src.rearrange("p (c m) -> p c m", c=dst.shape[1])
                act.activation(dst, src, ACT.Copy).then_inc(t_hi, 1)

            def copy_kv(J):
                act.wait_ge(akv_full, J + 1)
                act.activation(kvown[:, :, :].rearrange("p a d -> p (a d)"), ps_o[:, 0:2 * P], ACT.Copy
                               ).then_inc(kv_copied, 1)

            def square_k(J, par):
                act.wait_ge(kv_copied, J + 1)
                act.activation(rope_b[:, HG, :], kvown[:, 0, :], ACT.Square, accum_out=ss[:, par, HG:HG + 1]
                               ).then_inc(sq_done, 1)

            def own_k_hi(J, par):
                act.wait_ge(kt_full, J + 1)
                act.activation(kT_hi[:, par, CACHED:KEYS], ps_k, ACT.Copy).then_inc(kt_hi, 1)

            def squares_q(J, par, heads=range(HG)):
                for h in heads:
                    if h == 0:
                        act.wait_ge(ro_ab, (J + 1) * 3)
                    act.wait_ge(sqq_done, J * HG + h + 1)
                    act.activation(squares[:], ps_q[:, h * P:(h + 1) * P], ACT.Square, accum_out=ss[:, par, h:h + 1]
                                   ).then_inc(sqq_done, 1)

            act.sem_inc(sqq_done, 1)
            copy_kv(0)
            square_k(0, 0)
            x2_hi(N - 1)
            for t in range(HG):
                copy_hi(t, t % 2, w_dst(wa_hi, wo_hi, 0, 6 + t))
            for i in range(2):
                act.wait_ge(x2_out[i], 16 * (N // 2))
            squares_q(0, 0)
            copy_hi(HG, HG % 2, kT_hi[:, 0, 0:CACHED])
            copy_hi(HG + 1, (HG + 1) % 2, qT_hi[:, :])
            own_k_hi(0, 0)

            def output_hi(count):
                act.wait_ge(pv_full, count + 1)
                act.activation(oT_hi[:, :, :].rearrange("p h m -> p (h m)"), ps_o[:, :], ACT.Copy).then_inc(o_hi, 1)

            def late_copy(idx, bank, i):
                act.wait_ge(t_full, idx + 1)
                if i < 6:
                    dst, src = late_parts(bank, i, 0)
                else:
                    dst = ebT[:, :].rearrange("p (o j) -> p j o", j=NC_)
                    src = ps_t[bank][:, :].rearrange("p (j o) -> p j o", j=NC_)
                act.activation(dst, src, ACT.Copy).then_inc(t_hi, 1)

            def step(g, n, first, last):
                first = first and n == 0
                J = g * N + n
                base = g * PER_G + PRO
                names = groups_of(n, last)
                nxt = not (last and n == N - 1)
                kpar1 = 1 - n % 2

                def group(name):
                    i, bank = t_index(n, name, last)
                    if name[0] == "L":
                        late_copy(base + i, bank, int(name[1:]))
                        return
                    dst, width = hi_lo_target(name, g, kpar1, 0)
                    copy_hi(base + i, bank, dst, width)

                def exponentials(h):
                    act.wait_ge(s_read, J * 4 + h + 1 + 2)
                    act.activation(sm[:, h, :], sm[:, h, :], ACT.Exp, bias=mn[:, h:h + 1], scale=-1.0,
                                   accum_out=den[:, h:h + 1]).then_inc(e_done, 1)

                def own_v_hi():
                    act.wait_ge(kv_copied, J + 1)
                    act.wait_ge(pv_full, J + 1)
                    act.activation(v_hi[:, KC, :], kvown[:, 1, :], ACT.Copy).then_inc(vs_hi, 1)

                def normalise(h):
                    act.wait_ge(r_done, J * 4 + h + 1)
                    act.activation(sm[:, h, :], sm[:, h, :], ACT.Copy, scale=rd[:, h:h + 1]).then_inc(p_act, 1)

                w = [m for m in names if m[0] in "WL"]
                exponentials(0)
                if w:
                    group(w[0])
                exponentials(1)
                if len(w) > 1:
                    group(w[1])
                if not first:
                    output_hi(J)
                own_v_hi()
                if nxt:
                    group("K")
                group("D0")
                exponentials(2)
                group("D1")
                normalise(2)
                if nxt:
                    squares_q(J + 1, kpar1, [0])
                    copy_kv(J + 1)
                exponentials(3)
                if nxt:
                    square_k(J + 1, kpar1)
                group("D2")
                if nxt:
                    squares_q(J + 1, kpar1, [1])
                normalise(3)
                if nxt:
                    group("q")
                    squares_q(J + 1, kpar1, [2, 3])
                group("D3")
                if nxt:
                    own_k_hi(J + 1, kpar1)
                group("DS")

            for n in range(N):
                step(0, n, True, False)
            with act.Fori(1, G - 1) as g:
                for n in range(N):
                    step(g, n, False, False)
            for n in range(N):
                step(G - 1, n, False, True)
            def y_copy(n):
                act.wait_ge(yt_full, n + 1)
                if n >= 2:
                    act.wait_ge(g_full, n - 1)
                    act.wait_ge(base_full, n - 1)
                act.activation(yT_hi[:, n % 2, :, :].rearrange("p c m -> p (c m)"), yt_bank(n)[:, :], ACT.Copy
                               ).then_inc(yt_hi, 1)

            def gate_exp(n):
                act.wait_ge(gm, n + 1)
                act.activation(routes[:, n % 2, 0, :], ps_b[:, (n % 2) * HID + P:(n % 2) * HID + P + E], ACT.Exp,
                               bias=route1[:, n % 2, 0:1], accum_out=route1[:, n % 2, 1:2]).then_inc(ge, 1)

            def hw_copy(n):
                act.wait_ge(ht_full, n + 1)
                act.activation(hwT[:, n % 2, :], ps_q[:, 0:P], ACT.Copy).then_inc(ht_done, 1)

            y_copy(0)
            output_hi(G * N)
            y_copy(1)
            for n in range(N):
                gate_exp(n)
                if 2 <= n + 1 < N:
                    y_copy(n + 1)
                if n >= 1:
                    hw_copy(n - 1)
            hw_copy(N - 1)

        @block.vector
        def _(dve):
            for n in range(1, N, 2):
                dve.wait_ge(xt_full, n + 1)
                dve.tensor_copy(xT[:, :, n, :], ps_t[1][:, :].rearrange("p (c b) -> p c b", c=NC_)
                                ).then_inc(xt_dve, 1)
            dve.wait_ge(bt_full, 1)
            dve.tensor_copy(bselT[:, :, :].rearrange("p c m -> p (c m)"), ps_q[:, :]).then_inc(bt_done, 1)
            dve.memset(score[:], NEG).then_inc(smx0, 1)
            dve.wait_ge(bmask_ok, 3)
            for h in range(2):
                dve.wait_ge(zT_full, h + 1)
                dve.tensor_tensor(zlT[:, 4 * h:4 * h + 4, :],
                                  ps_a[:, h * HID:(h + 1) * HID].rearrange("p (n b) -> p n b", n=4),
                                  blockmask[:, 4 * h:4 * h + 4].unsqueeze(2).broadcast_to([P, 4, P]), ALU.mult
                                  ).then_inc(zT_done, 1)
            dve.wait_ge(zl_full, 1)
            dve.tensor_copy(zl[:, :, :].rearrange("p n r -> p (n r)"), ps_o[:, 0:P]).then_inc(zl_done, 1)
            dve.wait_ge(zl_done, 1)
            dve.wait_ge(smx0, 1)
            dve.sem_inc(y_done, 2)
            dve.sem_inc(fv_odd, 1)

            def scores_s(g, s, end=False):
                w = R * (s + 1)
                dve.wait_ge(y_full, g * 8 + s + 1)
                dve.wait_ge(y_red, g * 8 + s + 1)
                src = y_bank(s, end)[:, 0:HG * w].rearrange("p (h m) -> p h m", h=HG)
                zz = zl[:, 0:s + 1, :].rearrange("p n r -> p (n r)").unsqueeze(1).broadcast_to([P, HG, w])
                dve.tensor_tensor(prod[:, s % 2, :, 0:w], src, zz, ALU.mult).then_inc(y_done, 1)

            def sums_s(g, s):
                dve.wait_ge(y_done, g * 8 + s + 1 + 2)
                dve.tensor_reduce(score[:, s, bass.ds(g * HG, HG), 0:s + 1],
                                  prod[:, s % 2, :, 0:R * (s + 1)].rearrange("p h (t r) -> p h t r", r=R),
                                  AX.X, ALU.add).then_inc(y_red, 1)

            def fold_v_copy(g, h, tps):
                if tps[0] == 0:
                    dve.wait_ge(fv_full, g * 4 + h + 1)
                for tp in tps:
                    ins = dve.tensor_copy(
                        fold_v[2 * R * h:2 * R * h + 2 * R, tp, bass.ds(g, 1), :].rearrange("p a m -> p (a m)"),
                        ps_b[2 * R * tp:2 * R * tp + 2 * R, (h % 2) * HID:(h % 2 + 1) * HID])
                if tps[-1] == 3:
                    ins.then_inc(fv_odd, 1)

            def mix_copy(g):
                dve.wait_ge(mix_full, g + 1)
                dve.tensor_copy(mix[:, :, :].rearrange("p h m -> p (h m)"), ps_q[:, :]).then_inc(mix_done, 1)

            def part_a(g):
                o = g - 1
                scores_s(o, 0)
                scores_s(o, 1)
                sums_s(o, 0)
                fold_v_copy(o, 1, range(2))
                scores_s(o, 2)
                sums_s(o, 1)
                fold_v_copy(o, 1, range(2, 4))
                scores_s(o, 3)
                sums_s(o, 2)
                scores_s(o, 4)
                sums_s(o, 3)
                fold_v_copy(o, 3, range(2))
                scores_s(o, 5)
                sums_s(o, 4)
                fold_v_copy(o, 3, range(2, 4))
                scores_s(o, 6)
                sums_s(o, 5)
                scores_s(o, 7)
                sums_s(o, 6)
                sums_s(o, 7)
                mix_copy(g)

            dve.sem_inc(y_red, 2)
            mix_copy(0)
            with dve.Fori(1, G) as g:
                part_a(g)

            def soft_views(i):
                s0, count = SOFT[i]
                sc = score[:, s0:s0 + count, :, :].rearrange("p s h t -> p (s h) t")
                return sc, count * NH, rmax[:, s0 * NH:(s0 + count) * NH], rden[:, s0 * NH:(s0 + count) * NH]

            def soft_max(i):
                s0, count = SOFT[i]
                sc, rows, rm, _ = soft_views(i)
                dve.wait_ge(y_red, 8 * (G - 1) + s0 + count + 2)
                dve.tensor_reduce(rm, sc, AX.X, ALU.max).then_inc(smx, 1)
                dve.wait_ge(smx, 4 * i + 1)
                dve.tensor_tensor(sc, sc, rm.unsqueeze(2).broadcast_to([P, rows, N]), ALU.subtract).then_inc(smx, 1)

            def soft_sum(i):
                sc, rows, _, rr = soft_views(i)
                dve.wait_ge(exp2, i + 1)
                dve.tensor_reduce(rr, sc, AX.X, ALU.add).then_inc(smx, 1)
                dve.wait_ge(smx, 4 * i + 3)
                dve.reciprocal(rr, rr).then_inc(smx, 1)
                dve.wait_ge(smx, 4 * i + 4)
                dve.tensor_tensor(sc, sc, rr.unsqueeze(2).broadcast_to([P, rows, N]), ALU.mult).then_inc(prob, 1)

            def last_scores(s0):
                scores_s(G - 1, s0, True)
                scores_s(G - 1, s0 + 1, True)
                sums_s(G - 1, s0)
                sums_s(G - 1, s0 + 1)

            last_scores(0)
            soft_max(0)
            last_scores(2)
            soft_sum(0)

            def z_pair(k):
                s, tp = PAIRS[k]
                dve.wait_ge(prob, [i for i, (s0, _) in enumerate(SOFT) if s0 <= s][-1] + 1)
                if k >= 2:
                    dve.wait_ge(zt_full, 2 * (k - 1))
                pr = score[:, s, :, 2 * tp:2 * tp + 2].unsqueeze(3).broadcast_to([P, NH, 2, R])
                zz = zl[:, 2 * tp:2 * tp + 2, :].unsqueeze(1).broadcast_to([P, NH, 2, R])
                dve.tensor_tensor(z_ring[:, k % 2, :, :].rearrange("p h (t r) -> p h t r", r=R), pr, zz, ALU.mult
                                  ).then_inc(z_done, 1)

            def x2_sum(s):
                dve.wait_ge(out2_full, s + 1)
                dve.wait_ge(xres_in[s % 2], 16 * (s // 2 + 1))
                if s >= 2:
                    dve.wait_ge(x2_out[s % 2], 16 * (s // 2))
                    dve.wait_ge(x2t_full, s - 1)
                dve.tensor_tensor(x2sb[:, s % 2, :], ps_o[:, :] if s % 2 == 0 else ps_q[:, :],
                                  xres[:, s % 2, :], ALU.add).then_inc(out2_done, 1)

            def x2_low(s):
                dve.wait_ge(x2t_hi, s + 1)
                dve.tensor_tensor(x2T_lo[:, :, s, :],
                                  ps_b[:, (s % 2) * HID:(s % 2 + 1) * HID].rearrange("p (c b) -> p c b", c=NC_),
                                  x2T_hi[:, :, s, :].bitcast(F32), ALU.subtract).then_inc(x2t_lo, 1)

            def angles():
                dve.wait_ge(small_in, 64)
                dve.wait_ge(iota_ok, 5)
                dve.wait_ge(y_full, 8 * G)
                c1 = 6.28125
                c2 = float(2 * np.pi - c1)
                magic = 1.5 * 2.0 ** 23
                dve.tensor_copy(len_f[:], len_i[:]).then_inc(tb, 1)
                dve.wait_ge(tb, 1)
                dve.tensor_scalar(pos[:], len_f[:], tok[:, 0:1], None, ALU.add).then_inc(tb, 1)
                dve.wait_ge(tb, 2)
                dve.tensor_tensor(theta[:], pos[:].unsqueeze(2).broadcast_to([P, N, 64]),
                                  freqs[:].unsqueeze(1).broadcast_to([P, N, 64]), ALU.mult).then_inc(tb, 1)
                dve.wait_ge(tb, 3)
                i = 3
                for dst, quarter in ((sin_t, 0.0), (cos_t, 0.25)):
                    dve.tensor_scalar(turns[:], theta[:], float(1 / (2 * np.pi)), quarter, ALU.mult, ALU.add
                                      ).then_inc(tb, 1)
                    dve.wait_ge(tb, i + 1)
                    dve.tensor_scalar(turns2[:], turns[:], magic, None, ALU.add).then_inc(tb, 1)
                    dve.wait_ge(tb, i + 2)
                    dve.tensor_scalar(turns[:], turns2[:], -magic, None, ALU.add).then_inc(tb, 1)
                    dve.wait_ge(tb, i + 3)
                    dve.scalar_tensor_tensor(out=turns2[:], in0=turns[:], scalar=-c1, in1=theta[:],
                                             op0=ALU.mult, op1=ALU.add).then_inc(tb, 1)
                    dve.wait_ge(tb, i + 4)
                    dve.scalar_tensor_tensor(out=dst[:], in0=turns[:], scalar=-c2, in1=turns2[:],
                                             op0=ALU.mult, op1=ALU.add).then_inc(tb, 1)
                    dve.wait_ge(tb, i + 5)
                    i += 5
                dve.tensor_scalar(cos_t[:], cos_t[:], float(np.pi / 2), None, ALU.add).then_inc(tb, 1)
                dve.wait_ge(tb, i + 1)
                for dst in (sin_t, cos_t):
                    dve.tensor_scalar(dst[:], dst[:], 3.1415925, -3.1415925, ALU.min, ALU.max).then_inc(tb, 1)
                assert i + 3 == TB_ANGLES

            def tables():
                dve.wait_ge(sin_ok, 2)
                for which, w in ((0, qn_b), (2, kn_b)):
                    for half in range(2):
                        wh = w[:, 64 * half:64 * half + 64].unsqueeze(1).broadcast_to([P, N, 64])
                        dve.tensor_tensor(tabs[:, :, which, 64 * half:64 * half + 64], cos_t[:], wh, ALU.mult
                                          ).then_inc(tb, 1)
                    dve.scalar_tensor_tensor(out=tabs[:, :, which + 1, 0:64], in0=sin_t[:], scalar=-1.0,
                                             in1=w[:, 64:128].unsqueeze(1).broadcast_to([P, N, 64]),
                                             op0=ALU.mult, op1=ALU.mult).then_inc(tb, 1)
                    dve.tensor_tensor(tabs[:, :, which + 1, 64:128], sin_t[:],
                                      w[:, 0:64].unsqueeze(1).broadcast_to([P, N, 64]), ALU.mult).then_inc(tb, 1)
                for n in range(N):
                    dve.tensor_scalar(maskall[:, n, :], keyidx[:], len_f[:, n:n + 1], MASKED, ALU.is_ge, ALU.mult
                                      ).then_inc(tb, 1)
                assert TB_ANGLES + 8 + N == TB_ALL

            z_pair(0)
            z_pair(1)
            last_scores(4)
            last_scores(6)
            soft_max(1)
            soft_sum(1)
            z_pair(2)
            soft_max(2)
            z_pair(3)
            soft_sum(2)
            for k in range(len(PAIRS)):
                if 4 <= k + 2 < len(PAIRS):
                    z_pair(k + 2)
                s, tp = PAIRS[k]
                if tp == 0 and s >= 2:
                    x2_low(s - 2)
                if tp == s // 2:
                    x2_sum(s)
                if k == 1:
                    angles()
                if k == 3:
                    tables()
                if 0 <= k - K_W0 < 6:
                    t = k - K_W0
                    dve.wait_ge(w0_hi, t + 1)
                    dve.tensor_tensor(w_dst(wa_lo, wo_lo, 0, t),
                                      ps_a[:, (t % 2) * HID:(t % 2 + 1) * HID].rearrange("p (c m) -> p c m", c=NC_),
                                      w_dst(wa_hi, wo_hi, 0, t).bitcast(F32), ALU.subtract).then_inc(w0_lo, 1)
            x2_low(N - 2)
            x2_low(N - 1)

            dve.wait_ge(zt_done, 2 * len(PAIRS))
            dve.sem_inc(t_lo, 2)
            dve.sem_inc(s_read, 2)
            dve.sem_inc(f_done, 1)

            def copy_lo(idx, bank, hi, lo, width=HID):
                dve.wait_ge(t_hi, idx + 1)
                src = ps_t[bank][:, 0:width]
                if len(hi.shape) == 3:
                    src = src.rearrange("p (c m) -> p c m", c=hi.shape[1])
                dve.tensor_tensor(lo, src, hi.bitcast(F32), ALU.subtract).then_inc(t_lo, 1)

            def rope_q_parts(J, par):
                q = ps_q[:, :].rearrange("p (h d) -> p h d", h=HG)
                dve.wait_ge(aq_full, J + 1)
                dve.wait_ge(tab_in[par], tab_count(J, par))
                ta = tab[:, par, 0, :].unsqueeze(1).broadcast_to([P, HG, P])
                dve.tensor_tensor(rope_a[:, 0:HG, :], q, ta, ALU.mult).then_inc(ro_ab, 1)
                rope_q_half(par, 0)

            def rope_q_half(par, half):
                q = ps_q[:, :].rearrange("p (h d) -> p h d", h=HG)
                a, b = 64 * half, 64 * (1 - half)
                dve.tensor_tensor(rope_b[:, 0:HG, a:a + 64], q[:, :, b:b + 64],
                                  tab[:, par, 1, a:a + 64].unsqueeze(1).broadcast_to([P, HG, 64]), ALU.mult
                                  ).then_inc(ro_ab, 1)

            def rope_q(J):
                dve.wait_ge(ro_ab, (J + 1) * 3)
                dve.tensor_tensor(rope_a[:, 0:HG, :], rope_a[:, 0:HG, :], rope_b[:, 0:HG, :], ALU.add
                                  ).then_inc(rq_done, 1)

            def own_k_lo(J, par):
                dve.wait_ge(kt_hi, J + 1)
                dve.tensor_tensor(kT_lo[:, par, CACHED:KEYS], ps_k, kT_hi[:, par, CACHED:KEYS].bitcast(F32),
                                  ALU.subtract).then_inc(kt_lo, 1)

            def rope_k(J, par):
                k = kvown[:, 0, :]
                dve.wait_ge(rms_k, J + 1)
                r = rs[:, par, HG:HG + 1]
                dve.scalar_tensor_tensor(out=rope_a[:, HG, :], in0=k, scalar=r, in1=tab[:, par, 2, :],
                                         op0=ALU.mult, op1=ALU.mult).then_inc(rk_ab, 1)
                for half in range(2):
                    a, b = 64 * half, 64 * (1 - half)
                    dve.scalar_tensor_tensor(out=rope_b[:, HG, a:a + 64], in0=k[:, b:b + 64], scalar=r,
                                             in1=tab[:, par, 3, a:a + 64], op0=ALU.mult, op1=ALU.mult
                                             ).then_inc(rk_ab, 1)
                dve.wait_ge(rk_ab, (J + 1) * 3)
                dve.tensor_tensor(rope_a[:, HG, :], rope_a[:, HG, :], rope_b[:, HG, :], ALU.add).then_inc(rk_done, 1)

            tab_g = [0, 0]

            def tab_count(J, par):
                g, n = tab_g
                return (g * 4 + n // 2 + 1) * 32

            rope_q_parts(0, 0)
            rope_q_half(0, 1)
            rope_q(0)
            for t in range(HG):
                copy_lo(t, t % 2, w_dst(wa_hi, wo_hi, 0, 6 + t), w_dst(wa_lo, wo_lo, 0, 6 + t))
            rope_k(0, 0)
            for i in range(2):
                dve.wait_ge(x2_out[i], 16 * (N // 2))
            dve.wait_ge(x2t_full, N)
            copy_lo(HG, HG % 2, kT_hi[:, 0, 0:CACHED], kT_lo[:, 0, 0:CACHED])
            copy_lo(HG + 1, (HG + 1) % 2, qT_hi[:, :], qT_lo[:, :])
            own_k_lo(0, 0)

            def output_lo(count):
                dve.wait_ge(o_hi, count)
                dve.tensor_tensor(oT_lo[:, :, :].rearrange("p h m -> p (h m)"), ps_o[:, :],
                                  oT_hi[:, :, :].rearrange("p h m -> p (h m)").bitcast(F32), ALU.subtract
                                  ).then_inc(o_lo, 1)

            def add_output(count, m, new=False):
                dve.wait_ge(f_full, count)
                if new:
                    dve.tensor_copy(y[:, m, :], ps_o[:, :]).then_inc(f_done, 1)
                else:
                    dve.tensor_tensor(y[:, m, :], ps_o[:, :], y[:, m, :], ALU.add).then_inc(f_done, 1)

            def step(g, n, first, last):
                J = g * N + n
                base = g * PER_G + PRO
                par = n % 2
                names = groups_of(n, last)
                nxt = not (last and n == N - 1)
                w = [m for m in names if m[0] in "WL"]

                def group(name):
                    i, bank = t_index(n, name, last)
                    if name[0] == "L":
                        dve.wait_ge(t_hi, base + i + 1)
                        if name == "L6":
                            dve.sem_inc(t_lo, 1)
                        else:
                            lo, src = late_parts(bank, int(name[1:]), 1)
                            hi, _ = late_parts(bank, int(name[1:]), 0)
                            dve.tensor_tensor(lo, src, hi.bitcast(F32), ALU.subtract).then_inc(t_lo, 1)
                        return
                    hi, width = hi_lo_target(name, g, 1 - par, 0)
                    lo, _ = hi_lo_target(name, g, 1 - par, 1)
                    copy_lo(base + i, bank, hi, lo, width)

                def least(h):
                    wait_alone(dve, s_full, J * 4 + h + 1)
                    if h == 0:
                        wait_alone(dve, st_done, J + 1)
                        wait_alone(dve, tab_in[par], (g * 4 + n // 2 + 1) * 32)
                    halves = ps_s[h % 2][:, :].rearrange("p (b k) -> p b k", b=2)[:, :, 0:HALF]
                    dve.tensor_tensor_reduce(out=sm[:, h, :].rearrange("p (b k) -> p b k", b=2), in0=halves,
                                             in1=mask[:, par, :].rearrange("p (b k) -> p b k", b=2),
                                             scale=qs[:, par, h:h + 1], scalar=3.0e38, op0=ALU.add, op1=ALU.min,
                                             accum_out=mn[:, h:h + 1]).then_inc(s_read, 1)

                def reciprocal(h):
                    dve.wait_ge(e_done, J * 4 + h + 1)
                    dve.reciprocal(rd[:, h:h + 1], den[:, h:h + 1]).then_inc(r_done, 1)

                def normalise(h):
                    reciprocal(h)
                    dve.wait_ge(r_done, J * 4 + h + 1)
                    dve.tensor_scalar(sm[:, h, :], sm[:, h, :], rd[:, h:h + 1], None, ALU.mult).then_inc(p_dve, 1)

                if first and n == 3:
                    dve.wait_ge(init3, 1)
                least(0)
                least(1)
                if w:
                    group(w[0])
                normalise(0)
                normalise(1)
                if len(w) > 1:
                    group(w[1])
                if not (first and n < 1):
                    output_lo(J)
                dve.wait_ge(vs_hi, J + 1)
                dve.tensor_tensor(v_lo[:, KC, :], kvown[:, 1, :], v_hi[:, KC, :].bitcast(F32), ALU.subtract
                                  ).then_inc(vs_lo, 1)
                if nxt:
                    group("K")
                group("D0")
                least(2)
                tab_g[:] = [g + (n == N - 1), (n + 1) % N]
                if nxt:
                    rope_q_parts(J + 1, 1 - par)
                reciprocal(2)
                if nxt:
                    rope_q_half(1 - par, 1)
                least(3)
                group("D1")
                if nxt:
                    rope_q(J + 1)
                reciprocal(3)
                group("D2")
                if nxt:
                    rope_k(J + 1, 1 - par)
                    group("q")
                group("D3")
                if nxt:
                    own_k_lo(J + 1, 1 - par)
                if not (first and n < 1):
                    add_output(J, (n - 1) % N, first)
                group("DS")
                if first and n == 2:
                    dve.memset(y[:, N - 1, :], 0.0).then_inc(init3, 1)

            for n in range(N):
                step(0, n, True, False)
            with dve.Fori(1, G - 1) as g:
                for n in range(N):
                    step(g, n, False, False)
            for n in range(N):
                step(G - 1, n, False, True)

            def y_low(n):
                dve.wait_ge(yt_hi, n + 1)
                dve.tensor_tensor(yT_lo[:, n % 2, :, :].rearrange("p c m -> p (c m)"), yt_bank(n)[:, :],
                                  yT_hi[:, n % 2, :, :].rearrange("p c m -> p (c m)").bitcast(F32), ALU.subtract
                                  ).then_inc(yt_done, 1)

            RT = 11

            def route(n):
                i = n % 2
                g_ps = ps_b[:, i * HID:i * HID + P + E]
                e, p, sel, keep, wgt = (routes[:, i, m, :] for m in range(5))
                neg_max, total, inv, s2 = (route1[:, i, m:m + 1] for m in range(4))
                gt, eq = pairs[:, i, 0, :, :], pairs[:, i, 1, :, :]
                c = [n * RT]

                def after_last():
                    dve.wait_ge(rt, c[0])

                def chained(ins):
                    c[0] += 1
                    ins.then_inc(rt, 1)

                dve.wait_ge(g_full, n + 1)
                dve.tensor_reduce(neg_max, g_ps[:, P:P + E], AX.X, ALU.max, negate=True).then_inc(gm, 1)
                if 2 <= n + 1 < N:
                    y_low(n + 1)
                dve.wait_ge(ge, n + 1)
                chained(dve.reciprocal(inv, total))
                after_last()
                chained(dve.tensor_scalar(p, e, inv, None, ALU.mult))
                after_last()
                later = p.unsqueeze(1).broadcast_to([P, E, E])
                mine = p.unsqueeze(2).broadcast_to([P, E, E])
                chained(dve.tensor_tensor(gt, later, mine, ALU.is_gt))
                chained(dve.tensor_tensor(eq, later, mine, ALU.is_equal))
                after_last()
                chained(dve.tensor_tensor(eq, eq, before[:], ALU.mult))
                after_last()
                chained(dve.tensor_tensor(gt, gt, eq, ALU.add))
                after_last()
                chained(dve.tensor_reduce(sel, gt, AX.X, ALU.add))
                after_last()
                chained(dve.tensor_scalar(keep, sel, 1.5, None, ALU.is_lt))
                after_last()
                chained(dve.tensor_tensor(wgt, keep, p, ALU.mult))
                after_last()
                chained(dve.tensor_reduce(s2, wgt, AX.X, ALU.add))
                after_last()
                chained(dve.reciprocal(inv, s2))
                after_last()
                assert c[0] == (n + 1) * RT
                if n >= 2:
                    dve.wait_ge(ht_full, n - 1)
                dve.scalar_tensor_tensor(out=hw[:, i, :, :], in0=g_ps[:, 0:P].rearrange("p (e r) -> p e r", r=R),
                                         scalar=inv, in1=wgt.unsqueeze(2).broadcast_to([P, E, R]),
                                         op0=ALU.mult, op1=ALU.mult).then_inc(hw_done, 1)

            def finish(n):
                dve.wait_ge(d_full, n + 1)
                dve.wait_ge(x2b, n + 1)
                if n >= 2:
                    dve.wait_ge(fin_out[n % 2], 16 * (n // 2))
                dve.tensor_tensor(fin[:, n % 2, :], ps_a[:, (n % 2) * HID:(n % 2 + 1) * HID], x2r[:, n % 2, :],
                                  ALU.add).then_inc(fin_done, 1)

            y_low(0)
            output_lo(G * N)
            y_low(1)
            add_output(G * N, N - 1)
            dve.wait_ge(bias_ok, 2)
            for n in range(N):
                route(n)
                if n >= 1:
                    finish(n - 1)
            finish(N - 1)


_INS = ['x', 'itok_B_3_7', 'itok_Bx16_0_63', 'itok_B_207_1644', 'L0_cond_A', 'L0_cond_B', 'L0_attn_weight_qkv',
        'L0_attn_weight_proj', 'L0_cond2_Wq', 'L0_cond2_Wk', 'L0_cond2_Wv', 'L0_cond2_Wo', 'L0_cond2_q_norm_w',
        'L0_cond2_k_norm_w', 'L0_cond2_k_cache', 'L0_cond2_v_cache', 'L0_ffn_W_base', 'L0_ffn_b_base',
        'L0_ffn_W_gate', 'L0_ffn_A', 'L0_ffn_B']
_OUTS = [((8, 128, 512), 'float32')]


def kernel(**inputs):
    import numpy as _np
    import concourse.bacc as _bacc
    from concourse import mybir as _mybir
    from concourse.bass_utils import run_bass_kernel_spmd as _run

    nc = _bacc.Bacc("TRN2", target_bir_lowering=False, num_devices=1)
    arrays, args = {}, []
    for name in _INS:
        a = _np.ascontiguousarray(inputs[name])
        arrays[f"in_{name}_dram"] = a
        args.append(nc.dram_tensor(f"in_{name}_dram", a.shape, _mybir.dt.from_np(a.dtype), kind="ExternalInput").ap())
    for i, (shape, dtype) in enumerate(_OUTS):
        dt = _mybir.dt.from_np(_np.dtype(dtype))
        args.append(nc.dram_tensor(f"out_{i}_dram", shape, dt, kind="ExternalOutput").ap())
    block_program(nc, *args)
    r = _run(nc, [arrays], core_ids=[0])
    got = tuple(r.results[0][f"out_{i}_dram"] for i in range(len(_OUTS)))
    return got[0]
```
